# Optimizing a Trainium2 kernel written in Bass

```python
import numpy as np
import jax
import jax.numpy as jnp

def _softmax(x, axis=-1):
    return jax.nn.softmax(x, axis=axis)

def _gelu(x):
    return jax.nn.gelu(x, approximate=True)

def _silu(x):
    return jax.nn.silu(x)

def _sigmoid(x):
    return jax.nn.sigmoid(x)

def _layernorm(x, axis=-1, eps=1e-05):
    m = jnp.mean(x, axis=axis, keepdims=True)
    v = jnp.var(x, axis=axis, keepdims=True)
    return (x - m) / jnp.sqrt(v + eps)

def _scatter_add(tgt, idx, src, axis=0):
    return tgt.at[idx].add(src)

def _segment_sum(src, seg, n):
    return jax.ops.segment_sum(src, seg, n)
kernel_name = 'mk_gps_d2_gnn_r8_d6e15e'

def setup_inputs(seed: int=0):
    np.random.seed(seed)
    _w = jnp.asarray

    def _rec_inputs():
        import jax
        import jax.numpy as jnp
        _gk = jax.random.key(seed)
        x = -0.0001126 + 1 * jax.random.normal(jax.random.fold_in(_gk, 1), (6250, 256), jnp.float32)
        src = jax.random.randint(jax.random.fold_in(_gk, 2), (200000,), 0, 6250, jnp.int32)
        dst = jnp.minimum((6250 * jax.random.uniform(jax.random.fold_in(_gk, 3), (200000,)) ** 2.0).astype(jnp.int32), 49999)
        _o = jnp.argsort(dst, stable=True)
        src = src[_o]
        dst = dst[_o]
        edge_type_8 = jax.random.randint(jax.random.fold_in(_gk, 13), (200000,), 0, 8, jnp.int32)
        return (x, src, dst, edge_type_8)
    x, src, dst, edge_type_8 = _rec_inputs()

    def _L0_gnn_setup():
        import jax, jax.numpy as jnp
        import numpy as np
        N = 3750
        E = 75000
        FIN = 256
        FOUT = 256
        R = 8
        key = jax.random.key(seed)
        ks = jax.random.split(key, 6)
        x = jax.random.normal(ks[0], (N, FIN), dtype=jnp.float32)
        W = jax.random.normal(ks[1], (R, FIN, FOUT), dtype=jnp.float32) * (1.0 / np.sqrt(FIN))
        W_root = jax.random.normal(ks[2], (FIN, FOUT), dtype=jnp.float32) * (1.0 / np.sqrt(FIN))
        bias = jax.random.normal(ks[3], (FOUT,), dtype=jnp.float32) * 0.01
        edge_index = jax.random.randint(ks[4], (2, E), 0, N, dtype=jnp.int64)
        edge_type = jax.random.randint(ks[5], (E,), 0, R, dtype=jnp.int64)
        return {'x': x, 'W': W, 'W_root': W_root, 'bias': bias, 'edge_index': edge_index, 'edge_type': edge_type}
    _L0_gnn_all = _L0_gnn_setup()
    _L0_gnn_in = {k: v for k, v in _L0_gnn_all.items() if k in ('W', 'W_root', 'bias')}
    del _L0_gnn_all

    def _L0_mix_setup():
        import jax, jax.numpy as jnp
        import numpy as np
        B, N, C, H = (8, 2048, 256, 8)
        D = C // H
        GH = C // 4
        key = jax.random.key(seed)
        ks = jax.random.split(key, 6)
        s = 0.02
        return {'x': jax.random.normal(ks[0], (B, N, C), dtype=jnp.float32), 'Wqkv': jax.random.normal(ks[1], (C, 3 * C), dtype=jnp.float32) * s, 'Wproj': jax.random.normal(ks[2], (C, C), dtype=jnp.float32) * s, 'bproj': jnp.zeros((C,), dtype=jnp.float32), 'ln_g': jnp.ones((C,), dtype=jnp.float32), 'ln_b': jnp.zeros((C,), dtype=jnp.float32), 'Wg1': jax.random.normal(ks[3], (C, GH), dtype=jnp.float32) * s, 'bg1': jnp.zeros((GH,), dtype=jnp.float32), 'Wg2': jax.random.normal(ks[4], (GH, C), dtype=jnp.float32) * s, 'bg2': jnp.zeros((C,), dtype=jnp.float32)}
    _L0_mix_all = _L0_mix_setup()
    _L0_mix_in = {k: v for k, v in _L0_mix_all.items() if k in ('Wqkv', 'Wproj', 'bproj', 'ln_g', 'ln_b', 'Wg1', 'bg1', 'Wg2', 'bg2')}
    del _L0_mix_all

    def _L0_ffn_setup():
        import jax, jax.numpy as jnp
        import numpy as np
        DIM = 256
        H = 8
        D = 64
        G = 64
        INNER = H * D
        SCALE = D ** (-0.5)
        key = jax.random.key(seed)
        ks = jax.random.split(key, 12)
        B, N = (4, 2048)
        x = jax.random.normal(ks[0], (B, N, DIM), dtype=jnp.float32)
        s = lambda fan_in: 1.0 / np.sqrt(fan_in)
        W_fx = jax.random.normal(ks[1], (DIM, INNER), dtype=jnp.float32) * s(DIM)
        b_fx = jnp.zeros((INNER,), dtype=jnp.float32)
        W_x = jax.random.normal(ks[2], (DIM, INNER), dtype=jnp.float32) * s(DIM)
        b_x = jnp.zeros((INNER,), dtype=jnp.float32)
        A = jax.random.normal(ks[3], (G, D), dtype=jnp.float32)
        Q, _ = jnp.linalg.qr(A.T)
        W_slice = Q[:, :G].astype(jnp.float32)
        b_slice = jnp.zeros((G,), dtype=jnp.float32)
        W_q = jax.random.normal(ks[4], (D, D), dtype=jnp.float32) * s(D)
        W_k = jax.random.normal(ks[5], (D, D), dtype=jnp.float32) * s(D)
        W_v = jax.random.normal(ks[6], (D, D), dtype=jnp.float32) * s(D)
        W_out = jax.random.normal(ks[7], (INNER, DIM), dtype=jnp.float32) * s(INNER)
        b_out = jnp.zeros((DIM,), dtype=jnp.float32)
        temperature = jnp.ones((1, H, 1, 1), dtype=jnp.float32) * 0.5
        return {'x': x, 'W_fx': W_fx, 'b_fx': b_fx, 'W_x': W_x, 'b_x': b_x, 'W_slice': W_slice, 'b_slice': b_slice, 'W_q': W_q, 'W_k': W_k, 'W_v': W_v, 'W_out': W_out, 'b_out': b_out, 'temperature': temperature}
    _L0_ffn_all = _L0_ffn_setup()
    _L0_ffn_in = {k: v for k, v in _L0_ffn_all.items() if k in ('W_fx', 'b_fx', 'W_x', 'b_x', 'W_slice', 'b_slice', 'W_q', 'W_k', 'W_v', 'W_out', 'b_out', 'temperature')}
    del _L0_ffn_all

    def _L1_gnn_setup():
        import jax, jax.numpy as jnp
        import numpy as np
        N_NODES = 12500
        N_EDGES = 200000
        D_IN = 256
        D_OUT = 256
        key = jax.random.key(seed)
        k1, k2, k3, k4, k5 = jax.random.split(key, 5)
        feat = jax.random.normal(k1, (N_NODES, D_IN), dtype=jnp.float32)
        src = jax.random.randint(k2, (N_EDGES,), 0, N_NODES, dtype=jnp.int32)
        dst = jax.random.randint(k3, (N_EDGES,), 0, N_NODES, dtype=jnp.int32)
        gain = float(np.sqrt(2.0))
        limit = gain * float(np.sqrt(6.0 / (D_IN + D_OUT)))
        w_neigh = jax.random.uniform(k4, (D_OUT, D_IN), minval=-limit, maxval=limit, dtype=jnp.float32)
        w_self = jax.random.uniform(k5, (D_OUT, D_IN), minval=-limit, maxval=limit, dtype=jnp.float32)
        b_self = jnp.zeros((D_OUT,), dtype=jnp.float32)
        return {'feat': feat, 'src': src, 'dst': dst, 'w_neigh': w_neigh, 'w_self': w_self, 'b_self': b_self}
    _L1_gnn_all = _L1_gnn_setup()
    _L1_gnn_in = {k: v for k, v in _L1_gnn_all.items() if k in ('w_neigh', 'w_self', 'b_self')}
    del _L1_gnn_all

    def _L1_mix_setup():
        import jax, jax.numpy as jnp
        import numpy as np
        HEADS = 8
        DIM_HEAD = 64
        EPS = 1e-05

        def _inst_norm_lastdim(t):
            mu = jnp.mean(t, axis=-1, keepdims=True)
            var = jnp.mean(jnp.square(t - mu), axis=-1, keepdims=True)
            return (t - mu) * jax.lax.rsqrt(var + EPS)
        key = jax.random.key(seed)
        k1, k2, k3, k4 = jax.random.split(key, 4)
        b, n, dim = (4, 1024, 256)
        inner = HEADS * DIM_HEAD
        x = jax.random.normal(k1, (b, n, dim), dtype=jnp.float32)
        Wqkv = jax.random.normal(k2, (3 * inner, dim), dtype=jnp.float32) * (1.0 / np.sqrt(dim))
        Wout = jax.random.normal(k3, (dim, inner), dtype=jnp.float32) * (1.0 / np.sqrt(inner))
        bout = jax.random.normal(k4, (dim,), dtype=jnp.float32) * 0.01
        return {'x': x, 'Wqkv': Wqkv, 'Wout': Wout, 'bout': bout}
    _L1_mix_all = _L1_mix_setup()
    _L1_mix_in = {k: v for k, v in _L1_mix_all.items() if k in ('Wqkv', 'Wout', 'bout')}
    del _L1_mix_all

    def _L1_ffn_setup():
        import jax, jax.numpy as jnp
        import numpy as np
        NUM_EXPERTS = 8
        TOP_K = 2
        B, S, D = (8, 1024, 256)

        def _moe(tokens, router_w, w1, b1, w2, b2):
            N = tokens.shape[0]
            E = router_w.shape[0]
            logits = tokens.astype(jnp.float32) @ router_w.astype(jnp.float32).T
            probs = jax.nn.softmax(logits, axis=-1)
            rw, re = jax.lax.top_k(probs, TOP_K)
            if TOP_K > 1:
                rw = rw / jnp.maximum(rw.sum(-1, keepdims=True), 1e-12)
            rw = rw.astype(tokens.dtype)
            combine = jnp.zeros((N, E), tokens.dtype).at[jnp.arange(N)[:, None], re].set(rw)
            out = tokens
            for e in range(E):
                h = jax.nn.gelu(tokens @ w1[e] + b1[e], approximate=False)
                y = h @ w2[e] + b2[e]
                out = out + combine[:, e:e + 1] * y
            return out
        key = jax.random.key(seed)
        ks = jax.random.split(key, 4)
        scale = 1.0 / np.sqrt(D).astype(np.float32)
        return {'input_embeddings': jax.random.normal(ks[0], (B, S, D), jnp.float32), 'router_w': jax.random.normal(ks[1], (NUM_EXPERTS, D), jnp.float32) * scale, 'w1': jax.random.normal(ks[2], (NUM_EXPERTS, D, D), jnp.float32) * scale, 'b1': jnp.zeros((NUM_EXPERTS, D), jnp.float32), 'w2': jax.random.normal(ks[3], (NUM_EXPERTS, D, D), jnp.float32) * scale, 'b2': jnp.zeros((NUM_EXPERTS, D), jnp.float32)}
    _L1_ffn_all = _L1_ffn_setup()
    _L1_ffn_in = {k: v for k, v in _L1_ffn_all.items() if k in ('router_w', 'w1', 'b1', 'w2', 'b2')}
    del _L1_ffn_all
    return {'x': x, 'src': src, 'dst': dst, 'edge_type_8': edge_type_8, 'L0_gnn_W': _L0_gnn_in['W'], 'L0_gnn_W_root': _L0_gnn_in['W_root'], 'L0_gnn_bias': _L0_gnn_in['bias'], 'L0_mix_Wqkv': _L0_mix_in['Wqkv'], 'L0_mix_Wproj': _L0_mix_in['Wproj'], 'L0_mix_bproj': _L0_mix_in['bproj'], 'L0_mix_ln_g': _L0_mix_in['ln_g'], 'L0_mix_ln_b': _L0_mix_in['ln_b'], 'L0_mix_Wg1': _L0_mix_in['Wg1'], 'L0_mix_bg1': _L0_mix_in['bg1'], 'L0_mix_Wg2': _L0_mix_in['Wg2'], 'L0_mix_bg2': _L0_mix_in['bg2'], 'L0_ffn_W_fx': _L0_ffn_in['W_fx'], 'L0_ffn_b_fx': _L0_ffn_in['b_fx'], 'L0_ffn_W_x': _L0_ffn_in['W_x'], 'L0_ffn_b_x': _L0_ffn_in['b_x'], 'L0_ffn_W_slice': _L0_ffn_in['W_slice'], 'L0_ffn_b_slice': _L0_ffn_in['b_slice'], 'L0_ffn_W_q': _L0_ffn_in['W_q'], 'L0_ffn_W_k': _L0_ffn_in['W_k'], 'L0_ffn_W_v': _L0_ffn_in['W_v'], 'L0_ffn_W_out': _L0_ffn_in['W_out'], 'L0_ffn_b_out': _L0_ffn_in['b_out'], 'L0_ffn_temperature': _L0_ffn_in['temperature'], 'L1_gnn_w_neigh': _L1_gnn_in['w_neigh'], 'L1_gnn_w_self': _L1_gnn_in['w_self'], 'L1_gnn_b_self': _L1_gnn_in['b_self'], 'L1_mix_Wqkv': _L1_mix_in['Wqkv'], 'L1_mix_Wout': _L1_mix_in['Wout'], 'L1_mix_bout': _L1_mix_in['bout'], 'L1_ffn_router_w': _L1_ffn_in['router_w'], 'L1_ffn_w1': _L1_ffn_in['w1'], 'L1_ffn_b1': _L1_ffn_in['b1'], 'L1_ffn_w2': _L1_ffn_in['w2'], 'L1_ffn_b2': _L1_ffn_in['b2']}

def reference(x, src, dst, edge_type_8, L0_gnn_W, L0_gnn_W_root, L0_gnn_bias, L0_mix_Wqkv, L0_mix_Wproj, L0_mix_bproj, L0_mix_ln_g, L0_mix_ln_b, L0_mix_Wg1, L0_mix_bg1, L0_mix_Wg2, L0_mix_bg2, L0_ffn_W_fx, L0_ffn_b_fx, L0_ffn_W_x, L0_ffn_b_x, L0_ffn_W_slice, L0_ffn_b_slice, L0_ffn_W_q, L0_ffn_W_k, L0_ffn_W_v, L0_ffn_W_out, L0_ffn_b_out, L0_ffn_temperature, L1_gnn_w_neigh, L1_gnn_w_self, L1_gnn_b_self, L1_mix_Wqkv, L1_mix_Wout, L1_mix_bout, L1_ffn_router_w, L1_ffn_w1, L1_ffn_b1, L1_ffn_w2, L1_ffn_b2):
    import jax
    import jax.numpy as jnp

    def _L0_gnn_ref(x, W, W_root, bias, edge_index, edge_type):
        import jax, jax.numpy as jnp
        import numpy as np
        N = 3750
        E = 75000
        FIN = 256
        FOUT = 256
        R = 8
        n, fin = x.shape
        r = W.shape[0]
        src, dst = (edge_index[0], edge_index[1])
        seg = dst * r + edge_type
        sums = jax.ops.segment_sum(x[src], seg, num_segments=n * r)
        cnt = jax.ops.segment_sum(jnp.ones_like(src, dtype=x.dtype), seg, num_segments=n * r)
        mean = (sums / jnp.maximum(cnt, 1.0)[:, None]).reshape(n, r, fin)
        out = jnp.einsum('nri,rio->no', mean, W) + x @ W_root + bias
        return jax.nn.relu(out)

    def _L0_mix_ref(x, Wqkv, Wproj, bproj, ln_g, ln_b, Wg1, bg1, Wg2, bg2):
        import jax, jax.numpy as jnp
        import numpy as np
        B, N, C, H = (8, 2048, 256, 8)
        D = C // H
        GH = C // 4
        b, n, c = x.shape
        h, d = (H, D)
        qkv = (x @ Wqkv).reshape(b, n, 3, h, d)
        q, k, v = (qkv[:, :, 0], qkv[:, :, 1], qkv[:, :, 2])
        k = jax.nn.softmax(k, axis=1)
        context = jnp.einsum('bnhd,bnhv->bhdv', k, v)
        out = jnp.einsum('bnhd,bhdv->bnhv', q, context).reshape(b, n, c)
        mu = jnp.mean(x, axis=-1, keepdims=True)
        var = jnp.var(x, axis=-1, keepdims=True)
        xn = (x - mu) * jax.lax.rsqrt(var + 1e-05) * ln_g + ln_b
        hgate = jax.nn.gelu(xn @ Wg1 + bg1, approximate=False)
        gate = jax.nn.sigmoid(hgate @ Wg2 + bg2)
        return out * gate @ Wproj + bproj

    def _L0_ffn_ref(x, W_fx, b_fx, W_x, b_x, W_slice, b_slice, W_q, W_k, W_v, W_out, b_out, temperature):
        import jax, jax.numpy as jnp
        import numpy as np
        DIM = 256
        H = 8
        D = 64
        G = 64
        INNER = H * D
        SCALE = D ** (-0.5)
        B, N, _ = x.shape
        fx_mid = (x @ W_fx + b_fx).reshape(B, N, H, D).transpose(0, 2, 1, 3)
        x_mid = (x @ W_x + b_x).reshape(B, N, H, D).transpose(0, 2, 1, 3)
        temp = jnp.clip(temperature, 0.1, 5.0)
        slice_weights = jax.nn.softmax((x_mid @ W_slice + b_slice) / temp, axis=-1)
        slice_norm = slice_weights.sum(axis=2)
        slice_token = jnp.einsum('bhnc,bhng->bhgc', fx_mid, slice_weights)
        slice_token = slice_token / (slice_norm[..., None] + 1e-05)
        q = slice_token @ W_q
        k = slice_token @ W_k
        v = slice_token @ W_v
        attn = jax.nn.softmax(jnp.einsum('bhgc,bhkc->bhgk', q, k) * SCALE, axis=-1)
        out_slice = jnp.einsum('bhgk,bhkc->bhgc', attn, v)
        out_x = jnp.einsum('bhgc,bhng->bhnc', out_slice, slice_weights)
        out_x = out_x.transpose(0, 2, 1, 3).reshape(B, N, INNER)
        return out_x @ W_out + b_out

    def _L1_gnn_ref(feat, src, dst, w_neigh, w_self, b_self):
        import jax, jax.numpy as jnp
        import numpy as np
        N_NODES = 12500
        N_EDGES = 200000
        D_IN = 256
        D_OUT = 256
        n = feat.shape[0]
        summed = jax.ops.segment_sum(feat[src], dst, num_segments=n)
        deg = jax.ops.segment_sum(jnp.ones_like(dst, dtype=feat.dtype), dst, num_segments=n)
        h_neigh_raw = summed / jnp.maximum(deg, 1.0)[:, None]
        h_neigh = h_neigh_raw @ w_neigh.T
        rst = feat @ w_self.T + b_self + h_neigh
        return rst

    def _L1_mix_ref(x, Wqkv, Wout, bout):
        import jax, jax.numpy as jnp
        import numpy as np
        HEADS = 8
        DIM_HEAD = 64
        EPS = 1e-05

        def _inst_norm_lastdim(t):
            mu = jnp.mean(t, axis=-1, keepdims=True)
            var = jnp.mean(jnp.square(t - mu), axis=-1, keepdims=True)
            return (t - mu) * jax.lax.rsqrt(var + EPS)
        b, n, dim = x.shape
        qkv = jnp.einsum('bnc,fc->bnf', x, Wqkv)
        q, k, v = jnp.split(qkv, 3, axis=-1)

        def to_heads(t):
            return t.reshape(b, n, HEADS, DIM_HEAD).transpose(0, 2, 1, 3)
        q, k, v = (to_heads(q), to_heads(k), to_heads(v))
        k = _inst_norm_lastdim(k)
        v = _inst_norm_lastdim(v)
        dots = jnp.einsum('bhnd,bhne->bhde', k, v)
        out = jnp.einsum('bhnd,bhde->bhne', q, dots) / n
        out = out.transpose(0, 2, 1, 3).reshape(b, n, HEADS * DIM_HEAD)
        return jnp.einsum('bnf,cf->bnc', out, Wout) + bout

    def _L1_ffn_ref(input_embeddings, router_w, w1, b1, w2, b2):
        import jax, jax.numpy as jnp
        import numpy as np
        NUM_EXPERTS = 8
        TOP_K = 2
        B, S, D = (8, 1024, 256)

        def _moe(tokens, router_w, w1, b1, w2, b2):
            N = tokens.shape[0]
            E = router_w.shape[0]
            logits = tokens.astype(jnp.float32) @ router_w.astype(jnp.float32).T
            probs = jax.nn.softmax(logits, axis=-1)
            rw, re = jax.lax.top_k(probs, TOP_K)
            if TOP_K > 1:
                rw = rw / jnp.maximum(rw.sum(-1, keepdims=True), 1e-12)
            rw = rw.astype(tokens.dtype)
            combine = jnp.zeros((N, E), tokens.dtype).at[jnp.arange(N)[:, None], re].set(rw)
            out = tokens
            for e in range(E):
                h = jax.nn.gelu(tokens @ w1[e] + b1[e], approximate=False)
                y = h @ w2[e] + b2[e]
                out = out + combine[:, e:e + 1] * y
            return out
        b, s, d = input_embeddings.shape
        tokens = input_embeddings.reshape(b * s, d)
        return _moe(tokens, router_w, w1, b1, w2, b2).reshape(b, s, d)
    edge_index = jnp.stack([src, dst])
    xn = _layernorm(x, axis=-1)
    x = x + _L0_gnn_ref(xn, L0_gnn_W, L0_gnn_W_root, L0_gnn_bias, edge_index, edge_type_8) + _L0_mix_ref(xn[None], L0_mix_Wqkv, L0_mix_Wproj, L0_mix_bproj, L0_mix_ln_g, L0_mix_ln_b, L0_mix_Wg1, L0_mix_bg1, L0_mix_Wg2, L0_mix_bg2)[0]
    x = x + _L0_ffn_ref(_layernorm(x, axis=-1)[None], L0_ffn_W_fx, L0_ffn_b_fx, L0_ffn_W_x, L0_ffn_b_x, L0_ffn_W_slice, L0_ffn_b_slice, L0_ffn_W_q, L0_ffn_W_k, L0_ffn_W_v, L0_ffn_W_out, L0_ffn_b_out, L0_ffn_temperature)[0]
    xn = _layernorm(x, axis=-1)
    x = x + _L1_gnn_ref(xn, src, dst, L1_gnn_w_neigh, L1_gnn_w_self, L1_gnn_b_self) + _L1_mix_ref(xn[None], L1_mix_Wqkv, L1_mix_Wout, L1_mix_bout)[0]
    x = x + _L1_ffn_ref(_layernorm(x, axis=-1)[None], L1_ffn_router_w, L1_ffn_w1, L1_ffn_b1, L1_ffn_w2, L1_ffn_b2)[0]
    return x

_drawn_inputs = setup_inputs


def setup_inputs(seed=0):
    import zlib

    import numpy as np

    out = dict(_drawn_inputs(seed))
    spreads = {'L0_mix_bproj': (0.0, 0.8),
     'L0_mix_ln_g': (1.0, 0.6),
     'L0_mix_ln_b': (0.0, 0.8),
     'L0_mix_bg1': (0.0, 0.8),
     'L0_mix_bg2': (0.0, 0.8),
     'L0_ffn_b_fx': (0.0, 0.529),
     'L0_ffn_b_x': (0.0, 2.0),
     'L0_ffn_b_slice': (0.0, 2.0),
     'L0_ffn_b_out': (0.0, 0.8),
     'L0_ffn_temperature': (0.5, 0.6),
     'L1_gnn_b_self': (0.0, 0.8),
     'L1_ffn_b1': (0.0, 2.0),
     'L1_ffn_b2': (0.0, 1.578)}
    factors = {'L0_gnn_bias': 47.584,
     'L0_mix_Wqkv': 8.0,
     'L0_mix_Wproj': 8.0,
     'L0_mix_Wg1': 8.0,
     'L0_mix_Wg2': 8.0,
     'L0_ffn_W_x': 18.538,
     'L0_ffn_W_slice': 23.075,
     'L0_ffn_W_q': 21.614,
     'L0_ffn_W_k': 21.353,
     'L1_mix_bout': 63.728,
     'L0_ffn_W_fx': 2.714}
    for name, (base, spread) in spreads.items():
        noise = np.random.default_rng([zlib.crc32(name.encode()), seed]).standard_normal(out[name].shape)
        drawn = base * np.exp(spread * noise) if base else spread * noise
        out[name] = jnp.asarray(drawn.astype(out[name].dtype))
    for name, factor in factors.items():
        out[name] = (out[name] * factor).astype(out[name].dtype)
    return out
```

```python
import concourse.bass as bass
from concourse import mybir
from contextlib import ExitStack

FP32 = mybir.dt.float32
BF16 = mybir.dt.bfloat16
I32 = mybir.dt.int32
ALU = mybir.AluOpType
ACT = mybir.ActivationFunctionType
AX = mybir.AxisListType.X

P = 128
N = 6250
C = 256
KC = C // P
NT = -(-N // P)
NP = NT * P
LAST = N - (NT - 1) * P
E = 200000
R = 8
ET = -(-E // P)
GRP = 4
BODY = 16
T = -(-(ET + NT - 1) // BODY) * BODY
NG = T // GRP
BPB = BODY // GRP
TW = T + BODY
TB = -(-ET // P)
EROWS, ECOLS = 80, E // 80
PAD = TB * P * P + P - E
PROWS = 80
PAD_DST = 8191
EPS = 1e-5


def build(nc, x, src, dst, etype, gnn0_w, gnn0_root, gnn0_bias, mix_wqkv, mix_wq_t, mix_wproj, mix_bproj,
          mix_ln_g, mix_ln_b, mix_wg1, mix_bg1, mix_wg2, mix_bg2, ffn_wfx, ffn_bfx, ffn_wx_t, ffn_bx,
          ffn_wslice, ffn_bslice, ffn_wq, ffn_wk, ffn_wv, ffn_wout, ffn_bout, ffn_temp,
          gnn1_wneigh_t, gnn1_wself_t, gnn1_bself, mix1_wqkv, mix1_wkv_t, mix1_wout_t, mix1_bout,
          router_t, w1, b1, w2, b2, out, stop_after=99):
    ctx = ExitStack()
    with ctx:
        sems = {}

        share = {}
        ended = {}

        def take_turns(lane, step, count):
            share[step] = (lane, ended.get(lane, 0))
            ended[lane] = ended.get(lane, 0) + count

        for steps in (
                "n0_t n0_xnt n0_xn n0_var n0_rstd n0_gvar n0_grstd n0_gst n0_gag n0_st n0_ag n0_km n0_km_mm n0_root "
                "n0_root_mm n0_ga n0_gate n0_hg n0_hg_t n0_hgt n0_y_mm0 n0_y_mm1 n0_y_mm2 n0_y_mm3",
                "m1_k_mm m1_v_mm m1_ek m1_v m1_ctx_mm m2_xb m2_g_mm m2_sig m2_pr m2_prt_mm m2_prt m2_f_mm m2_out",
                "f1_x1 f1_st f1_ag f1_var f1_rstd f1_xn f1_t f1_xnt f1_l_mm f1_mx f1_lg f1_ex f1_sm f1_rs f1_sw "
                "f1_swt_mm f1_swt f1_u_mm",
                "f2_o_mm f2_x2 f2_st f2_ag f2_var f2_rstd f2_xn f2_t f2_xnt f2_kv_mm f2_ss f2_v1 f2_pv f2_krs f2_kn "
                "f2_v f2_dots_mm",
                "c_hn c_hn_t c_hnt c_x_mm c_x3 c_st c_ag c_var c_rstd c_xn c_x4_t c_x4t c_x34 c_r c_r_mm"):
            for n_, step_ in enumerate(steps.split()):
                take_turns(f"tile_step_{n_}", step_, NT)
        for lane, steps in (
                ("load", [("n0_in", 1), ("m1_in", 1), ("m2_in", 3), ("f1_in", 1), ("f2_in", 2), ("c_in", 2)]),
                ("store_a", [("n0_xnt_out", 1), ("m2_st", 1), ("f1_x1_out", 1), ("f2_x2_out", 1), ("c_x34_out", 1)]),
                ("store_b", [("n0_y_out", 1), ("f1_swt_out", 1), ("f2_xn_out", 1), ("c_x4t_out", 1)]),
                ("store_c", [("n0_hgt_out", 1), ("f2_xnt_out", 1)])):
            for step_, dmas in steps:
                for s in range(2):
                    take_turns(f"{lane}_{s}", f"{step_}{s}", 16 * dmas * (NT // 2 + 1 - s))

        def sem(name):
            name = share.get(name, (name, 0))[0]
            if name not in sems:
                sems[name] = ctx.enter_context(nc.semaphore(name))
            return sems[name]

        def dram(name, shape, dt=FP32):
            return nc.dram_tensor(name, shape, dt, kind="Internal").ap()

        def sb(name, shape, dt=FP32):
            return ctx.enter_context(nc.sbuf_tensor(name, shape, dt))

        words = dram("edge_words", (E + PAD, 1), I32)
        y_table = dram("y_table", (NP * R, C))
        y_rows = y_table.rearrange("(n r) c -> n (r c)", r=R)
        xnt_d = dram("xn_t", (NT, P, C))
        hgt_d = dram("hgate_t", (NT, 64, P))
        xm_d = dram("x_mixed", (NP, C))
        x1_d = dram("x_1", (NP, C))
        swt_d = dram("slice_weights_t", (NT, P, 512))
        x2_d = dram("x_2", (NP, C))
        xn3_d = dram("xn_3", (NP, C))
        xnt3_d = dram("xn_3_t", (NT, P, C))
        x34_d = dram("x_3_plus_xn_4", (NP, C))
        xnt4_d = dram("xn_4_t", (NT, P, C))

        acc = sb("acc", [P, NT, C])
        idx_t = sb("idx_t", [P, TW], I32)
        dl_t = sb("dl_t", [P, TW])
        typ_t = sb("typ_t", [P, TW])
        win = sb("win", [1, TW], I32)
        cnt = sb("cnt", [P, NT, R])
        rdeg = sb("rdeg", [P, NT])
        rc3 = sb("rc3", [P, NT, 3 * R], BF16)
        ident = sb("ident", [P, P])
        identb = sb("identb", [P, P], BF16)
        iota = sb("iota", [P, P])
        ones = sb("ones", [P, P])
        bd32 = sb("bd32", [P, P])
        bd64 = sb("bd64", [P, P])
        off64 = sb("off64", [P, P])
        mhalf = sb("mhalf", [P, 16])
        arena = sb("arena", [P, 30000])
        bank = [ctx.enter_context(nc.psum_tensor(f"bank{i}", [P, 512], FP32)) for i in range(8)]

        class Arena:
            def __init__(self, at=0):
                self.at = at

            def take(self, cols, dt=FP32, parts=P):
                words_ = cols if dt != BF16 else -(-cols // 2)
                a = arena[0:parts, self.at:self.at + words_]
                self.at += words_
                assert self.at <= 30000, self.at
                return a if dt == FP32 else a.bitcast(dt)

        ar = Arena()
        e_src = ar.take(ECOLS, I32, EROWS)
        e_dst = ar.take(ECOLS, I32, EROWS)
        e_typ = ar.take(ECOLS, I32, EROWS)
        e_pad = ar.take(PAD // PROWS, I32, PROWS)
        r_word = ar.take(TB * P, I32)
        r_int = ar.take(TB * P, I32)
        r_dst = ar.take(TB * P)
        r_idx = ar.take(TB * P)
        r_dl = ar.take(TB * P)
        r_next = ar.take(TB, I32)
        r_w0i = ar.take(TB, I32)
        r_w0 = ar.take(TB)
        r_w1i = ar.take(TB, I32)
        r_w1 = ar.take(TB)
        r_sel = ar.take(TB * (NT - 1))
        r_sel2 = ar.take(TB * (NT - 1))
        x_base = ar.take(NT - 1)
        iota_i = ar.take(P, I32)
        col_i = ar.take(1, I32)
        blk_i = ar.take(2, I32)
        blk_f = ar.take(2)
        row_b = ar.take(P)
        row_bi = ar.take(P, I32)

        ar = Arena()
        w_all = ar.take(KC * R * C).rearrange("p (k n) -> p k n", k=KC)
        w_root = ar.take(KC * C).rearrange("p (k n) -> p k n", k=KC)
        w_k0 = ar.take(KC * C).rearrange("p (k n) -> p k n", k=KC)
        w_v0 = ar.take(KC * C).rearrange("p (k n) -> p k n", k=KC)
        wg1_raw = ar.take(KC * 64).rearrange("p (k n) -> p k n", k=KC)
        wg1 = ar.take(KC * 64).rearrange("p (k n) -> p k n", k=KC)
        lng = ar.take(KC)
        lnb = ar.take(KC)
        lnb_b = ar.take(KC * P).rearrange("p (k n) -> p k n", k=KC)
        bg1_b = ar.take(64)
        wg1_sum = ar.take(64)
        gate_b = ar.take(64)
        bias0_b = ar.take(C)
        kmax = ar.take(NT * KC).rearrange("p (t k) -> p t k", k=KC)
        kmax1 = ar.take(KC)
        negmax = ar.take(C, FP32, 1)
        xin = [ar.take(C) for _ in range(2)]
        xn = [ar.take(C + 1) for _ in range(2)]
        stats = [ar.take(6) for _ in range(2)]
        mv = [ar.take(2) for _ in range(2)]
        veps = [ar.take(16) for _ in range(2)]
        rstd = [ar.take(16) for _ in range(2)]
        gstats = [ar.take(6) for _ in range(2)]
        gmv = [ar.take(2) for _ in range(2)]
        gveps = [ar.take(1) for _ in range(2)]
        grstd = [ar.take(1) for _ in range(2)]
        xnt = [ar.take(C) for _ in range(2)]
        ysb = [ar.take(R * C) for _ in range(2)]
        g_a = [ar.take(64) for _ in range(2)]
        g_b = [ar.take(64) for _ in range(2)]
        hg = [ar.take(64) for _ in range(2)]
        hgt = [ar.take(P, FP32, 64) for _ in range(2)]
        after_norm0 = ar.at

        ar = Arena(after_norm0)
        ring = [ar.take(C) for _ in range(BODY)]
        idx_s = ar.take(BODY, I32)
        oh = [ar.take(GRP * P).rearrange("p (j n) -> p j n", j=GRP) for _ in range(2)]
        woh = [ar.take(GRP * P).rearrange("p (j n) -> p j n", j=GRP) for _ in range(2)]
        ohb = [ar.take(GRP * P, BF16).rearrange("p (j n) -> p j n", j=GRP) for _ in range(BPB)]
        tohb = [ar.take(GRP * R, BF16).rearrange("p (j n) -> p j n", j=GRP) for _ in range(BPB)]
        oht = [ar.take(GRP * P, BF16) for _ in range(2)]
        wsel = [ar.take(GRP * 3 * R).rearrange("p (j k n) -> p j k n", j=GRP, k=3) for _ in range(2)]
        wgt = [ar.take(GRP) for _ in range(2)]
        zerob = ar.take(512, BF16)
        rc_rest = ar.take(NT * R).rearrange("p (w r) -> p w r", r=R)
        rc_part = ar.take(NT * R).rearrange("p (w r) -> p w r", r=R)

        ar = Arena(0)
        w_qt = ar.take(KC * C).rearrange("p (k n) -> p k n", k=KC)
        w_qc = ar.take(KC * C).rearrange("p (k n) -> p k n", k=KC)
        w_proj = ar.take(KC * C).rearrange("p (k n) -> p k n", k=KC)
        bproj_b = ar.take(C)
        wg2 = ar.take(C, FP32, 64)
        bg2 = ar.take(C, FP32, 1)
        bdc = ar.take(KC * P).rearrange("p (k n) -> p k n", k=KC)
        cden = ar.take(KC)
        assert ar.at <= KC * R * C
        ar = Arena(after_norm0)
        m_xnt = [ar.take(C) for _ in range(2)]
        m_ek = [ar.take(C) for _ in range(2)]
        m_v = [ar.take(2 * (P + 1)) for _ in range(2)]
        m_hgt = [ar.take(P, FP32, 64) for _ in range(2)]
        m_x = [ar.take(C) for _ in range(2)]
        m_sig = [ar.take(C) for _ in range(2)]
        m_pr = [ar.take(C) for _ in range(2)]
        m_prt = [ar.take(C) for _ in range(2)]
        m_xb = [ar.take(C) for _ in range(2)]
        m_out = [ar.take(C) for _ in range(2)]

        ar = Arena()
        wx_t = ar.take(4 * C).rearrange("p (j n) -> p j n", j=4)
        w_fx = ar.take(KC * 512).rearrange("p (k n) -> p k n", k=KC)
        w_out = ar.take(4 * C).rearrange("p (j n) -> p j n", j=4)
        w_log = ar.take(KC * 512).rearrange("p (k n) -> p k n", k=KC)
        b_log = ar.take(512, FP32, 1)
        bslice8 = ar.take(512, FP32, 1)
        bx_c = ar.take(4)
        temp_c = ar.take(8, FP32, 1)
        rtemp_r = ar.take(8, FP32, 1)
        rtemp_b = ar.take(8)
        bfx_b = ar.take(512)
        wsl_bd = ar.take(P)
        wq_bd = ar.take(P)
        wk_bd = ar.take(P)
        wv_bd = ar.take(P)
        bout_r = ar.take(C, FP32, 1)
        f_m = ar.take(4 * C).rearrange("p (j n) -> p j n", j=4)
        after_ffn_w = ar.at
        f_u = ar.take(4 * 257).rearrange("p (j n) -> p j n", j=4)
        f_ut = ar.take(KC * 512).rearrange("p (k n) -> p k n", k=KC)
        f_den = ar.take(4)
        f_rden = ar.take(4)
        f_tok = ar.take(512)
        f_tok2 = ar.take(512)
        f_tokt = ar.take(512)
        f_qt = ar.take(512)
        f_kt = ar.take(512)
        f_v = ar.take(512)
        f_s = ar.take(512)
        f_s2 = ar.take(512)
        f_max = ar.take(4)
        f_sum = ar.take(4)
        f_rsum = ar.take(4)
        f_at = ar.take(512)
        f_ost = ar.take(512)
        a_x1 = [ar.take(C) for _ in range(2)]
        a_xin = [ar.take(C) for _ in range(2)]
        a_xn = [ar.take(C + 1) for _ in range(2)]
        a_xnt = [ar.take(C) for _ in range(2)]
        a_stats = [ar.take(6) for _ in range(2)]
        a_mv = [ar.take(2) for _ in range(2)]
        a_veps = [ar.take(1) for _ in range(2)]
        a_rstd = [ar.take(1) for _ in range(2)]
        a_max = [ar.take(8) for _ in range(2)]
        a_sum = [ar.take(8) for _ in range(2)]
        a_rsum = [ar.take(8) for _ in range(2)]
        a_lg = [ar.take(512) for _ in range(2)]
        a_ex = [ar.take(512) for _ in range(2)]
        a_sw = [ar.take(512) for _ in range(2)]
        a_swt = [ar.take(512) for _ in range(2)]
        after_a = ar.at
        ar = Arena(after_a)
        w_kv1 = ar.take(KC * 1024).rearrange("p (k n) -> p k n", k=KC)
        kv_mean = ar.take(KC * 16).rearrange("p (k n) -> p k n", k=KC)
        k_swt = [ar.take(512) for _ in range(2)]
        k_x1 = [ar.take(C) for _ in range(2)]
        k_x2 = [ar.take(C) for _ in range(2)]
        k_sq = [ar.take(1024) for _ in range(2)]
        k_ss = [ar.take(16) for _ in range(2)]
        k_v1 = [ar.take(16) for _ in range(2)]
        k_pv = [ar.take(8) for _ in range(2)]
        k_rs = [ar.take(8) for _ in range(2)]
        k_kn = [ar.take(512) for _ in range(2)]
        k_v = [ar.take(512) for _ in range(2)]
        ar = Arena()
        w_q1 = ar.take(4 * C).rearrange("p (j n) -> p j n", j=4)
        w_o1t = ar.take(4 * C).rearrange("p (j n) -> p j n", j=4)
        w_neigh = ar.take(KC * C).rearrange("p (k n) -> p k n", k=KC)
        w_self = ar.take(KC * C).rearrange("p (k n) -> p k n", k=KC)
        w_comb = ar.take(KC * C).rearrange("p (k n) -> p k n", k=KC)
        w_rt = ar.take(KC * 8).rearrange("p (k n) -> p k n", k=KC)
        b_self = ar.take(C, FP32, 1)
        b_out1 = ar.take(C, FP32, 1)
        b_comb = ar.take(C, FP32, 1)
        d_bd = ar.take(512)
        d_t1 = ar.take(4 * C).rearrange("p (j n) -> p j n", j=4)
        logits = ar.take(NT * 8).rearrange("p (t e) -> p t e", e=8)
        comb = ar.take(NT * 8).rearrange("p (t e) -> p t e", e=8)
        ra = [ar.take(NT * 8).rearrange("p (t e) -> p t e", e=8) for _ in range(4)]
        rb = [ar.take(NT) for _ in range(6)]
        after_c = ar.at
        c_hn = [ar.take(C) for _ in range(2)]
        c_hnt = [ar.take(C) for _ in range(2)]
        c_xnt = [ar.take(C) for _ in range(2)]
        c_x2 = [ar.take(C) for _ in range(2)]
        c_x3 = [ar.take(C) for _ in range(2)]
        c_xn = [ar.take(C) for _ in range(2)]
        c_x34 = [ar.take(C) for _ in range(2)]
        c_x4t = [ar.take(C) for _ in range(2)]
        c_stats = [ar.take(6) for _ in range(2)]
        c_mv = [ar.take(2) for _ in range(2)]
        c_veps = [ar.take(1) for _ in range(2)]
        c_rstd = [ar.take(1) for _ in range(2)]
        assert ar.at < after_norm0
        ar = Arena(after_c)
        w1_sb = ar.take(8 * KC * C).rearrange("p (e k n) -> p e k n", e=8, k=KC)
        w2_sb = ar.take(8 * KC * C).rearrange("p (e k n) -> p e k n", e=8, k=KC)
        b1_c = ar.take(16).rearrange("p (e k) -> p e k", k=KC)
        b2_sb = ar.take(C, FP32, 8)
        s_xt = [ar.take(4 * C).rearrange("p (j k n) -> p j k n", j=4, k=KC) for _ in range(2)]
        s_o = [ar.take(4 * C).rearrange("p (j n) -> p j n", j=4) for _ in range(2)]
        s_ct = [ar.take(512, FP32, 8) for _ in range(2)]
        s_cg = [ar.take(32) for _ in range(2)]
        s_h = [[ar.take(512) for _ in range(KC)] for _ in range(2)]

        def upto(step, value):
            return sem(step), value + share.get(step, (step, 0))[1]

        def due(value):
            return not isinstance(value, int) or value > 0

        def alone(eng):
            eng.nop(nofuse=True)

        def node_tiles(eng):
            yield 0, 0, 0
            yield 1, 1, 0
            with eng.Fori(1, NT // 2) as i:
                yield 2 * i, 0, i
                yield 2 * i + 1, 1, i
            yield NT - 1, 0, NT // 2

        def expert_groups(eng):
            yield 0, 0, 0, 4
            yield 1, 1, 0, 4
            with eng.Fori(1, NT // 8) as i:
                yield 2 * i, 0, i, 4
                yield 2 * i + 1, 1, i, 4
            yield NT // 4, 0, NT // 8, 1

        def following(t, s, n):
            return t + 1, 1 - s, n + s

        def skewed(eng):
            none = (None, None, None)
            yield (0, 0, 0), none, None
            for t, s, n in node_tiles(eng):
                if is_last(t):
                    yield none, (t, s, n), None
                else:
                    yield following(t, s, n), (t, s, n), None

        def is_last(t):
            return isinstance(t, int) and t == NT - 1

        def rows_of(t):
            return LAST if is_last(t) else P

        def bodies(eng):
            yield 0
            with eng.Fori(1, T // BODY) as i:
                yield i

        phase = {}

        def phase_end(eng):
            k = phase[eng.engine] = phase.get(eng.engine, 0) + 1
            eng.drain().then_inc(sem("phase_ended"), 1)
            eng.wait_ge(sem("phase_ended"), 5 * k)
            return k >= stop_after

        def col(v, t):
            return v[:, t:t + 1] if isinstance(t, int) else v[:, bass.ds(t, 1)]

        def rows(v, t):
            return v[t * P:(t + 1) * P, :] if isinstance(t, int) else v[bass.ds(t * P, P), :]

        def tile(v, t):
            return v[t, :, :] if isinstance(t, int) else v[bass.ds(t, 1), :, :].rearrange("a p c -> (a p) c")

        def at(v, t):
            return v[:, t, :] if isinstance(t, int) else v[:, bass.ds(t, 1), :].rearrange("p a c -> p (a c)")

        def span(v, start, n):
            return v[:, start:start + n] if isinstance(start, int) else v[:, bass.ds(start, n)]

        def windows(eng, first, n):
            _, ws = nc.values_load_multi_w_load_instructions(
                span(win, first, n), engines=[eng.engine], min_val=0, max_val=NT - 1,
                skip_runtime_bounds_check_because="a target is below N, so its window is below NT")
            return list(ws)

        def copy_indices(act, pre, g, h, again):
            if due(again):
                act.wait_ge(*upto(f"{pre}_rows{h}", 16 * GRP * again))
            act.activation(idx_s[:, GRP * h:GRP * h + GRP], span(idx_t, g * GRP, GRP), ACT.Copy).then_inc(sem(f"{pre}_idx"), 1)

        def gather_rows(pool, pre, table):
            for i in bodies(pool):
                for h in range(BPB):
                    g = i * BPB + h
                    pool.wait_ge(*upto(f"{pre}_idx", g + 1))
                    alone(pool)
                    if due(i):
                        pool.wait_ge(*upto(f"{pre}_sum_mm", g - BPB + 1))
                        alone(pool)
                    for j in range(GRP):
                        k = GRP * h + j
                        pool.indirect_dma_start(
                            out=ring[k], out_offset=None, in_=table,
                            in_offset=bass.IndirectOffsetOnAxis(ap=idx_s[:, k:k + 1], axis=0),
                        ).then_inc(sem(f"{pre}_rows{h}"), 16)

        heads = lambda v, h=8: v.rearrange("p (h g) -> p h g", h=h)
        block = ctx.enter_context(nc.Block())

        @block.sync
        def _(sp):
            sp.dma_start(e_dst, dst.rearrange("(p c) -> p c", p=EROWS)).then_inc(sem("edges_in"), 16)
            sp.dma_start(e_src, src.rearrange("(p c) -> p c", p=EROWS)).then_inc(sem("edges_in"), 16)
            sp.dma_start(e_typ, etype.rearrange("(p c) -> p c", p=EROWS)).then_inc(sem("edges_in"), 16)
            sp.wait_ge(*upto("words_packed", 2))
            sp.dma_start(words[0:E, :].rearrange("(p c) o -> p (c o)", p=EROWS), e_dst).then_inc(sem("words_out"), 16)
            sp.dma_start(words[E:E + PAD, :].rearrange("(p c) o -> p (c o)", p=PROWS), e_pad).then_inc(sem("words_out"), 16)
            sp.wait_ge(*upto("words_out", 32))
            full = words[0:TB * P * P, :].rearrange("(b t e) o -> t b (e o)", t=P, e=P)
            sp.dma_start(r_word.rearrange("t (b e) -> t b e", b=TB), full).then_inc(sem("rows_in"), 16)
            nxt = words[P:P + TB * P * P, :].rearrange("(b t e) o -> t b (e o)", t=P, e=P)[:, :, 0:1]
            sp.dma_start(r_next.rearrange("t (b e) -> t b e", e=1), nxt, allow_slow_non_contiguous=True).then_inc(sem("rows_in"), 16)
            if phase_end(sp):
                return
            for n_, (d_, s_) in enumerate([
                    (w_all, gnn0_w.rearrange("(k p) n -> p k n", p=P)),
                    (w_root, gnn0_root.rearrange("(k p) n -> p k n", p=P)),
                    (w_k0, mix_wqkv[:, C:2 * C].rearrange("(k p) n -> p k n", p=P)),
                    (w_v0, mix_wqkv[:, 2 * C:3 * C].rearrange("(k p) n -> p k n", p=P)),
                    (wg1_raw, mix_wg1.rearrange("(k p) n -> p k n", p=P)),
                    (lng, mix_ln_g),
                    (lnb, mix_ln_b),
                    (bg1_b, mix_bg1.partition_broadcast(P)),
                    (bias0_b, gnn0_bias.partition_broadcast(P))]):
                sp.dma_start(d_, s_).then_inc(sem("w0_in"), 16)
            for t, s, n in node_tiles(sp):
                r = rows_of(t)
                if due(t - 1):
                    sp.wait_ge(*upto("n0_xn", t - 1))
                    alone(sp)
                source = x[(NT - 1) * P:N, :] if is_last(t) else rows(x, t)
                sp.dma_start(xin[s][0:r, :], source).then_inc(sem(f"n0_in{s}"), 16)
            if phase_end(sp):
                return
            if phase_end(sp):
                return
            if phase_end(sp):
                return
            for d_, s_ in [(w_qt, mix_wq_t.rearrange("(k p) n -> p k n", p=P)),
                           (w_proj, mix_wproj.rearrange("(k p) n -> p k n", p=P)),
                           (bproj_b, mix_bproj.partition_broadcast(P)),
                           (wg2, mix_wg2), (bg2, mix_bg2.rearrange("(a n) -> a n", a=1))]:
                sp.dma_start(d_, s_).then_inc(sem("w_mix_in"), 16)
            for t, s, n in node_tiles(sp):
                if due(t - 1):
                    sp.wait_ge(*upto("m1_v_mm", t - 1))
                    alone(sp)
                sp.dma_start(m_xnt[s], tile(xnt_d, t)).then_inc(sem(f"m1_in{s}"), 16)
            sp.wait_ge(*upto("m1_v_mm", NT))
            for t, s, n in node_tiles(sp):
                r = rows_of(t)
                if due(t - 1):
                    sp.wait_ge(*upto("m2_g_mm", t - 1))
                    alone(sp)
                if due(t - 1):
                    sp.wait_ge(*upto("m2_xb", t - 1))
                    alone(sp)
                sp.dma_start(m_xnt[s], tile(xnt_d, t)).then_inc(sem(f"m2_in{s}"), 16)
                sp.dma_start(m_hgt[s], tile(hgt_d, t)).then_inc(sem(f"m2_in{s}"), 16)
                source = x[(NT - 1) * P:N, :] if is_last(t) else rows(x, t)
                sp.dma_start(m_x[s][0:r, :], source).then_inc(sem(f"m2_in{s}"), 16)
            if phase_end(sp):
                return
            for d_, s_ in [(wx_t, ffn_wx_t.rearrange("(j p) n -> p j n", p=P)),
                           (w_fx, ffn_wfx.rearrange("(k p) n -> p k n", p=P)),
                           (w_out, ffn_wout.rearrange("(j p) n -> p j n", p=P)),
                           (bx_c, ffn_bx),
                           (temp_c, ffn_temp),
                           (bfx_b, ffn_bfx.partition_broadcast(P)),
                           (bout_r, ffn_bout.rearrange("(a n) -> a n", a=1))]:
                sp.dma_start(d_, s_).then_inc(sem("w_ffn_in"), 16)
            sp.wait_ge(*upto("bd_zeroed", 4))
            for d_, s_ in [(wsl_bd, ffn_wslice), (wq_bd, ffn_wq), (wk_bd, ffn_wk), (wv_bd, ffn_wv)]:
                for b_ in range(2):
                    sp.dma_start(d_[64 * b_:64 * b_ + 64, 64 * b_:64 * b_ + 64], s_).then_inc(sem("w_ffn_in"), 16)
            for h in range(8):
                sp.dma_start(bslice8[0:1, 64 * h:64 * h + 64], ffn_bslice.rearrange("(a n) -> a n", a=1)).then_inc(sem("w_ffn_in"), 16)
            for t, s, n in node_tiles(sp):
                if due(t - 1):
                    sp.wait_ge(*upto("f1_x1", t - 1))
                    alone(sp)
                sp.dma_start(a_xin[s], rows(xm_d, t)).then_inc(sem(f"f1_in{s}"), 16)
            if phase_end(sp):
                return
            sp.dma_start(w_kv1, mix1_wkv_t.rearrange("(k p) n -> p k n", p=P)).then_inc(sem("w_kv_in"), 16)
            for t, s, n in node_tiles(sp):
                if due(t - 1):
                    sp.wait_ge(*upto("f2_o_mm", t - 1))
                    alone(sp)
                if due(t - 1):
                    sp.wait_ge(*upto("f2_x2", t - 1))
                    alone(sp)
                sp.dma_start(k_swt[s], tile(swt_d, t)).then_inc(sem(f"f2_in{s}"), 16)
                sp.dma_start(k_x1[s], rows(x1_d, t)).then_inc(sem(f"f2_in{s}"), 16)
            if phase_end(sp):
                return
            for d_, s_ in [(w_q1, mix1_wqkv[0:512, :].rearrange("(j p) n -> p j n", p=P)),
                           (w_o1t, mix1_wout_t.rearrange("(j p) n -> p j n", p=P)),
                           (w_neigh, gnn1_wneigh_t.rearrange("(k p) n -> p k n", p=P)),
                           (w_self, gnn1_wself_t.rearrange("(k p) n -> p k n", p=P)),
                           (w_rt, router_t.rearrange("(k p) n -> p k n", p=P)),
                           (b_self, gnn1_bself.rearrange("(a n) -> a n", a=1)),
                           (b_out1, mix1_bout.rearrange("(a n) -> a n", a=1))]:
                sp.dma_start(d_, s_).then_inc(sem("w_l1_in"), 16)
            if phase_end(sp):
                return
            for t, s, n in node_tiles(sp):
                if due(t - 1):
                    sp.wait_ge(*upto("c_x_mm", t - 1))
                    alone(sp)
                if due(t - 1):
                    sp.wait_ge(*upto("c_x3", t - 1))
                    alone(sp)
                sp.dma_start(c_xnt[s], tile(xnt3_d, t)).then_inc(sem(f"c_in{s}"), 16)
                sp.dma_start(c_x2[s], rows(x2_d, t)).then_inc(sem(f"c_in{s}"), 16)
            if phase_end(sp):
                return
            sp.dma_start(w1_sb, w1.rearrange("e (k p) n -> p e k n", p=P)).then_inc(sem("w_moe_in"), 16)
            sp.dma_start(w2_sb, w2.rearrange("e (k p) n -> p e k n", p=P)).then_inc(sem("w_moe_in"), 16)
            sp.dma_start(b1_c, b1.rearrange("p (e k) -> p e k", k=KC)).then_inc(sem("w_moe_in"), 16)
            sp.dma_start(b2_sb, b2).then_inc(sem("w_moe_in"), 16)
            for g, s, n, m in expert_groups(sp):
                if due(16 * (g - 1)):
                    sp.wait_ge(*upto("s_h_mm", 16 * (g - 1)))
                    alone(sp)
                if due(16 * n):
                    sp.wait_ge(*upto(f"s_out{s}", 16 * n))
                    alone(sp)
                if m == 4:
                    xs = xnt4_d[4 * g:4 * g + 4, :, :] if isinstance(g, int) else xnt4_d[bass.ds(g * 4, 4), :, :]
                    os_ = x34_d[512 * g:512 * g + 512, :] if isinstance(g, int) else x34_d[bass.ds(g * 512, 512), :]
                else:
                    xs, os_ = xnt4_d[NT - 1:NT, :, :], x34_d[(NT - 1) * P:NP, :]
                sp.dma_start(s_xt[s][:, 0:m, :, :].rearrange("p j k n -> p j (k n)"),
                             xs.rearrange("j p c -> p j c")).then_inc(sem(f"s_in{s}"), 16)
                sp.dma_start(s_o[s][:, 0:m, :], os_.rearrange("(j p) c -> p j c", p=P)).then_inc(sem(f"s_in{s}"), 16)
            phase_end(sp)

        @block.gpsimd
        def _(pool):
            pool.iota(iota_i, pattern=[[1, P]], base=0, channel_multiplier=0).then_inc(sem("iotas"), 1)
            pool.iota(col_i, pattern=[[0, 1]], base=0, channel_multiplier=1).then_inc(sem("iotas"), 1)
            pool.memset(ones[:, :], 1.0).then_inc(sem("const"), 1)
            pool.memset(mhalf[:, :], -0.5).then_inc(sem("const"), 1)
            pool.memset(e_pad, PAD_DST << 16).then_inc(sem("words_packed"), 1)
            for v in (idx_t, dl_t):
                pool.memset(v[:, ET + NT - 1:TW], 0 if v is idx_t else -1.0).then_inc(sem("table_pad"), 1)
            pool.memset(win[:, ET + NT - 1:TW], NT - 1).then_inc(sem("table_pad"), 1)
            pool.memset(cnt[:, :, :], 0.0).then_inc(sem("const"), 1)
            if phase_end(pool):
                return
            for t, s, n in skewed(pool):
                if t[0] is not None:
                    t_, s_, n_ = t
                    pool.wait_ge(*upto("n0_var", t_ + 1))
                    alone(pool)
                    pool.tensor_tensor(rstd[s_][:, 0:1], veps[s_][:, 0:1], mhalf[:, 0:1], ALU.pow).then_inc(sem("n0_rstd"), 1)
                    pool.wait_ge(*upto("n0_gvar", t_ + 1))
                    alone(pool)
                    pool.tensor_tensor(grstd[s_], gveps[s_], mhalf[:, 0:1], ALU.pow).then_inc(sem("n0_grstd"), 1)
                if s[0] is not None:
                    t_, s_, n_ = s
                    pool.wait_ge(*upto("n0_xnt", t_ + 1))
                    alone(pool)
                    pool.dma_start(tile(xnt_d, t_), xnt[s_]).then_inc(sem(f"n0_xnt_out{s_}"), 16)
                    pool.wait_ge(*upto("n0_y_act", 2 * t_ + 2))
                    alone(pool)
                    pool.wait_ge(*upto("n0_y_dve", 2 * t_ + 2))
                    alone(pool)
                    pool.dma_start(rows(y_rows, t_), ysb[s_]).then_inc(sem(f"n0_y_out{s_}"), 16)
                    pool.wait_ge(*upto("n0_hgt", t_ + 1))
                    alone(pool)
                    pool.dma_start(tile(hgt_d, t_), hgt[s_]).then_inc(sem(f"n0_hgt_out{s_}"), 16)
            for s in range(2):
                v = NT // 2 + 1 - s
                for name in (f"n0_xnt_out{s}", f"n0_y_out{s}", f"n0_hgt_out{s}"):
                    pool.wait_ge(*upto(name, 16 * v))
            if phase_end(pool):
                return
            if phase_end(pool):
                return
            gather_rows(pool, "g0", y_table)
            if phase_end(pool):
                return
            for t, s, n in node_tiles(pool):
                pool.wait_ge(*upto("m2_out", t + 1))
                alone(pool)
                pool.dma_start(rows(xm_d, t), m_out[s]).then_inc(sem(f"m2_st{s}"), 16)
            for s in range(2):
                if due(16 * (NT // 2 + 1 - s)):
                    pool.wait_ge(*upto(f"m2_st{s}", 16 * (NT // 2 + 1 - s)))
                    alone(pool)
            if phase_end(pool):
                return
            for v in (wsl_bd, wq_bd, wk_bd, wv_bd):
                pool.memset(v, 0.0).then_inc(sem("bd_zeroed"), 1)
            for s in range(2):
                pool.memset(a_xn[s][:, C:C + 1], 1.0).then_inc(sem("a_ones"), 1)
            for t, s, n in skewed(pool):
                if t[0] is not None:
                    t_, s_, n_ = t
                    pool.wait_ge(*upto("f1_var", t_ + 1))
                    alone(pool)
                    pool.tensor_tensor(a_rstd[s_], a_veps[s_], mhalf[:, 0:1], ALU.pow).then_inc(sem("f1_rstd"), 1)
                    pool.dma_start(rows(x1_d, t_), a_x1[s_]).then_inc(sem(f"f1_x1_out{s_}"), 16)
                if s[0] is not None:
                    t_, s_, n_ = s
                    pool.wait_ge(*upto("f1_swt", t_ + 1))
                    alone(pool)
                    pool.dma_start(tile(swt_d, t_), a_swt[s_]).then_inc(sem(f"f1_swt_out{s_}"), 16)
            for s in range(2):
                if due(16 * (NT // 2 + 1 - s)):
                    pool.wait_ge(*upto(f"f1_x1_out{s}", 16 * (NT // 2 + 1 - s)))
                    alone(pool)
                if due(16 * (NT // 2 + 1 - s)):
                    pool.wait_ge(*upto(f"f1_swt_out{s}", 16 * (NT // 2 + 1 - s)))
                    alone(pool)
            if phase_end(pool):
                return
            for t, s, n in skewed(pool):
                if t[0] is not None:
                    t_, s_, n_ = t
                    pool.wait_ge(*upto("f2_var", t_ + 1))
                    alone(pool)
                    pool.tensor_tensor(a_rstd[s_], a_veps[s_], mhalf[:, 0:1], ALU.pow).then_inc(sem("f2_rstd"), 1)
                    pool.dma_start(rows(x2_d, t_), k_x2[s_]).then_inc(sem(f"f2_x2_out{s_}"), 16)
                    pool.wait_ge(*upto("f2_xn", t_ + 1))
                    alone(pool)
                    pool.dma_start(rows(xn3_d, t_), a_xn[s_][:, 0:C]).then_inc(sem(f"f2_xn_out{s_}"), 16)
                if s[0] is not None:
                    t_, s_, n_ = s
                    pool.wait_ge(*upto("f2_pv", t_ + 1))
                    alone(pool)
                    pool.tensor_tensor(k_rs[s_], k_pv[s_], mhalf[:, 0:8], ALU.pow).then_inc(sem("f2_krs"), 1)
                    pool.wait_ge(*upto("f2_xnt", t_ + 1))
                    alone(pool)
                    pool.dma_start(tile(xnt3_d, t_), a_xnt[s_]).then_inc(sem(f"f2_xnt_out{s_}"), 16)
            for s in range(2):
                for name in (f"f2_x2_out{s}", f"f2_xn_out{s}", f"f2_xnt_out{s}"):
                    pool.wait_ge(*upto(name, 16 * (NT // 2 + 1 - s)))
            if phase_end(pool):
                return
            gather_rows(pool, "g1", xn3_d)
            if phase_end(pool):
                return
            for t_, s_, n_ in node_tiles(pool):
                    pool.wait_ge(*upto("c_var", t_ + 1))
                    alone(pool)
                    pool.tensor_tensor(c_rstd[s_], c_veps[s_], mhalf[:, 0:1], ALU.pow).then_inc(sem("c_rstd"), 1)
                    pool.wait_ge(*upto("c_x34", t_ + 1))
                    alone(pool)
                    pool.dma_start(rows(x34_d, t_), c_x34[s_]).then_inc(sem(f"c_x34_out{s_}"), 16)
                    pool.wait_ge(*upto("c_x4t", t_ + 1))
                    alone(pool)
                    pool.dma_start(tile(xnt4_d, t_), c_x4t[s_]).then_inc(sem(f"c_x4t_out{s_}"), 16)
            for s in range(2):
                if due(16 * (NT // 2 + 1 - s)):
                    pool.wait_ge(*upto(f"c_x34_out{s}", 16 * (NT // 2 + 1 - s)))
                    alone(pool)
                if due(16 * (NT // 2 + 1 - s)):
                    pool.wait_ge(*upto(f"c_x4t_out{s}", 16 * (NT // 2 + 1 - s)))
                    alone(pool)
            if phase_end(pool):
                return
            for g, s, n, m in expert_groups(pool):
                pool.wait_ge(*upto("s_acc", 32 * (g + 1) if m == 4 else 32 * g + 8))
                alone(pool)
                if m == 4:
                    o_ = out[512 * g:512 * g + 512, :] if isinstance(g, int) else out[bass.ds(g * 512, 512), :]
                    pool.dma_start(o_.rearrange("(j p) c -> p j c", p=P), s_o[s]).then_inc(sem(f"s_out{s}"), 16)
                else:
                    pool.dma_start(out[(NT - 1) * P:N, :], s_o[s][0:LAST, 0, :]).then_inc(sem(f"s_out{s}"), 16)
            pool.wait_ge(*upto("s_out0", 16 * (NT // 8 + 1)))
            pool.wait_ge(*upto("s_out1", 16 * (NT // 8)))
            phase_end(pool)

        @block.scalar
        def _(act):
            if phase_end(act):
                return
            for t, s, n in skewed(act):
                if t[0] is not None:
                    t_, s_, n_ = t
                    act.wait_ge(*upto("n0_t", t_ + 1))
                    if due(t_ - 1):
                        act.wait_ge(*upto("n0_km_mm", t_ - 1))
                    if due(16 * n_):
                        act.wait_ge(*upto(f"n0_xnt_out{s_}", 16 * n_))
                    act.activation(xnt[s_], bank[4][:, 0:C], ACT.Copy).then_inc(sem("n0_xnt"), 1)
                if s[0] is not None:
                    t_, s_, n_ = s
                    if due(16 * n_):
                        act.wait_ge(*upto(f"n0_y_out{s_}", 16 * n_))
                    for b_ in (0, 2):
                        act.wait_ge(*upto(f"n0_y_mm{b_}", t_ + 1))
                        act.activation(ysb[s_][:, 512 * b_:512 * b_ + 512], bank[b_][:, :], ACT.Copy).then_inc(sem("n0_y_act"), 1)
                    act.wait_ge(*upto("n0_gate", t_ + 1))
                    if due(t_ - 1):
                        act.wait_ge(*upto("n0_hg_t", t_ - 1))
                    act.activation(hg[s_], g_b[s_], ACT.Gelu, scale=-1.0).then_inc(sem("n0_hg"), 1)
                    act.wait_ge(*upto("n0_hg_t", t_ + 1))
                    if due(16 * n_):
                        act.wait_ge(*upto(f"n0_hgt_out{s_}", 16 * n_))
                    act.activation(hgt[s_], bank[7][0:64, 0:P], ACT.Copy).then_inc(sem("n0_hgt"), 1)
            if phase_end(act):
                return
            if phase_end(act):
                return
            def copy_oht(g, b_):
                act.wait_ge(*upto("g0_oht_mm", g + 1))
                if due(g - 1):
                    act.wait_ge(*upto("g0_look_mm", g - 1))
                act.activation(oht[b_], bank[6][:, :], ACT.Copy).then_inc(sem("g0_oht"), 1)

            for g in range(BPB):
                copy_indices(act, "g0", g, g, 0)
            for g in range(2):
                copy_oht(g, g)
            for i in bodies(act):
                for h in range(BPB):
                    g = i * BPB + h
                    copy_oht(g + 2, h % 2)
                    copy_indices(act, "g0", g + BPB, h, i + 1)
            if phase_end(act):
                return
            for t, s, n in node_tiles(act):
                act.wait_ge(*upto("m1_k_mm", t + 1))
                if due(t - 1):
                    act.wait_ge(*upto("m1_ctx_mm", t - 1))
                act.activation(m_ek[s], bank[s][:, 0:C], ACT.Exp).then_inc(sem("m1_ek"), 1)
            for t, s, n in node_tiles(act):
                act.wait_ge(*upto("m2_g_mm", t + 1))
                if due(t - 1):
                    act.wait_ge(*upto("m2_pr", t - 1))
                act.activation(m_sig[s], bank[4 + s][:, 0:C], ACT.Sigmoid).then_inc(sem("m2_sig"), 1)
                act.wait_ge(*upto("m2_prt_mm", t + 1))
                if due(t - 1):
                    act.wait_ge(*upto("m2_f_mm", t - 1))
                act.activation(m_prt[s], bank[2][:, 0:C], ACT.Copy).then_inc(sem("m2_prt"), 1)
            if phase_end(act):
                return
            for t, s, n in skewed(act):
                if t[0] is not None:
                    t_, s_, n_ = t
                    act.wait_ge(*upto("f1_t", t_ + 1))
                    if due(t_ - 1):
                        act.wait_ge(*upto("f1_l_mm", t_ - 1))
                    act.activation(a_xnt[s_], bank[0][:, 0:C], ACT.Copy).then_inc(sem("f1_xnt"), 1)
                if s[0] is not None:
                    t_, s_, n_ = s
                    act.wait_ge(*upto("f1_lg", t_ + 1))
                    if due(t_ - 1):
                        act.wait_ge(*upto("f1_sw", t_ - 1))
                    act.activation(a_ex[s_], a_lg[s_], ACT.Exp).then_inc(sem("f1_ex"), 1)
                    act.wait_ge(*upto("f1_swt_mm", t_ + 1))
                    if due(16 * n_):
                        act.wait_ge(*upto(f"f1_swt_out{s_}", 16 * n_))
                    act.activation(a_swt[s_], bank[3][:, :], ACT.Copy).then_inc(sem("f1_swt"), 1)
            for j in range(4):
                act.wait_ge(*upto("fs_max", j + 1))
                act.activation(f_s2[:, P * j:P * j + P], f_s[:, P * j:P * j + P], ACT.Exp, bias=f_max[:, j:j + 1],
                               scale=1.0, accum_out=f_sum[:, j:j + 1]).then_inc(sem("fs_exp"), 1)
            if phase_end(act):
                return
            for t_, s_, n_ in node_tiles(act):
                    act.wait_ge(*upto("f2_t", t_ + 1))
                    if due(t_ - 1):
                        act.wait_ge(*upto("f2_kv_mm", t_ - 1))
                    if due(16 * n_):
                        act.wait_ge(*upto(f"f2_xnt_out{s_}", 16 * n_))
                    act.activation(a_xnt[s_], bank[1][:, 0:C], ACT.Copy).then_inc(sem("f2_xnt"), 1)
                    act.wait_ge(*upto("f2_kv_mm", t_ + 1))
                    if due(t_ - 1):
                        act.wait_ge(*upto("f2_ss", t_ - 1))
                    act.activation(k_sq[s_][:, 0:512], bank[2][:, :], ACT.Square).then_inc(sem("f2_sq"), 1)
                    act.activation(k_sq[s_][:, 512:1024], bank[3][:, :], ACT.Square).then_inc(sem("f2_sq"), 1)
                    if due(t_ - 1):
                        act.wait_ge(*upto("f2_dots_mm", t_ - 1))
                    act.activation(k_v[s_], bank[3][:, :], ACT.Copy).then_inc(sem("f2_v"), 1)
            if phase_end(act):
                return
            for g in range(BPB):
                copy_indices(act, "g1", g, g, 0)
            for i in bodies(act):
                for h in range(BPB):
                    copy_indices(act, "g1", (i + 1) * BPB + h, h, i + 1)
            if phase_end(act):
                return
            for t, s, n in skewed(act):
                if t[0] is not None:
                    t_, s_, n_ = t
                    act.wait_ge(*upto("c_hn_t", t_ + 1))
                    if due(t_ - 1):
                        act.wait_ge(*upto("c_x_mm", t_ - 1))
                    act.activation(c_hnt[s_], bank[0][:, 0:C], ACT.Copy).then_inc(sem("c_hnt"), 1)
                if s[0] is not None:
                    t_, s_, n_ = s
                    act.wait_ge(*upto("c_x4_t", t_ + 1))
                    if due(t_ - 1):
                        act.wait_ge(*upto("c_r_mm", t_ - 1))
                    if due(16 * n_):
                        act.wait_ge(*upto(f"c_x4t_out{s_}", 16 * n_))
                    act.activation(c_x4t[s_], bank[2][:, 0:C], ACT.Copy).then_inc(sem("c_x4t"), 1)
            act.wait_ge(*upto("r_exp_in", 1))
            act.activation(ra[1], ra[0], ACT.Exp).then_inc(sem("r_exp"), 1)
            if phase_end(act):
                return
            for g, s, n, m in expert_groups(act):
                act.wait_ge(*upto("s_ct_mm", g + 1))
                if due(g - 1):
                    act.wait_ge(*upto("s_cb_mm", g - 1))
                act.activation(s_ct[s][:, 0:m * P], bank[6][0:8, 0:m * P], ACT.Copy).then_inc(sem("s_ct"), 1)
                act.wait_ge(*upto("w_moe_in", 64))
                for e in range(8):
                    for f in range(KC):
                        k = 16 * g + 2 * e + f
                        act.wait_ge(*upto("s_h_mm", k + 1))
                        if due(8 * g + e - 1):
                            act.wait_ge(*upto("s_y_mm", 8 * g + e - 1))
                        act.activation(s_h[e % 2][f][:, 0:m * P], bank[2 * (e % 2) + f][:, 0:m * P], ACT.Gelu,
                                       bias=b1_c[:, e, f:f + 1]).then_inc(sem("s_h"), 1)
            phase_end(act)

        @block.vector
        def _(dve):
            step = [0]

            def chain(ins):
                step[0] += 1
                ins.then_inc(sem("dve_chain"), 1)
                dve.wait_ge(sem("dve_chain"), step[0])

            dve.wait_ge(*upto("iotas", 2))
            chain(dve.tensor_copy(iota[:, :], iota_i))
            chain(dve.tensor_copy(blk_f[:, 0:1], col_i))
            chain(dve.tensor_scalar(ident[:, :], iota[:, :], blk_f[:, 0:1], None, ALU.is_equal))
            chain(dve.tensor_copy(identb[:, :], ident[:, :]))
            for bd, sh in ((bd32, 5), (bd64, 6)):
                chain(dve.tensor_scalar(row_bi, iota_i, sh, None, ALU.arith_shift_right))
                chain(dve.tensor_copy(row_b, row_bi))
                chain(dve.tensor_scalar(blk_i[:, 0:1], col_i, sh, None, ALU.arith_shift_right))
                chain(dve.tensor_copy(blk_f[:, 1:2], blk_i[:, 0:1]))
                chain(dve.tensor_scalar(bd[:, :], row_b, blk_f[:, 1:2], None, ALU.is_equal))
            chain(dve.tensor_scalar(off64[:, :], bd64[:, :], -1.0, 1e30, ALU.add, ALU.mult))
            dve.wait_ge(*upto("edges_in", 48))
            chain(dve.scalar_tensor_tensor(e_src, e_src, 3, e_typ, ALU.logical_shift_left, ALU.bitwise_or))
            dve.scalar_tensor_tensor(e_dst, e_dst, 16, e_src, ALU.logical_shift_left, ALU.bitwise_or).then_inc(sem("words_packed"), 1)
            dve.wait_ge(*upto("rows_in", 32))
            chain(dve.tensor_scalar(r_int, r_word, 16, None, ALU.logical_shift_right))
            chain(dve.tensor_copy(r_dst, r_int))
            r_first = r_int.rearrange("t (b e) -> t b e", b=TB)[:, :, 0]
            chain(dve.tensor_scalar(r_w0i, r_first, 7, None, ALU.logical_shift_right))
            chain(dve.tensor_copy(r_w0, r_w0i))
            chain(dve.tensor_scalar(r_w1i, r_next, 23, None, ALU.logical_shift_right))
            chain(dve.tensor_copy(r_w1, r_w1i))
            chain(dve.tensor_scalar(r_int, r_word, 0xFFFF, None, ALU.bitwise_and))
            chain(dve.tensor_copy(r_idx, r_int))
            for b_ in range(TB):
                cols = slice(P * b_, P * b_ + P)
                chain(dve.tensor_scalar(r_dl[:, cols], r_w0[:, b_:b_ + 1].broadcast_to([P, P]), -float(P), None, ALU.mult))
                chain(dve.tensor_tensor(r_dl[:, cols], r_dl[:, cols], r_dst[:, cols], ALU.add))
                sc = slice((NT - 1) * b_, (NT - 1) * (b_ + 1))
                dve.tensor_scalar(r_sel[:, sc], iota[:, 1:NT], r_w0[:, b_:b_ + 1], None, ALU.is_gt).then_inc(sem("sel"), 1)
                dve.tensor_scalar(r_sel2[:, sc], iota[:, 1:NT], r_w1[:, b_:b_ + 1], None, ALU.is_gt).then_inc(sem("sel"), 1)
            dve.wait_ge(*upto("sel", 2 * TB))
            dve.tensor_tensor(r_sel, r_sel, r_sel2, ALU.subtract).then_inc(sem("rows_ready"), 1)
            dve.tensor_scalar(x_base, iota[:, 1:NT], float(P), None, ALU.mult).then_inc(sem("x_base"), 1)
            for b_ in range(TB):
                n_ = min(P, ET - P * b_)
                cols = slice(P * b_, P * b_ + n_)
                if due(3 * b_ + 3):
                    dve.wait_ge(*upto("tables_mm", 3 * b_ + 3))
                dve.tensor_copy(dl_t[:, cols], bank[b_ % 2][:, 0:n_]).then_inc(sem("tables"), 1)
                dve.tensor_copy(idx_t[:, cols], bank[b_ % 2][:, P:P + n_]).then_inc(sem("tables"), 1)
                dve.tensor_copy(win[:, cols], bank[b_ % 2][0:1, 2 * P:2 * P + n_]).then_inc(sem("tables"), 1)
            cols = slice(ET, ET + NT - 1)
            dve.wait_ge(*upto("extra_mm", 2))
            dve.wait_ge(*upto("x_base", 1))
            dve.tensor_tensor(dl_t[:, cols], bank[2][:, 0:NT - 1], x_base, ALU.subtract).then_inc(sem("tables"), 1)
            dve.tensor_copy(idx_t[:, cols], bank[3][:, 0:NT - 1]).then_inc(sem("tables"), 1)
            dve.tensor_copy(win[:, cols], iota[0:1, 1:NT]).then_inc(sem("tables"), 1)
            dve.wait_ge(*upto("tables", 3 * TB + 3))
            dve.wait_ge(*upto("table_pad", 3))
            ti = typ_t[:, :].bitcast(I32)
            chain(dve.tensor_scalar(ti, idx_t[:, :], 7, None, ALU.bitwise_and))
            chain(dve.tensor_copy(typ_t[:, :], ti))
            if phase_end(dve):
                return
            dve.wait_ge(*upto("w0_in", 16 * 9))
            for k in range(KC):
                dve.tensor_scalar(wg1[:, k, :], wg1_raw[:, k, :], lng[:, k:k + 1], None, ALU.mult).then_inc(sem("gate_w"), 1)
                dve.tensor_copy(lnb_b[:, k, :], lnb[:, k:k + 1].broadcast_to([P, P])).then_inc(sem("gate_w"), 1)
            dve.wait_ge(*upto("gate_w_mm", 2))
            chain(dve.tensor_copy(wg1_sum, bank[7][:, 0:64]))
            dve.tensor_tensor(gate_b, bank[6][:, 0:64], bg1_b, ALU.add).then_inc(sem("gate_b"), 1)
            dve.wait_ge(*upto("gate_b", 1))

            def norm(pre, src_, dst_, st, mv_, ve, rs, t, ready, free):
                dve.wait_ge(*upto(*ready))
                dve.bn_stats(st, src_).then_inc(sem(pre + "_st"), 1)
                dve.wait_ge(*upto(pre + "_st", t + 1))
                alone(dve)
                dve.bn_aggr(mv_, st).then_inc(sem(pre + "_ag"), 1)
                dve.wait_ge(*upto(pre + "_ag", t + 1))
                dve.tensor_scalar(ve, mv_[:, 1:2], EPS, None, ALU.add).then_inc(sem(pre + "_var"), 1)
                dve.wait_ge(*upto(pre + "_rstd", t + 1))
                for f_ in free:
                    if due(f_[1]):
                        dve.wait_ge(*upto(*f_))
                dve.tensor_scalar(dst_, src_, mv_[:, 0:1], rs, ALU.subtract, ALU.mult).then_inc(sem(pre + "_xn"), 1)

            for t, s, n in skewed(dve):
                if t[0] is not None:
                    t_, s_, n_ = t
                    norm("n0", xin[s_], xn[s_][:, 0:C], stats[s_], mv[s_], veps[s_][:, 0:1], rstd[s_][:, 0:1], t_,
                         (f"n0_in{s_}", 16 * (n_ + 1)), [("n0_t", t_ - 1)])
                    dve.wait_ge(*upto("n0_xn", t_ + 1))
                    dve.bn_stats(gstats[s_], xn[s_][:, 0:C]).then_inc(sem("n0_gst"), 1)
                    dve.wait_ge(*upto("n0_gst", t_ + 1))
                    alone(dve)
                    dve.bn_aggr(gmv[s_], gstats[s_]).then_inc(sem("n0_gag"), 1)
                    dve.wait_ge(*upto("n0_gag", t_ + 1))
                    dve.tensor_scalar(gveps[s_], gmv[s_][:, 1:2], EPS, None, ALU.add).then_inc(sem("n0_gvar"), 1)
                if s[0] is not None:
                    t_, s_, n_ = s
                    if due(16 * n_):
                        dve.wait_ge(*upto(f"n0_y_out{s_}", 16 * n_))
                    for b_ in (1, 3):
                        dve.wait_ge(*upto(f"n0_y_mm{b_}", t_ + 1))
                        dve.tensor_copy(ysb[s_][:, 512 * b_:512 * b_ + 512], bank[b_][:, :]).then_inc(sem("n0_y_dve"), 1)
                    dve.wait_ge(*upto("n0_root_mm", t_ + 1))
                    dve.tensor_tensor(at(acc, t_), bank[5][:, 0:C], bias0_b, ALU.add).then_inc(sem("n0_root"), 1)
                    dve.wait_ge(*upto("n0_grstd", t_ + 1))
                    dve.scalar_tensor_tensor(g_a[s_], wg1_sum, gmv[s_][:, 0:1], bank[5][:, C:C + 64], ALU.mult, ALU.subtract).then_inc(sem("n0_ga"), 1)
                    dve.wait_ge(*upto("n0_ga", t_ + 1))
                    if due(t_ - 1):
                        dve.wait_ge(*upto("n0_hg", t_ - 1))
                    dve.scalar_tensor_tensor(g_b[s_], g_a[s_], grstd[s_], gate_b, ALU.mult, ALU.subtract).then_inc(sem("n0_gate"), 1)
                    dve.wait_ge(*upto("n0_km_mm", t_ + 1))
                    dve.tensor_reduce(at(kmax, t_), bank[6][:, 0:C].rearrange("p (k n) -> p k n", k=KC)[:, :, 0:rows_of(t_)],
                                      AX, ALU.max).then_inc(sem("n0_km"), 1)
            dve.wait_ge(*upto("n0_km", NT))
            dve.tensor_reduce(kmax1, kmax.rearrange("p t k -> p k t"), AX, ALU.max).then_inc(sem("kmax"), 1)
            dve.wait_ge(*upto("kmax_mm", 1))
            dve.tensor_scalar(negmax, bank[0][0:1, 0:C], -1.0, None, ALU.mult).then_inc(sem("negmax"), 1)
            if phase_end(dve):
                return

            def one_hots(v, wide, values, g):
                return dve.tensor_tensor(v, iota[:, 0:wide].unsqueeze(1).broadcast_to([P, GRP, wide]),
                                         span(values, g * GRP, GRP).unsqueeze(2).broadcast_to([P, GRP, wide]), ALU.is_equal)

            dve.memset(zerob, 0.0).then_inc(sem("zerob"), 1)
            for i in bodies(dve):
                for h in range(BPB):
                    g = i * BPB + h
                    if due(g - BPB + 1):
                        dve.wait_ge(*upto("ct_mm", g - BPB + 1))
                    one_hots(ohb[h], P, dl_t, g).then_inc(sem("ct_oh"), 1)
                    one_hots(tohb[h], R, typ_t, g).then_inc(sem("ct_oh"), 1)
            dve.wait_ge(*upto("ct_mm", NG))
            chain(dve.tensor_copy(cnt[:, :, :], bank[7][:, 0:NT * R].rearrange("p (w r) -> p w r", r=R)))
            chain(dve.tensor_reduce(rdeg[:, :], cnt[:, :, :], AX, ALU.add))
            chain(dve.tensor_scalar(rdeg[:, :], rdeg[:, :], 1.0, None, ALU.max))
            chain(dve.reciprocal(rdeg[:, :], rdeg[:, :]))
            chain(dve.tensor_scalar(cnt[:, :, :], cnt[:, :, :], 1.0, None, ALU.max))
            chain(dve.reciprocal(cnt[:, :, :], cnt[:, :, :]))
            rest = cnt[:, :, :]
            for k in range(3):
                part = rc3[:, :, R * k:R * k + R]
                chain(dve.tensor_copy(part, rest))
                if k < 2:
                    chain(dve.tensor_copy(rc_part, part))
                    chain(dve.tensor_tensor(rc_rest, rest, rc_part, ALU.subtract))
                    rest = rc_rest
            if phase_end(dve):
                return

            def add_sums(pre, g, ws, b_):
                dve.wait_ge(*upto(pre + "_sum_mm", g + 1))
                for j in range(GRP):
                    if due(g * GRP + j):
                        dve.wait_ge(*upto(pre + "_add", g * GRP + j))
                    dve.tensor_tensor(at(acc, ws[j]), at(acc, ws[j]), bank[2 * b_ + j // 2][:, C * (j % 2):C * (j % 2) + C],
                                      ALU.add).then_inc(sem(pre + "_add"), 1)

            def sum_windows(i):
                if isinstance(i, int):
                    return [None] * GRP + windows(dve, 0, BODY - GRP)
                return windows(dve, i * BODY - GRP, BODY)

            def targets(g, h):
                if due(g - BPB + 1):
                    dve.wait_ge(*upto("g0_oht_mm", g - BPB + 1))
                    dve.wait_ge(*upto("g0_woh", g - BPB + 1))
                one_hots(ohb[h], P, dl_t, g).then_inc(sem("g0_oh"), 1)
                one_hots(tohb[h], R, typ_t, g).then_inc(sem("g0_toh"), 1)

            def weights(g, h):
                b_ = h % 2
                dve.wait_ge(*upto("g0_toh", g + 1))
                dve.wait_ge(*upto("g0_look_mm", g + 1))
                if due(g - 1):
                    dve.wait_ge(*upto("g0_wgt", g - 1))
                dve.tensor_tensor(wsel[b_], tohb[h].unsqueeze(2).broadcast_to([P, GRP, 3, R]),
                                  bank[7][:, 0:GRP * 3 * R].rearrange("p (j k n) -> p j k n", j=GRP, k=3), ALU.mult).then_inc(sem("g0_wsel"), 1)
                dve.wait_ge(*upto("g0_wsel", g + 1))
                dve.tensor_reduce(wgt[b_], wsel[b_].rearrange("p j k n -> p j (k n)"), AX, ALU.add).then_inc(sem("g0_wgt"), 1)
                dve.wait_ge(*upto("g0_wgt", g + 1))
                if due(g - 1):
                    dve.wait_ge(*upto("g0_sum_mm", g - 1))
                dve.tensor_tensor(woh[b_], ohb[h], wgt[b_].unsqueeze(2).broadcast_to([P, GRP, P]), ALU.mult).then_inc(sem("g0_woh"), 1)

            for g in range(3):
                targets(g, g)
            weights(0, 0)
            for i in bodies(dve):
                ws = sum_windows(i)
                for h in range(BPB):
                    g = i * BPB + h
                    targets(g + 3, (h + 3) % BPB)
                    weights(g + 1, (h + 1) % BPB)
                    if due(g):
                        add_sums("g0", g - 1, ws[GRP * h:GRP * h + GRP], (h + 1) % 2)
            add_sums("g0", NG - 1, windows(dve, T - GRP, GRP), 1)
            dve.wait_ge(*upto("g0_idx", NG + BPB))
            chain(dve.tensor_scalar(idx_t[:, :], idx_t[:, :], 3, None, ALU.logical_shift_right))
            if phase_end(dve):
                return
            for s in range(2):
                for k in range(KC):
                    c_ = (P + 1) * k + P
                    dve.memset(m_v[s][:, c_:c_ + 1], 1.0).then_inc(sem("m1_ones"), 1)
            for t, s, n in node_tiles(dve):
                dve.wait_ge(*upto("m1_v_mm", t + 1))
                if due(t - 1):
                    dve.wait_ge(*upto("m1_ctx_mm", t - 1))
                dve.tensor_copy(m_v[s].rearrange("p (k n) -> p k n", k=KC)[:, :, 0:P],
                                bank[4 + s][:, 0:C].rearrange("p (k n) -> p k n", k=KC)).then_inc(sem("m1_v"), 1)
            dve.wait_ge(*upto("m1_ctx_mm", NT))
            for k in range(KC):
                chain(dve.reciprocal(cden[:, k:k + 1], bank[2 + k][:, P:P + 1]))
                chain(dve.tensor_scalar(bdc[:, k, :], bank[2 + k][:, 0:P], cden[:, k:k + 1], None, ALU.mult))
                dve.tensor_tensor(bdc[:, k, :], bdc[:, k, :], bd32[:, :], ALU.mult).then_inc(sem("m_bdc"), 1)
            dve.wait_ge(*upto("m_qc_mm", 2))
            for i in range(KC):
                dve.tensor_copy(w_qc[:, i, :], bank[6 + i][:, 0:C]).then_inc(sem("m_qc"), 1)
            for t, s, n in node_tiles(dve):
                r = rows_of(t)
                dve.wait_ge(*upto(f"m2_in{s}", 48 * (n + 1)))
                dve.wait_ge(*upto("w_mix_in", 80))
                if due(t - 1):
                    dve.wait_ge(*upto("m2_out", t - 1))
                dve.tensor_tensor(m_xb[s][0:r, :], m_x[s][0:r, :], bproj_b[0:r, :], ALU.add).then_inc(sem("m2_xb"), 1)
                dve.wait_ge(*upto("m2_sig", t + 1))
                if due(t - 1):
                    dve.wait_ge(*upto("m2_prt_mm", t - 1))
                dve.tensor_tensor(m_pr[s], m_sig[s], bank[s][:, 0:C], ALU.mult).then_inc(sem("m2_pr"), 1)
                dve.wait_ge(*upto("m2_f_mm", t + 1))
                dve.wait_ge(*upto("m2_xb", t + 1))
                if due(16 * n):
                    dve.wait_ge(*upto(f"m2_st{s}", 16 * n))
                dve.tensor_tensor(m_out[s], m_xb[s], bank[3][:, 0:C], ALU.add).then_inc(sem("m2_out"), 1)
            if phase_end(dve):
                return
            dve.wait_ge(*upto("w_ffn_in", 16 * 23))
            chain(dve.tensor_scalar(rtemp_r, temp_c, 0.1, 5.0, ALU.max, ALU.min))
            dve.reciprocal(rtemp_r, rtemp_r).then_inc(sem("rtemp"), 1)
            dve.wait_ge(*upto("rtemp", 1))
            dve.wait_ge(*upto("wl_mm", 4))
            chain(dve.tensor_copy(rtemp_b, bank[2][:, 0:8]))
            for k in range(KC):
                dve.tensor_tensor(heads(w_log[:, k, :]), heads(bank[k][:, :]), rtemp_b.unsqueeze(2).broadcast_to([P, 8, 64]), ALU.mult).then_inc(sem("w_log"), 1)
            chain(dve.tensor_tensor(b_log, bank[3][0:1, :], bslice8, ALU.add))
            dve.tensor_tensor(heads(b_log), heads(b_log), rtemp_r.unsqueeze(2).broadcast_to([1, 8, 64]), ALU.mult).then_inc(sem("w_log"), 1)
            for t, s, n in skewed(dve):
                if t[0] is not None:
                    t_, s_, n_ = t
                    dve.wait_ge(*upto(f"f1_in{s_}", 16 * (n_ + 1)))
                    if due(16 * n_):
                        dve.wait_ge(*upto(f"f1_x1_out{s_}", 16 * n_))
                    dve.scalar_tensor_tensor(a_x1[s_], at(acc, t_), 0.0, a_xin[s_], ALU.max, ALU.add).then_inc(sem("f1_x1"), 1)
                    norm("f1", a_x1[s_], a_xn[s_][:, 0:C], a_stats[s_], a_mv[s_], a_veps[s_], a_rstd[s_], t_,
                         ("f1_x1", t_ + 1), [("f1_t", t_ - 1), ("f1_u_mm", t_ - 1)])
                if s[0] is not None:
                    t_, s_, n_ = s
                    lg = bank[1 + s_]
                    dve.wait_ge(*upto("f1_l_mm", t_ + 1))
                    dve.tensor_reduce(a_max[s_], heads(lg[:, :]), AX, ALU.max).then_inc(sem("f1_mx"), 1)
                    dve.wait_ge(*upto("f1_mx", t_ + 1))
                    if due(t_ - 1):
                        dve.wait_ge(*upto("f1_ex", t_ - 1))
                    dve.tensor_tensor(heads(a_lg[s_]), heads(lg[:, :]), a_max[s_].unsqueeze(2).broadcast_to([P, 8, 64]), ALU.subtract).then_inc(sem("f1_lg"), 1)
                    dve.wait_ge(*upto("f1_ex", t_ + 1))
                    dve.tensor_reduce(a_sum[s_], heads(a_ex[s_]), AX, ALU.add).then_inc(sem("f1_sm"), 1)
                    dve.wait_ge(*upto("f1_sm", t_ + 1))
                    dve.reciprocal(a_rsum[s_], a_sum[s_]).then_inc(sem("f1_rs"), 1)
                    dve.wait_ge(*upto("f1_rs", t_ + 1))
                    if due(t_ - 1):
                        dve.wait_ge(*upto("f1_swt_mm", t_ - 1))
                    if due(t_ - 1):
                        dve.wait_ge(*upto("f1_u_mm", t_ - 1))
                    dve.tensor_tensor(heads(a_sw[s_]), heads(a_ex[s_]), a_rsum[s_].unsqueeze(2).broadcast_to([P, 8, 64]), ALU.mult).then_inc(sem("f1_sw"), 1)
            four = range(4)
            blk = lambda v, j: v[:, P * j:P * j + P]
            dve.wait_ge(*upto("f1_u_mm", NT))
            for j in four:
                dve.tensor_copy(f_u[:, j, :], bank[4 + j][:, 0:257]).then_inc(sem("fs_u"), 1)
            dve.wait_ge(*upto("fs_u", 4))
            chain(dve.tensor_scalar(f_den, f_u[:, :, 256], EPS, None, ALU.add))
            chain(dve.reciprocal(f_rden, f_den))
            dve.wait_ge(*upto("fs_ut_mm", 2))
            for k in range(KC):
                dve.tensor_copy(f_ut[:, k, :], bank[k][:, :]).then_inc(sem("fs_ut"), 1)
            dve.wait_ge(*upto("fs_tok_mm", 1))
            for j in four:
                chain(dve.scalar_tensor_tensor(blk(f_tok, j), blk(bfx_b, j), f_u[:, j, 256:257], blk(bank[2], j), ALU.mult, ALU.add))
                dve.scalar_tensor_tensor(blk(f_tok2, j), blk(f_tok, j), f_rden[:, j:j + 1], bd64[:, :], ALU.mult, ALU.mult).then_inc(sem("fs_tok"), 1)
            dve.wait_ge(*upto("fs_tokt_mm", 1))
            dve.tensor_copy(f_tokt, bank[0][:, :]).then_inc(sem("fs_tokt"), 1)
            dve.wait_ge(*upto("fs_qkv_mm", 3))
            for v, b_ in ((f_qt, 1), (f_kt, 2), (f_v, 4)):
                dve.tensor_copy(v, bank[b_][:, :]).then_inc(sem("fs_qkv"), 1)
            dve.wait_ge(*upto("fs_s_mm", 1))
            for j in four:
                chain(dve.scalar_tensor_tensor(blk(f_s, j), blk(bank[5], j), 64 ** -0.5, off64[:, :], ALU.mult, ALU.add))
                dve.tensor_reduce(f_max[:, j:j + 1], blk(f_s, j), AX, ALU.max, negate=True).then_inc(sem("fs_max"), 1)
            dve.wait_ge(*upto("fs_exp", 4))
            chain(dve.reciprocal(f_rsum, f_sum))
            for j in four:
                dve.tensor_scalar(blk(f_s, j), blk(f_s2, j), f_rsum[:, j:j + 1], None, ALU.mult).then_inc(sem("fs_a"), 1)
            dve.wait_ge(*upto("fs_at_mm", 1))
            dve.tensor_copy(f_at, bank[0][:, :]).then_inc(sem("fs_at"), 1)
            dve.wait_ge(*upto("fs_ost_mm", 1))
            dve.tensor_copy(f_ost, bank[1][:, :]).then_inc(sem("fs_ost"), 1)
            dve.wait_ge(*upto("fs_m_mm", 4))
            for j in four:
                dve.tensor_copy(f_m[:, j, :], bank[4 + j][:, 0:C]).then_inc(sem("fs_m"), 1)
            dve.wait_ge(*upto("fs_m", 4))
            if phase_end(dve):
                return
            dve.wait_ge(*upto("w_kv_in", 16))
            for k in range(KC):
                chain(dve.tensor_reduce(kv_mean[:, k, :], heads(w_kv1[:, k, :], 16), AX, ALU.add))
                chain(dve.tensor_scalar(kv_mean[:, k, :], kv_mean[:, k, :], 1.0 / 64, None, ALU.mult))
                dve.tensor_tensor(heads(w_kv1[:, k, :], 16), heads(w_kv1[:, k, :], 16),
                                  kv_mean[:, k, :].unsqueeze(2).broadcast_to([P, 16, 64]), ALU.subtract).then_inc(sem("w_kv"), 1)
            for t, s, n in skewed(dve):
                if t[0] is not None:
                    t_, s_, n_ = t
                    dve.wait_ge(*upto(f"f2_in{s_}", 32 * (n_ + 1)))
                    dve.wait_ge(*upto("f2_o_mm", t_ + 1))
                    if due(16 * n_):
                        dve.wait_ge(*upto(f"f2_x2_out{s_}", 16 * n_))
                    dve.tensor_tensor(k_x2[s_], k_x1[s_], bank[0][:, 0:C], ALU.add).then_inc(sem("f2_x2"), 1)
                    norm("f2", k_x2[s_], a_xn[s_][:, 0:C], a_stats[s_], a_mv[s_], a_veps[s_], a_rstd[s_], t_,
                         ("f2_x2", t_ + 1), [("f2_t", t_ - 1), (f"f2_xn_out{s_}", 16 * n_)])
                if s[0] is not None:
                    t_, s_, n_ = s
                    dve.wait_ge(*upto("f2_sq", 2 * t_ + 2))
                    dve.tensor_reduce(k_ss[s_], heads(k_sq[s_], 16), AX, ALU.add).then_inc(sem("f2_ss"), 1)
                    dve.wait_ge(*upto("f2_ss", t_ + 1))
                    dve.tensor_scalar(k_v1[s_], k_ss[s_], 1.0 / 64, EPS, ALU.mult, ALU.add).then_inc(sem("f2_v1"), 1)
                    dve.wait_ge(*upto("f2_v1", t_ + 1))
                    dve.tensor_tensor(k_pv[s_], k_v1[s_][:, 0:8], k_v1[s_][:, 8:16], ALU.mult).then_inc(sem("f2_pv"), 1)
                    dve.wait_ge(*upto("f2_krs", t_ + 1))
                    if due(t_ - 1):
                        dve.wait_ge(*upto("f2_dots_mm", t_ - 1))
                    dve.tensor_tensor(heads(k_kn[s_]), heads(bank[2][:, :]), k_rs[s_].unsqueeze(2).broadcast_to([P, 8, 64]), ALU.mult).then_inc(sem("f2_kn"), 1)
            dve.memset(acc[:, :, :], 0.0)
            if phase_end(dve):
                return
            def targets1(g, h):
                if due(g - 1):
                    dve.wait_ge(*upto("g1_sum_mm", g - 1))
                one_hots(oh[h % 2], P, dl_t, g).then_inc(sem("g1_oh"), 1)

            targets1(0, 0)
            for i in bodies(dve):
                ws = sum_windows(i)
                for h in range(BPB):
                    g = i * BPB + h
                    targets1(g + 1, h + 1)
                    if due(g):
                        add_sums("g1", g - 1, ws[GRP * h:GRP * h + GRP], (h + 1) % 2)
            add_sums("g1", NG - 1, windows(dve, T - GRP, GRP), 1)
            dve.wait_ge(*upto("w_l1_in", 16 * 7))
            dve.tensor_tensor(b_comb, b_self, b_out1, ALU.add).then_inc(sem("b_comb"), 1)
            for j in four:
                chain(dve.tensor_tensor(blk(d_bd, j), bank[4 + j][:, 0:P], bd64[:, :], ALU.mult))
            dve.tensor_scalar(d_bd, d_bd, 1.0 / N, None, ALU.mult).then_inc(sem("d_bd"), 1)
            dve.wait_ge(*upto("d_t1_mm", 4))
            for j in four:
                dve.tensor_copy(d_t1[:, j, :], bank[j][:, 0:C]).then_inc(sem("d_t1"), 1)
            dve.wait_ge(*upto("d_f_mm", 2))
            for k in range(KC):
                dve.tensor_tensor(w_comb[:, k, :], bank[4 + k][:, 0:C], w_self[:, k, :], ALU.add).then_inc(sem("w_comb"), 1)
            if phase_end(dve):
                return
            for t, s, n in skewed(dve):
                if t[0] is not None:
                    t_, s_, n_ = t
                    if due(t_ - 1):
                        dve.wait_ge(*upto("c_hn_t", t_ - 1))
                    dve.tensor_scalar(c_hn[s_], at(acc, t_), col(rdeg, t_), None, ALU.mult).then_inc(sem("c_hn"), 1)
                if s[0] is not None:
                    t_, s_, n_ = s
                    dve.wait_ge(*upto(f"c_in{s_}", 32 * (n_ + 1)))
                    dve.wait_ge(*upto("c_x_mm", t_ + 1))
                    dve.tensor_tensor(c_x3[s_], c_x2[s_], bank[1][:, 0:C], ALU.add).then_inc(sem("c_x3"), 1)
                    norm("c", c_x3[s_], c_xn[s_], c_stats[s_], c_mv[s_], c_veps[s_], c_rstd[s_], t_,
                         ("c_x3", t_ + 1), [("c_x4_t", t_ - 1)])
                    dve.wait_ge(*upto("c_xn", t_ + 1))
                    if due(16 * n_):
                        dve.wait_ge(*upto(f"c_x34_out{s_}", 16 * n_))
                    dve.tensor_tensor(c_x34[s_], c_x3[s_], c_xn[s_], ALU.add).then_inc(sem("c_x34"), 1)
                    dve.wait_ge(*upto("c_r_mm", t_ + 1))
                    dve.tensor_copy(at(logits, t_), bank[3][:, 0:8]).then_inc(sem("c_r"), 1)
            dve.wait_ge(*upto("c_r", NT))
            big = [P, NT, 8]
            m_, s_, i_ = rb[0], rb[1], rb[2]
            iota8 = iota[:, 0:8].unsqueeze(1).broadcast_to(big)
            each = lambda v: v.unsqueeze(2).broadcast_to(big)
            chain(dve.tensor_reduce(m_, logits, AX, ALU.max))
            dve.tensor_tensor(ra[0], logits, each(m_), ALU.subtract).then_inc(sem("r_exp_in"), 1)
            dve.wait_ge(*upto("r_exp", 1))
            chain(dve.tensor_reduce(s_, ra[1], AX, ALU.add))
            chain(dve.reciprocal(s_, s_))
            chain(dve.tensor_tensor(ra[0], ra[1], each(s_), ALU.mult))
            chain(dve.tensor_copy(ra[1], ra[0]))
            for pick in range(2):
                chain(dve.tensor_reduce(rb[3 + pick], ra[1], AX, ALU.max))
                chain(dve.tensor_tensor(ra[2], ra[1], each(rb[3 + pick]), ALU.is_ge))
                chain(dve.tensor_scalar(ra[3], iota8, -1.0, 8.0, ALU.mult, ALU.add))
                chain(dve.tensor_tensor(ra[2], ra[2], ra[3], ALU.mult))
                chain(dve.tensor_reduce(i_, ra[2], AX, ALU.max))
                chain(dve.tensor_tensor(ra[2], ra[3], each(i_), ALU.is_equal))
                if pick == 0:
                    chain(dve.tensor_copy(comb, ra[2]))
                    chain(dve.scalar_tensor_tensor(ra[1], ra[2], -2.0, ra[1], ALU.mult, ALU.add))
                else:
                    chain(dve.tensor_tensor(comb, comb, ra[2], ALU.add))
            chain(dve.tensor_tensor(rb[5], rb[3], rb[4], ALU.add))
            chain(dve.tensor_scalar(rb[5], rb[5], 1e-12, None, ALU.max))
            chain(dve.reciprocal(rb[5], rb[5]))
            chain(dve.tensor_tensor(comb, comb, ra[0], ALU.mult))
            chain(dve.tensor_tensor(comb, comb, each(rb[5]), ALU.mult))
            if phase_end(dve):
                return
            for g, s, n, m in expert_groups(dve):
                cf = comb.rearrange("p t e -> p (t e)")
                if due(g - 1):
                    dve.wait_ge(*upto("s_ct_mm", g - 1))
                dve.tensor_copy(s_cg[s][:, 0:8 * m], span(cf, 32 * g if isinstance(g, int) else g * 32, 8 * m)).then_inc(sem("s_cg"), 1)
                dve.wait_ge(*upto(f"s_in{s}", 32 * (n + 1)))
                dve.wait_ge(*upto("s_cb_mm", g + 1))
                for j in range(m):
                    dve.tensor_tensor(s_o[s][:, j, :], s_o[s][:, j, :], bank[4 + j // 2][:, C * (j % 2):C * (j % 2) + C], ALU.add).then_inc(sem("s_base"), 1)
                dve.wait_ge(*upto("s_base", 4 * g + m))
                for e in range(8):
                    dve.wait_ge(*upto("s_y_mm", 8 * g + e + 1))
                    for j in range(m):
                        if due(32 * g + m * e + j - m + 1 if e else 0):
                            dve.wait_ge(*upto("s_acc", 32 * g + m * e + j - m + 1 if e else 0))
                        c_ = s_cg[s][:, 8 * j + e:8 * j + e + 1]
                        dve.scalar_tensor_tensor(s_o[s][:, j, :], bank[4 + j // 2][:, C * (j % 2):C * (j % 2) + C], c_,
                                                 s_o[s][:, j, :], ALU.mult, ALU.add).then_inc(sem("s_acc"), 1)
            phase_end(dve)

        @block.tensor
        def _(pe):
            mm = pe.matmul

            def transposes(dst_, src_, n_=KC):
                for k in range(n_):
                    last = pe.transpose(dst_[:, P * k:P * k + P], src_[:, P * k:P * k + P], ident[:, :])
                return last

            pe.wait_ge(*upto("rows_ready", 1))
            for b_ in range(TB):
                cols = slice(P * b_, P * b_ + P)
                if due(3 * (b_ - 1)):
                    pe.wait_ge(*upto("tables", 3 * (b_ - 1)))
                mm(bank[b_ % 2][:, 0:P], r_dl[:, cols], ident[:, :], start=True, stop=True).then_inc(sem("tables_mm"), 1)
                mm(bank[b_ % 2][:, P:2 * P], r_idx[:, cols], ident[:, :], start=True, stop=True).then_inc(sem("tables_mm"), 1)
                mm(bank[b_ % 2][0:1, 2 * P:3 * P], r_w0[:, b_:b_ + 1], ident[:, :], start=True, stop=True).then_inc(sem("tables_mm"), 1)
            for v, b2_ in ((r_dst, 2), (r_idx, 3)):
                for b_ in range(TB):
                    last = mm(bank[b2_][:, 0:NT - 1], v[:, P * b_:P * b_ + P], r_sel[:, (NT - 1) * b_:(NT - 1) * (b_ + 1)],
                              start=b_ == 0, stop=b_ == TB - 1)
                last.then_inc(sem("extra_mm"), 1)
            if phase_end(pe):
                return
            pe.wait_ge(*upto("gate_w", 4))
            for k in range(KC):
                last = mm(bank[7][:, 0:64], ones[:, :], wg1[:, k, :], start=k == 0, stop=k == KC - 1)
            last.then_inc(sem("gate_w_mm"), 1)
            for k in range(KC):
                last = mm(bank[6][:, 0:64], lnb_b[:, k, :], wg1_raw[:, k, :], start=k == 0, stop=k == KC - 1)
            last.then_inc(sem("gate_w_mm"), 1)
            pe.wait_ge(*upto("gate_b", 1))
            for t, s, n in skewed(pe):
                if t[0] is not None:
                    t_, s_, n_ = t
                    pe.wait_ge(*upto("n0_xn", t_ + 1))
                    if due(t_):
                        pe.wait_ge(*upto("n0_xnt", t_))
                    transposes(bank[4], xn[s_]).then_inc(sem("n0_t"), 1)
                if s[0] is not None:
                    t_, s_, n_ = s
                    pe.wait_ge(*upto("n0_xnt", t_ + 1))
                    for b_ in range(4):
                        if b_ % 2:
                            if due(2 * t_ - 1 + b_ // 2):
                                pe.wait_ge(*upto("n0_y_dve", 2 * t_ - 1 + b_ // 2))
                        else:
                            if due(2 * t_ - 1 + b_ // 2):
                                pe.wait_ge(*upto("n0_y_act", 2 * t_ - 1 + b_ // 2))
                        for k in range(KC):
                            last = mm(bank[b_][:, :], xnt[s_][:, P * k:P * k + P], w_all[:, k, 512 * b_:512 * b_ + 512], start=k == 0, stop=k == KC - 1)
                        last.then_inc(sem(f"n0_y_mm{b_}"), 1)
                    if due(t_):
                        pe.wait_ge(*upto("n0_ga", t_))
                    for k in range(KC):
                        mm(bank[5][:, 0:C], xnt[s_][:, P * k:P * k + P], w_root[:, k, :], start=k == 0, stop=k == KC - 1)
                    for k in range(KC):
                        last = mm(bank[5][:, C:C + 64], xnt[s_][:, P * k:P * k + P], wg1[:, k, :], start=k == 0, stop=k == KC - 1)
                    last.then_inc(sem("n0_root_mm"), 1)
                    if due(t_):
                        pe.wait_ge(*upto("n0_km", t_))
                    for m in range(KC):
                        for k in range(KC):
                            last = mm(bank[6][:, P * m:P * m + P], w_k0[:, k, P * m:P * m + P], xnt[s_][:, P * k:P * k + P], start=k == 0, stop=k == KC - 1)
                    last.then_inc(sem("n0_km_mm"), 1)
                    pe.wait_ge(*upto("n0_hg", t_ + 1))
                    if due(t_):
                        pe.wait_ge(*upto("n0_hgt", t_))
                    alone(pe)
                    pe.transpose(bank[7][0:64, 0:P], hg[s_], ident[:, :]).then_inc(sem("n0_hg_t"), 1)
            pe.wait_ge(*upto("kmax", 1))
            pe.wait_ge(*upto("n0_y_act", 2 * NT))
            for k in range(KC):
                last = mm(bank[0][0:1, P * k:P * k + P], kmax1[:, k:k + 1], ident[:, :], start=True, stop=True)
            last.then_inc(sem("kmax_mm"), 1)
            if phase_end(pe):
                return
            pe.wait_ge(*upto("zerob", 1))
            mm(bank[7][:, :], zerob[:, 0:P], zerob, start=True, stop=False, skip_group_check=True)
            for i in bodies(pe):
                ws = windows(pe, i * BODY, BODY)
                for h in range(BPB):
                    g = i * BPB + h
                    pe.wait_ge(*upto("ct_oh", 2 * g + 2))
                    for j in range(GRP):
                        last = mm(bank[7][:, bass.ds(ws[GRP * h + j] * R, R)], ohb[h][:, j, :], tohb[h][:, j, :],
                                  start=False, stop=False, skip_group_check=True)
                    last.then_inc(sem("ct_mm"), 1)
            if phase_end(pe):
                return

            def sum_rows(pre, g, again, lhs, h):
                pe.wait_ge(*upto(f"{pre}_rows{h}", 16 * GRP * (again + 1)))
                if due(GRP * (g - 1)):
                    pe.wait_ge(*upto(pre + "_add", GRP * (g - 1)))
                for j in range(GRP):
                    last = mm(bank[2 * (h % 2) + j // 2][:, C * (j % 2):C * (j % 2) + C], lhs[:, j, :],
                              ring[GRP * h + j], start=True, stop=True)
                last.then_inc(sem(pre + "_sum_mm"), 1)

            def turn(g, h):
                pe.wait_ge(*upto("g0_oh", g + 1))
                if due(g):
                    pe.wait_ge(*upto("g0_oht", g))
                for j in range(GRP):
                    last = mm(bank[6][:, P * j:P * j + P], ohb[h][:, j, :], identb[:, :], start=True, stop=True)
                last.then_inc(sem("g0_oht_mm"), 1)

            def look(g, h, ws):
                pe.wait_ge(*upto("g0_oht", g + 1))
                if due(g):
                    pe.wait_ge(*upto("g0_wsel", g))
                for j in range(GRP):
                    last = mm(bank[7][:, 3 * R * j:3 * R * (j + 1)], oht[h % 2][:, P * j:P * j + P], at(rc3, ws[j]), start=True, stop=True)
                last.then_inc(sem("g0_look_mm"), 1)

            ws = windows(pe, 0, 2 * GRP)
            for g in range(2):
                turn(g, g)
                look(g, g, ws[GRP * g:GRP * g + GRP])
            for i in bodies(pe):
                ws = windows(pe, i * BODY + 2 * GRP, BODY)
                for h in range(BPB):
                    g = i * BPB + h
                    turn(g + 2, (h + 2) % BPB)
                    pe.wait_ge(*upto("g0_woh", g + 1))
                    sum_rows("g0", g, i, woh[h % 2], h)
                    look(g + 2, h, ws[GRP * h:GRP * h + GRP])
            if phase_end(pe):
                return
            for t, s, n in node_tiles(pe):
                pe.wait_ge(*upto(f"m1_in{s}", 16 * (n + 1)))
                if due(t - 1):
                    pe.wait_ge(*upto("m1_ek", t - 1))
                if due(t - 1):
                    pe.wait_ge(*upto("m1_v", t - 1))
                mm(bank[s][:, 0:C], ones[0:1, :], negmax, start=True, stop=False)
                for k in range(KC):
                    last = mm(bank[s][:, 0:C], m_xnt[s][:, P * k:P * k + P], w_k0[:, k, :], start=False, stop=k == KC - 1)
                last.then_inc(sem("m1_k_mm"), 1)
                for k in range(KC):
                    last = mm(bank[4 + s][:, 0:C], m_xnt[s][:, P * k:P * k + P], w_v0[:, k, :], start=k == 0, stop=k == KC - 1)
                last.then_inc(sem("m1_v_mm"), 1)
                r = rows_of(t)
                pe.wait_ge(*upto("m1_ek", t + 1))
                pe.wait_ge(*upto("m1_v", t + 1))
                pe.wait_ge(*upto("m1_ones", 4))
                for k in range(KC):
                    last = mm(bank[2 + k][:, 0:P + 1], m_ek[s][0:r, P * k:P * k + P], m_v[s][0:r, (P + 1) * k:(P + 1) * (k + 1)],
                              start=isinstance(t, int) and t == 0, stop=is_last(t), skip_group_check=True)
                last.then_inc(sem("m1_ctx_mm"), 1)
            pe.wait_ge(*upto("w_mix_in", 80))
            for i in range(KC):
                for j in range(KC):
                    pe.wait_ge(*upto("m_bdc", j + 1))
                    last = mm(bank[6 + i][:, P * j:P * j + P], w_qt[:, j, P * i:P * i + P], bdc[:, j, :], start=True, stop=True)
                last.then_inc(sem("m_qc_mm"), 1)
            pe.wait_ge(*upto("m_qc", 2))
            pe.wait_ge(*upto("m1_v", NT))
            for t, s, n in node_tiles(pe):
                pe.wait_ge(*upto(f"m2_in{s}", 48 * (n + 1)))
                if due(t - 1):
                    pe.wait_ge(*upto("m2_pr", t - 1))
                for k in range(KC):
                    mm(bank[s][:, 0:C], m_xnt[s][:, P * k:P * k + P], w_qc[:, k, :], start=k == 0, stop=k == KC - 1)
                mm(bank[4 + s][:, 0:C], ones[0:1, :], bg2, start=True, stop=False)
                mm(bank[4 + s][:, 0:C], m_hgt[s], wg2, start=False, stop=True).then_inc(sem("m2_g_mm"), 1)
                pe.wait_ge(*upto("m2_pr", t + 1))
                if due(t):
                    pe.wait_ge(*upto("m2_prt", t))
                transposes(bank[2], m_pr[s]).then_inc(sem("m2_prt_mm"), 1)
                pe.wait_ge(*upto("m2_prt", t + 1))
                if due(t):
                    pe.wait_ge(*upto("m2_out", t))
                for k in range(KC):
                    last = mm(bank[3][:, 0:C], m_prt[s][:, P * k:P * k + P], w_proj[:, k, :], start=k == 0, stop=k == KC - 1)
                last.then_inc(sem("m2_f_mm"), 1)
            if phase_end(pe):
                return
            pe.wait_ge(*upto("w_ffn_in", 16 * 23))
            pe.wait_ge(*upto("rtemp", 1))
            for i in range(KC):
                for j in range(4):
                    last = mm(bank[i][:, P * j:P * j + P], wx_t[:, j, P * i:P * i + P], wsl_bd, start=True, stop=True)
                last.then_inc(sem("wl_mm"), 1)
            mm(bank[2][:, 0:8], ones[0:1, :], rtemp_r, start=True, stop=True).then_inc(sem("wl_mm"), 1)
            for j in range(4):
                last = mm(bank[3][0:1, P * j:P * j + P], bx_c[:, j:j + 1], wsl_bd, start=True, stop=True)
            last.then_inc(sem("wl_mm"), 1)
            pe.wait_ge(*upto("w_log", 3))
            pe.wait_ge(*upto("a_ones", 2))
            for t, s, n in skewed(pe):
                if t[0] is not None:
                    t_, s_, n_ = t
                    pe.wait_ge(*upto("f1_xn", t_ + 1))
                    if due(t_):
                        pe.wait_ge(*upto("f1_xnt", t_))
                    transposes(bank[0], a_xn[s_]).then_inc(sem("f1_t"), 1)
                if s[0] is not None:
                    t_, s_, n_ = s
                    r = rows_of(t_)
                    pe.wait_ge(*upto("f1_xnt", t_ + 1))
                    if due(t_ - 1):
                        pe.wait_ge(*upto("f1_lg", t_ - 1))
                    mm(bank[1 + s_][:, :], ones[0:1, :], b_log, start=True, stop=False)
                    for k in range(KC):
                        last = mm(bank[1 + s_][:, :], a_xnt[s_][:, P * k:P * k + P], w_log[:, k, :], start=False, stop=k == KC - 1)
                    last.then_inc(sem("f1_l_mm"), 1)
                    pe.wait_ge(*upto("f1_sw", t_ + 1))
                    if due(t_):
                        pe.wait_ge(*upto("f1_swt", t_))
                    for j in range(4):
                        last = pe.transpose(bank[3][:, P * j:P * j + P], a_sw[s_][:, P * j:P * j + P], ident[:, :])
                    last.then_inc(sem("f1_swt_mm"), 1)
                    for j in range(4):
                        last = mm(bank[4 + j][:, 0:257], a_sw[s_][0:r, P * j:P * j + P], a_xn[s_][0:r, :],
                                  start=isinstance(t_, int) and t_ == 0, stop=is_last(t_), skip_group_check=True)
                    last.then_inc(sem("f1_u_mm"), 1)
            blk = lambda v, j: v[:, P * j:P * j + P]
            pe.wait_ge(*upto("fs_u", 4))
            for k in range(KC):
                for j in range(4):
                    last = pe.transpose(bank[k][:, P * j:P * j + P], f_u[:, j, P * k:P * k + P], ident[:, :])
                last.then_inc(sem("fs_ut_mm"), 1)
            pe.wait_ge(*upto("fs_ut", 2))
            for j in range(4):
                for k in range(KC):
                    last = mm(blk(bank[2], j), f_ut[:, k, P * j:P * j + P], w_fx[:, k, P * j:P * j + P], start=k == 0, stop=k == KC - 1)
            last.then_inc(sem("fs_tok_mm"), 1)
            pe.wait_ge(*upto("fs_tok", 4))
            for j in range(4):
                last = pe.transpose(blk(bank[0], j), blk(f_tok2, j), ident[:, :])
            last.then_inc(sem("fs_tokt_mm"), 1)
            pe.wait_ge(*upto("fs_tokt", 1))
            for w_, b_ in ((wq_bd, 1), (wk_bd, 2)):
                last = mm(bank[b_][:, :], w_, f_tokt, start=True, stop=True)
                last.then_inc(sem("fs_qkv_mm"), 1)
            for j in range(4):
                last = mm(blk(bank[4], j), blk(f_tokt, j), wv_bd, start=True, stop=True)
            last.then_inc(sem("fs_qkv_mm"), 1)
            pe.wait_ge(*upto("fs_qkv", 3))
            for j in range(4):
                last = mm(blk(bank[5], j), blk(f_qt, j), blk(f_kt, j), start=True, stop=True)
            last.then_inc(sem("fs_s_mm"), 1)
            pe.wait_ge(*upto("fs_a", 4))
            for j in range(4):
                last = pe.transpose(blk(bank[0], j), blk(f_s, j), ident[:, :])
            last.then_inc(sem("fs_at_mm"), 1)
            pe.wait_ge(*upto("fs_at", 1))
            for j in range(4):
                last = mm(blk(bank[1], j), blk(f_v, j), blk(f_at, j), start=True, stop=True)
            last.then_inc(sem("fs_ost_mm"), 1)
            pe.wait_ge(*upto("fs_ost", 1))
            for j in range(4):
                mm(bank[4 + j][:, 0:C], blk(f_ost, j), w_out[:, j, :], start=True, stop=True).then_inc(sem("fs_m_mm"), 1)
            if phase_end(pe):
                return
            pe.wait_ge(*upto("w_kv", 2))
            for t, s, n in skewed(pe):
                if t[0] is not None:
                    t_, s_, n_ = t
                    pe.wait_ge(*upto(f"f2_in{s_}", 32 * (n_ + 1)))
                    if due(t_):
                        pe.wait_ge(*upto("f2_x2", t_))
                    mm(bank[0][:, 0:C], ones[0:1, :], bout_r, start=True, stop=False)
                    for j in range(4):
                        last = mm(bank[0][:, 0:C], k_swt[s_][:, P * j:P * j + P], f_m[:, j, :], start=False, stop=j == 3)
                    last.then_inc(sem("f2_o_mm"), 1)
                if s[0] is not None:
                    t_, s_, n_ = s
                    r = rows_of(t_)
                    pe.wait_ge(*upto("f2_xn", t_ + 1))
                    if due(t_):
                        pe.wait_ge(*upto("f2_xnt", t_))
                    transposes(bank[1], a_xn[s_]).then_inc(sem("f2_t"), 1)
                    pe.wait_ge(*upto("f2_xnt", t_ + 1))
                    if due(t_):
                        pe.wait_ge(*upto("f2_kn", t_))
                    if due(t_):
                        pe.wait_ge(*upto("f2_v", t_))
                    for b_ in range(2):
                        for k in range(KC):
                            last = mm(bank[2 + b_][:, :], a_xnt[s_][:, P * k:P * k + P], w_kv1[:, k, 512 * b_:512 * b_ + 512], start=k == 0, stop=k == KC - 1)
                    last.then_inc(sem("f2_kv_mm"), 1)
                    pe.wait_ge(*upto("f2_kn", t_ + 1))
                    pe.wait_ge(*upto("f2_v", t_ + 1))
                    for j in range(4):
                        last = mm(bank[4 + j][:, 0:P], k_v[s_][0:r, P * j:P * j + P], k_kn[s_][0:r, P * j:P * j + P],
                                  start=isinstance(t_, int) and t_ == 0, stop=is_last(t_), skip_group_check=True)
                    last.then_inc(sem("f2_dots_mm"), 1)
            if phase_end(pe):
                return
            for i in bodies(pe):
                for h in range(BPB):
                    g = i * BPB + h
                    pe.wait_ge(*upto("g1_oh", g + 1))
                    sum_rows("g1", g, i, oh[h % 2], h)
            pe.wait_ge(*upto("g1_add", T))
            pe.wait_ge(*upto("d_bd", 1))
            for j in range(4):
                mm(bank[j][:, 0:C], blk(d_bd, j), w_o1t[:, j, :], start=True, stop=True).then_inc(sem("d_t1_mm"), 1)
            pe.wait_ge(*upto("d_t1", 4))
            for k in range(KC):
                for j in range(4):
                    last = mm(bank[4 + k][:, 0:C], w_q1[:, j, P * k:P * k + P], d_t1[:, j, :], start=j == 0, stop=j == 3)
                last.then_inc(sem("d_f_mm"), 1)
            if phase_end(pe):
                return
            for t, s, n in skewed(pe):
                if t[0] is not None:
                    t_, s_, n_ = t
                    pe.wait_ge(*upto("c_hn", t_ + 1))
                    if due(t_):
                        pe.wait_ge(*upto("c_hnt", t_))
                    transposes(bank[0], c_hn[s_]).then_inc(sem("c_hn_t"), 1)
                if s[0] is not None:
                    t_, s_, n_ = s
                    pe.wait_ge(*upto("c_hnt", t_ + 1))
                    pe.wait_ge(*upto(f"c_in{s_}", 32 * (n_ + 1)))
                    if due(t_):
                        pe.wait_ge(*upto("c_x3", t_))
                    mm(bank[1][:, 0:C], ones[0:1, :], b_comb, start=True, stop=False)
                    for k in range(KC):
                        mm(bank[1][:, 0:C], c_hnt[s_][:, P * k:P * k + P], w_neigh[:, k, :], start=False, stop=False)
                    for k in range(KC):
                        last = mm(bank[1][:, 0:C], c_xnt[s_][:, P * k:P * k + P], w_comb[:, k, :], start=False, stop=k == KC - 1)
                    last.then_inc(sem("c_x_mm"), 1)
                    pe.wait_ge(*upto("c_xn", t_ + 1))
                    if due(t_):
                        pe.wait_ge(*upto("c_x4t", t_))
                    transposes(bank[2], c_xn[s_]).then_inc(sem("c_x4_t"), 1)
                    pe.wait_ge(*upto("c_x4t", t_ + 1))
                    if due(t_):
                        pe.wait_ge(*upto("c_r", t_))
                    for k in range(KC):
                        last = mm(bank[3][:, 0:8], c_x4t[s_][:, P * k:P * k + P], w_rt[:, k, :], start=k == 0, stop=k == KC - 1)
                    last.then_inc(sem("c_r_mm"), 1)
            if phase_end(pe):
                return
            pe.wait_ge(*upto("w_moe_in", 64))
            for g, s, n, m in expert_groups(pe):
                pe.wait_ge(*upto(f"s_in{s}", 32 * (n + 1)))
                if due(g):
                    pe.wait_ge(*upto("s_ct", g))
                pe.wait_ge(*upto("s_cg", g + 1))
                for j in range(m):
                    last = pe.transpose(bank[6][0:8, P * j:P * j + P], s_cg[s][:, 8 * j:8 * j + 8], ident[:, :])
                last.then_inc(sem("s_ct_mm"), 1)
                pe.wait_ge(*upto("s_ct", g + 1))
                if due(32 * g):
                    pe.wait_ge(*upto("s_acc", 32 * g))
                for j in range(m):
                    last = mm(bank[4 + j // 2][:, C * (j % 2):C * (j % 2) + C], s_ct[s][:, P * j:P * j + P], b2_sb, start=True, stop=True)
                last.then_inc(sem("s_cb_mm"), 1)

                def hidden(e):
                    for f in range(KC):
                        if due(16 * g + 2 * e + f - 3):
                            pe.wait_ge(*upto("s_h", 16 * g + 2 * e + f - 3))
                        for k in range(KC):
                            last = mm(bank[2 * (e % 2) + f][:, 0:m * P], w1_sb[:, e, k, P * f:P * f + P], s_xt[s][:, 0:m, k, :], start=k == 0, stop=k == KC - 1)
                        last.then_inc(sem("s_h_mm"), 1)

                hidden(0)
                for e in range(8):
                    if e < 7:
                        hidden(e + 1)
                    pe.wait_ge(*upto("s_h", 16 * g + 2 * e + 2))
                    pe.wait_ge(*upto("s_base", 4 * g + m))
                    if due(32 * g + m * e):
                        pe.wait_ge(*upto("s_acc", 32 * g + m * e))
                    for j in range(m):
                        for f in range(KC):
                            last = mm(bank[4 + j // 2][:, C * (j % 2):C * (j % 2) + C], s_h[e % 2][f][:, P * j:P * j + P], w2_sb[:, e, f, :], start=f == 0, stop=f == KC - 1)
                    last.then_inc(sem("s_y_mm"), 1)
            phase_end(pe)



def kernel(x, src, dst, edge_type_8, L0_gnn_W, L0_gnn_W_root, L0_gnn_bias, L0_mix_Wqkv, L0_mix_Wproj, L0_mix_bproj,
           L0_mix_ln_g, L0_mix_ln_b, L0_mix_Wg1, L0_mix_bg1, L0_mix_Wg2, L0_mix_bg2, L0_ffn_W_fx, L0_ffn_b_fx,
           L0_ffn_W_x, L0_ffn_b_x, L0_ffn_W_slice, L0_ffn_b_slice, L0_ffn_W_q, L0_ffn_W_k, L0_ffn_W_v, L0_ffn_W_out,
           L0_ffn_b_out, L0_ffn_temperature, L1_gnn_w_neigh, L1_gnn_w_self, L1_gnn_b_self, L1_mix_Wqkv, L1_mix_Wout,
           L1_mix_bout, L1_ffn_router_w, L1_ffn_w1, L1_ffn_b1, L1_ffn_w2, L1_ffn_b2):
    import numpy as np
    import concourse.bacc as bacc
    from concourse.bass_utils import run_bass_kernel_spmd

    a = np.asarray
    arrays = {
        "x": a(x), "src": a(src), "dst": a(dst), "etype": a(edge_type_8),
        "gnn0_w": a(L0_gnn_W).transpose(1, 0, 2).reshape(C, R * C), "gnn0_root": a(L0_gnn_W_root),
        "gnn0_bias": a(L0_gnn_bias), "mix_wqkv": a(L0_mix_Wqkv), "mix_wq_t": a(L0_mix_Wqkv)[:, 0:C].T,
        "mix_wproj": a(L0_mix_Wproj), "mix_bproj": a(L0_mix_bproj), "mix_ln_g": a(L0_mix_ln_g).reshape(KC, P).T,
        "mix_ln_b": a(L0_mix_ln_b).reshape(KC, P).T, "mix_wg1": a(L0_mix_Wg1), "mix_bg1": a(L0_mix_bg1), "mix_wg2": a(L0_mix_Wg2),
        "mix_bg2": a(L0_mix_bg2), "ffn_wfx": a(L0_ffn_W_fx), "ffn_bfx": a(L0_ffn_b_fx), "ffn_wx_t": a(L0_ffn_W_x).T,
        "ffn_bx": a(L0_ffn_b_x).reshape(4, P).T, "ffn_wslice": a(L0_ffn_W_slice), "ffn_bslice": a(L0_ffn_b_slice),
        "ffn_wq": a(L0_ffn_W_q), "ffn_wk": a(L0_ffn_W_k), "ffn_wv": a(L0_ffn_W_v), "ffn_wout": a(L0_ffn_W_out),
        "ffn_bout": a(L0_ffn_b_out), "ffn_temp": a(L0_ffn_temperature).reshape(1, 8),
        "gnn1_wneigh_t": a(L1_gnn_w_neigh).T, "gnn1_wself_t": a(L1_gnn_w_self).T, "gnn1_bself": a(L1_gnn_b_self),
        "mix1_wqkv": a(L1_mix_Wqkv), "mix1_wkv_t": a(L1_mix_Wqkv)[512:1536, :].T, "mix1_wout_t": a(L1_mix_Wout).T,
        "mix1_bout": a(L1_mix_bout), "router_t": a(L1_ffn_router_w).T, "w1": a(L1_ffn_w1), "b1": a(L1_ffn_b1).reshape(8 * KC, P).T,
        "w2": a(L1_ffn_w2), "b2": a(L1_ffn_b2),
    }
    nc = bacc.Bacc("TRN2", target_bir_lowering=False, num_devices=1)
    given, args = {}, {}
    for name, v in arrays.items():
        given[f"in_{name}"] = v = np.ascontiguousarray(v)
        args[name] = nc.dram_tensor(f"in_{name}", v.shape, mybir.dt.from_np(v.dtype), kind="ExternalInput").ap()
    args["out"] = nc.dram_tensor("out_x", (N, C), FP32, kind="ExternalOutput").ap()
    build(nc, **args)
    r = run_bass_kernel_spmd(nc, [given], core_ids=[0])
    return r.results[0]["out_x"]
```

```python
import concourse.bass as bass
from concourse import mybir
from contextlib import ExitStack

FP32 = mybir.dt.float32
BF16 = mybir.dt.bfloat16
I32 = mybir.dt.int32
ALU = mybir.AluOpType
ACT = mybir.ActivationFunctionType
AX = mybir.AxisListType.X

P = 128
N = 6250
C = 256
KC = C // P
NT = -(-N // P)
NP = NT * P
LAST = N - (NT - 1) * P
E = 200000
R = 8
ET = -(-E // P)
GRP = 4
BODY = 16
T = -(-(ET + NT - 1) // BODY) * BODY
NG = T // GRP
BPB = BODY // GRP
TW = T + BODY
TB = -(-ET // P)
EROWS, ECOLS = 80, E // 80
PAD = TB * P * P + P - E
PROWS = 80
SCAT = 20
PAD_DST = 8191
EPS = 1e-5


def build(nc, x, src, dst, etype, gnn0_w, gnn0_root, gnn0_bias, mix_wqkv, mix_wq_t, mix_wproj, mix_bproj,
          mix_ln_g, mix_ln_b, mix_wg1, mix_bg1, mix_wg2, mix_bg2, ffn_wfx, ffn_bfx, ffn_wx_t, ffn_bx,
          ffn_wslice, ffn_bslice, ffn_wq, ffn_wk, ffn_wv, ffn_wout, ffn_bout, ffn_temp,
          gnn1_wneigh_t, gnn1_wself_t, gnn1_bself, mix1_wqkv, mix1_wkv_t, mix1_wout_t, mix1_bout,
          router_t, w1, b1, w2, b2, out, stop_after=99):
    ctx = ExitStack()
    with ctx:
        sems = {}

        share = {}
        ended = {}

        def take_turns(lane, step, count):
            share[step] = (lane, ended.get(lane, 0))
            ended[lane] = ended.get(lane, 0) + count

        for steps in (
                "n0_t n0_xnt n0_xn n0_var n0_rstd n0_gvar n0_grstd n0_gst n0_gag n0_st n0_ag n0_km n0_km_mm n0_root "
                "n0_root_mm n0_ga n0_gate n0_hg n0_hg_t n0_hgt n0_y_mm0 n0_y_mm1 n0_y_mm2 n0_y_mm3",
                "m1_k_mm m1_v_mm m1_ek m1_v m1_ctx_mm m2_xb m2_g_mm m2_sig m2_pr m2_prt_mm m2_prt m2_f_mm m2_out",
                "f1_x1 f1_st f1_ag f1_var f1_rstd f1_xn f1_t f1_xnt f1_l_mm f1_mx f1_lg f1_ex f1_sm f1_rs f1_sw "
                "f1_swt_mm f1_swt f1_u_mm",
                "f2_o_mm f2_x2 f2_st f2_ag f2_var f2_rstd f2_xn f2_t f2_xnt",
                "kv_k_mm kv_v_mm kv_sqk kv_sqv kv_v kv_ss kv_v1 kv_pv kv_root kv_inv kv_n1 kv_n2 kv_n3 kv_krs kv_kn "
                "kv_dots_mm",
                "c_hn c_hn_t c_hnt c_x_mm c_x3 c_st c_ag c_var c_rstd c_xn c_x4_t c_x4t c_x34 c_r c_r_mm"):
            for n_, step_ in enumerate(steps.split()):
                take_turns(f"tile_step_{n_}", step_, NT)
        for lane, steps in (
                ("load", [("n0_in", 1), ("f1_in", 1), ("f2_in", 2), ("c_in", 2)]),
                ("store_a", [("n0_xnt_out", 1), ("f1_x1_out", 1), ("c_x34_out", 1)]),
                ("store_b", [("n0_y_out", 1), ("f1_swt_out", 1), ("c_x4t_out", 1)]),
                ("store_c", [("n0_hgt_out", 1)]), ("store_d", [("f2_x2_out", 1)]), ("store_e", [("f2_xn_out", 1)]),
                ("store_f", [("f2_xnt_out", 1)])):
            for step_, dmas in steps:
                for s in range(2):
                    take_turns(f"{lane}_{s}", f"{step_}{s}", 16 * dmas * (NT // 2 + 1 - s))

        for lane, steps in (
                ("sum_mm", [("g0_sum_mm", 2 * NG), ("g1_sum_mm", 2 * NG)]),
                ("add", [("g0_add", T), ("g1_add", T)]),
                ("oh", [("g0_oh", NG + 3), ("g1_oh", NG + 1)]),
                ("idx", [("g0_idx", NG + BPB), ("g1_idx", NG + BPB)]),
                ("once_0", [("fs_u", 4), ("d_bd", 1)]),
                ("once_1", [("fs_ut_mm", KC), ("d_t1_mm", 4)]),
                ("once_2", [("fs_ut", KC), ("d_t1", 4)]),
                ("once_3", [("fs_tok_mm", 1), ("d_f_mm", KC)]),
                ("once_4", [("fs_tok", 4), ("w_comb", KC)]),
                ("once_5", [("fs_tokt_mm", 1), ("b_comb", 1)])):
            for step_, count_ in steps:
                take_turns(lane, step_, count_)
        for step_ in ("g0", "g1"):
            for h in range(BPB):
                take_turns(f"rows{h}", f"{step_}_rows{h}", 16 * GRP * (T // BODY))

        def sem(name):
            name = share.get(name, (name, 0))[0]
            if name not in sems:
                sems[name] = ctx.enter_context(nc.semaphore(name))
            return sems[name]

        def dram(name, shape, dt=FP32):
            return nc.dram_tensor(name, shape, dt, kind="Internal").ap()

        def sb(name, shape, dt=FP32):
            return ctx.enter_context(nc.sbuf_tensor(name, shape, dt))

        words = dram("edge_words", (E + PAD, 1), I32)
        y_table = dram("y_table", (NP * R, C))
        y_rows = y_table.rearrange("(n r) c -> n (r c)", r=R)
        xnt_d = dram("xn_t", (NT, P, C))
        hgt_d = dram("hgate_t", (NT, 64, P))
        xm_d = dram("x_mixed", (NP, C))
        x1_d = dram("x_1", (NP, C))
        swt_d = dram("slice_weights_t", (NT, P, 512))
        x2_d = dram("x_2", (NP, C))
        xn3_d = dram("xn_3", (NP, C))
        xnt3_d = dram("xn_3_t", (NT, P, C))
        x34_d = dram("x_3_plus_xn_4", (NP, C))
        xnt4_d = dram("xn_4_t", (NT, P, C))

        acc = sb("acc", [P, NT, C])
        idx_t = sb("idx_t", [P, TW], I32)
        dl_t = sb("dl_t", [P, TW])
        typ_t = sb("typ_t", [P, TW])
        win = sb("win", [1, TW], I32)
        cnt = sb("cnt", [P, NT, R])
        rdeg = sb("rdeg", [P, NT])
        rc3 = sb("rc3", [P, NT, 3 * R], BF16)
        ident = sb("ident", [P, P])
        identb = sb("identb", [P, P], BF16)
        iota = sb("iota", [P, P])
        ones = sb("ones", [P, P])
        bd32 = sb("bd32", [P, P])
        bd64 = sb("bd64", [P, P])
        off64 = sb("off64", [P, P])
        mhalf = sb("mhalf", [P, 16])
        arena = sb("arena", [P, 30000])
        bank = [ctx.enter_context(nc.psum_tensor(f"bank{i}", [P, 512], FP32)) for i in range(8)]

        class Arena:
            def __init__(self, at=0):
                self.at = at

            def take(self, cols, dt=FP32, parts=P):
                words_ = cols if dt != BF16 else -(-cols // 2)
                a = arena[0:parts, self.at:self.at + words_]
                self.at += words_
                assert self.at <= 30000, self.at
                return a if dt == FP32 else a.bitcast(dt)

        ar = Arena()
        e_src = ar.take(ECOLS, I32, EROWS)
        e_dst = ar.take(ECOLS, I32, EROWS)
        e_typ = ar.take(ECOLS, I32, EROWS)
        e_pad = ar.take(PAD // PROWS, I32, PROWS)
        r_word = ar.take(TB * P, I32)
        r_int = ar.take(TB * P, I32)
        r_dst = ar.take(TB * P)
        r_idx = ar.take(TB * P)
        r_dl = ar.take(TB * P)
        r_next = ar.take(TB, I32)
        r_w0i = ar.take(TB, I32)
        r_w0 = ar.take(TB)
        r_w1i = ar.take(TB, I32)
        r_w1 = ar.take(TB)
        r_sel = ar.take(TB * (NT - 1))
        r_sel2 = ar.take(TB * (NT - 1))
        x_base = ar.take(NT - 1)
        e_win = e_typ.bitcast(FP32)
        q_mask = ar.take(ECOLS, FP32, EROWS)
        q_pre = ar.take(ECOLS, FP32, EROWS)
        q_pos = ar.take(ECOLS, FP32, EROWS)
        q_posi = e_src
        q_offs = ar.take(1, FP32, EROWS)
        q_base = ar.take(1, FP32, EROWS)
        q_viol = ar.take(1, FP32, EROWS)
        q_row = ar.take(3 * EROWS, FP32, 1)
        q_one = ar.take(2, FP32, 1)
        q_flag = ar.take(1, I32, 1)
        q_tri = ar.take(EROWS, FP32, EROWS)
        q_islot = ar.take(SCAT, I32, EROWS)
        q_wslot = ar.take(SCAT, I32, EROWS)
        iota_i = ar.take(P, I32)
        col_i = ar.take(1, I32)
        blk_i = ar.take(2, I32)
        blk_f = ar.take(2)
        row_b = ar.take(P)
        row_bi = ar.take(P, I32)

        ar = Arena()
        w_all = ar.take(KC * R * C).rearrange("p (k n) -> p k n", k=KC)
        w_root = ar.take(KC * C).rearrange("p (k n) -> p k n", k=KC)
        w_k0 = ar.take(KC * C).rearrange("p (k n) -> p k n", k=KC)
        w_v0 = ar.take(KC * C).rearrange("p (k n) -> p k n", k=KC)
        wg1_raw = ar.take(KC * 64).rearrange("p (k n) -> p k n", k=KC)
        wg1 = ar.take(KC * 64).rearrange("p (k n) -> p k n", k=KC)
        lng = ar.take(KC)
        lnb = ar.take(KC)
        lnb_b = ar.take(KC * P).rearrange("p (k n) -> p k n", k=KC)
        bg1_b = ar.take(64)
        wg1_sum = ar.take(64)
        gate_b = ar.take(64)
        bias0_b = ar.take(C)
        kmax = ar.take(NT * KC).rearrange("p (t k) -> p t k", k=KC)
        kmax1 = ar.take(KC)
        negmax = ar.take(C, FP32, 1)
        after_weights0 = ar.at
        xin = [ar.take(C) for _ in range(2)]
        xn = [ar.take(C + 1) for _ in range(2)]
        stats = [ar.take(6) for _ in range(2)]
        mv = [ar.take(2) for _ in range(2)]
        veps = [ar.take(16) for _ in range(2)]
        rstd = [ar.take(16) for _ in range(2)]
        gstats = [ar.take(6) for _ in range(2)]
        gmv = [ar.take(2) for _ in range(2)]
        gveps = [ar.take(1) for _ in range(2)]
        grstd = [ar.take(1) for _ in range(2)]
        xnt = [ar.take(C) for _ in range(2)]
        ysb = [ar.take(R * C) for _ in range(2)]
        g_a = [ar.take(64) for _ in range(2)]
        g_b = [ar.take(64) for _ in range(2)]
        hg = [ar.take(64) for _ in range(2)]
        hgt = [ar.take(P, FP32, 64) for _ in range(2)]
        after_norm0 = ar.at

        ar = Arena(after_norm0)
        ring = [ar.take(C) for _ in range(BODY)]
        idx_s = ar.take(BODY, I32)
        oh = [ar.take(GRP * P).rearrange("p (j n) -> p j n", j=GRP) for _ in range(2)]
        woh = [ar.take(GRP * P).rearrange("p (j n) -> p j n", j=GRP) for _ in range(2)]
        ohb = [ar.take(GRP * P, BF16).rearrange("p (j n) -> p j n", j=GRP) for _ in range(BPB)]
        tohb = [ar.take(GRP * R, BF16).rearrange("p (j n) -> p j n", j=GRP) for _ in range(BPB)]
        oht = [ar.take(GRP * P, BF16) for _ in range(2)]
        wsel = [ar.take(GRP * 3 * R).rearrange("p (j k n) -> p j k n", j=GRP, k=3) for _ in range(2)]
        wgt = [ar.take(GRP) for _ in range(2)]
        zerob = ar.take(512, BF16)
        rc_rest = ar.take(NT * R).rearrange("p (w r) -> p w r", r=R)
        rc_part = ar.take(NT * R).rearrange("p (w r) -> p w r", r=R)

        ar = Arena(0)
        w_qt = ar.take(KC * C).rearrange("p (k n) -> p k n", k=KC)
        w_qc = ar.take(KC * C).rearrange("p (k n) -> p k n", k=KC)
        w_proj = ar.take(KC * C).rearrange("p (k n) -> p k n", k=KC)
        bproj_b = ar.take(C)
        wg2 = ar.take(C, FP32, 64)
        bg2 = ar.take(C, FP32, 1)
        bdc = ar.take(KC * P).rearrange("p (k n) -> p k n", k=KC)
        cden = ar.take(KC)
        assert ar.at <= KC * R * C
        ar = Arena(after_weights0)
        m_xnt = ar.take(C)
        m_ek = ar.take(C)
        m_v = ar.take(2 * (P + 1))
        m_hgt = ar.take(P, FP32, 64)
        m_x = ar.take(C)
        m_sig = ar.take(C)
        m_pr = ar.take(C)
        m_prt = ar.take(C)
        m_xb = ar.take(C)
        m_out = ar.take(C)
        assert ar.at <= after_norm0

        ar = Arena()
        wx_t = ar.take(4 * C).rearrange("p (j n) -> p j n", j=4)
        w_fx = ar.take(KC * 512).rearrange("p (k n) -> p k n", k=KC)
        w_out = ar.take(4 * C).rearrange("p (j n) -> p j n", j=4)
        w_log = ar.take(KC * 512).rearrange("p (k n) -> p k n", k=KC)
        b_log = ar.take(512, FP32, 1)
        bslice8 = ar.take(512, FP32, 1)
        bx_c = ar.take(4)
        temp_c = ar.take(8, FP32, 1)
        rtemp_r = ar.take(8, FP32, 1)
        rtemp_b = ar.take(8)
        bfx_b = ar.take(512)
        wsl_bd = ar.take(P)
        wq_bd = ar.take(P)
        wk_bd = ar.take(P)
        wv_bd = ar.take(P)
        bout_r = ar.take(C, FP32, 1)
        f_m = ar.take(4 * C).rearrange("p (j n) -> p j n", j=4)
        after_ffn_w = ar.at
        f_u = ar.take(4 * 257).rearrange("p (j n) -> p j n", j=4)
        f_ut = ar.take(KC * 512).rearrange("p (k n) -> p k n", k=KC)
        f_den = ar.take(4)
        f_rden = ar.take(4)
        f_tok = ar.take(512)
        f_tok2 = ar.take(512)
        f_tokt = ar.take(512)
        f_qt = ar.take(512)
        f_kt = ar.take(512)
        f_v = ar.take(512)
        f_s = ar.take(512)
        f_s2 = ar.take(512)
        f_max = ar.take(4)
        f_sum = ar.take(4)
        f_rsum = ar.take(4)
        f_at = ar.take(512)
        f_ost = ar.take(512)
        a_x1 = [ar.take(C) for _ in range(2)]
        a_xin = [ar.take(C) for _ in range(2)]
        a_xn = [ar.take(C + 1) for _ in range(2)]
        a_xnt = [ar.take(C) for _ in range(2)]
        a_stats = [ar.take(6) for _ in range(2)]
        a_mv = [ar.take(2) for _ in range(2)]
        a_veps = [ar.take(1) for _ in range(2)]
        a_rstd = [ar.take(1) for _ in range(2)]
        a_max = [ar.take(8) for _ in range(2)]
        a_sum = [ar.take(8) for _ in range(2)]
        a_rsum = [ar.take(8) for _ in range(2)]
        a_lg = [ar.take(512) for _ in range(2)]
        a_ex = [ar.take(512) for _ in range(2)]
        a_sw = [ar.take(512) for _ in range(2)]
        a_swt = [ar.take(512) for _ in range(2)]
        after_a = ar.at
        ar = Arena(after_a)
        k_swt = [ar.take(512) for _ in range(2)]
        k_x1 = [ar.take(C) for _ in range(2)]
        k_x2 = [ar.take(C) for _ in range(2)]
        ar = Arena()
        w_q1 = ar.take(4 * C).rearrange("p (j n) -> p j n", j=4)
        w_o1t = ar.take(4 * C).rearrange("p (j n) -> p j n", j=4)
        w_neigh = ar.take(KC * C).rearrange("p (k n) -> p k n", k=KC)
        w_self = ar.take(KC * C).rearrange("p (k n) -> p k n", k=KC)
        w_comb = ar.take(KC * C).rearrange("p (k n) -> p k n", k=KC)
        w_rt = ar.take(KC * 8).rearrange("p (k n) -> p k n", k=KC)
        b_self = ar.take(C, FP32, 1)
        b_out1 = ar.take(C, FP32, 1)
        b_comb = ar.take(C, FP32, 1)
        d_bd = ar.take(512)
        d_t1 = ar.take(4 * C).rearrange("p (j n) -> p j n", j=4)
        logits = ar.take(NT * 8).rearrange("p (t e) -> p t e", e=8)
        comb = ar.take(NT * 8).rearrange("p (t e) -> p t e", e=8)
        ra = [ar.take(NT * 8).rearrange("p (t e) -> p t e", e=8) for _ in range(4)]
        rb = [ar.take(NT) for _ in range(6)]
        after_c = ar.at
        w_kv1 = ar.take(KC * 1024).rearrange("p (k n) -> p k n", k=KC)
        kv_mean = ar.take(KC * 16).rearrange("p (k n) -> p k n", k=KC)
        k_xnt = ar.take(C)
        k_sq = ar.take(1024)
        k_ss = ar.take(16)
        k_v1 = ar.take(16)
        k_pv = ar.take(8)
        k_root = ar.take(8)
        k_inv = ar.take(8)
        k_n = [ar.take(8) for _ in range(3)]
        k_rs = ar.take(8)
        k_kn = ar.take(512)
        k_v = ar.take(512)
        assert ar.at <= after_norm0, (ar.at, after_norm0)
        ar = Arena(after_c)
        c_hn = [ar.take(C) for _ in range(2)]
        c_hnt = [ar.take(C) for _ in range(2)]
        c_xnt = [ar.take(C) for _ in range(2)]
        c_x2 = [ar.take(C) for _ in range(2)]
        c_x3 = [ar.take(C) for _ in range(2)]
        c_xn = [ar.take(C) for _ in range(2)]
        c_x34 = [ar.take(C) for _ in range(2)]
        c_x4t = [ar.take(C) for _ in range(2)]
        c_stats = [ar.take(6) for _ in range(2)]
        c_mv = [ar.take(2) for _ in range(2)]
        c_veps = [ar.take(1) for _ in range(2)]
        c_rstd = [ar.take(1) for _ in range(2)]
        assert ar.at < after_norm0
        ar = Arena(after_c)
        w1_sb = ar.take(8 * KC * C).rearrange("p (e k n) -> p e k n", e=8, k=KC)
        w2_sb = ar.take(8 * KC * C).rearrange("p (e k n) -> p e k n", e=8, k=KC)
        b1_c = ar.take(16).rearrange("p (e k) -> p e k", k=KC)
        b2_sb = ar.take(C, FP32, 8)
        s_xt = [ar.take(4 * C).rearrange("p (j k n) -> p j k n", j=4, k=KC) for _ in range(2)]
        s_o = [ar.take(4 * C).rearrange("p (j n) -> p j n", j=4) for _ in range(2)]
        s_ct = [ar.take(512, FP32, 8) for _ in range(2)]
        s_cg = [ar.take(32) for _ in range(2)]
        s_h = [[ar.take(512) for _ in range(KC)] for _ in range(2)]

        def upto(step, value):
            return sem(step), value + share.get(step, (step, 0))[1]

        def due(value):
            return not isinstance(value, int) or value > 0

        def alone(eng):
            eng.nop(nofuse=True)

        def node_tiles(eng):
            yield 0, 0, 0
            yield 1, 1, 0
            with eng.Fori(1, NT // 2) as i:
                yield 2 * i, 0, i
                yield 2 * i + 1, 1, i
            yield NT - 1, 0, NT // 2

        def expert_groups(eng):
            yield 0, 0, 0, 4
            yield 1, 1, 0, 4
            with eng.Fori(1, NT // 8) as i:
                yield 2 * i, 0, i, 4
                yield 2 * i + 1, 1, i, 4
            yield NT // 4, 0, NT // 8, 1

        def following(t, s, n):
            return t + 1, 1 - s, n + s

        def skewed(eng):
            none = (None, None, None)
            yield (0, 0, 0), none, None
            for t, s, n in node_tiles(eng):
                if is_last(t):
                    yield none, (t, s, n), None
                else:
                    yield following(t, s, n), (t, s, n), None

        def is_last(t):
            return isinstance(t, int) and t == NT - 1

        def rows_of(t):
            return LAST if is_last(t) else P

        def bodies(eng):
            yield 0
            with eng.Fori(1, T // BODY) as i:
                yield i

        phase = {}

        def phase_end(eng):
            k = phase[eng.engine] = phase.get(eng.engine, 0) + 1
            eng.drain().then_inc(sem("phase_ended"), 1)
            eng.wait_ge(sem("phase_ended"), 5 * k)
            return k >= stop_after

        def col(v, t):
            return v[:, t:t + 1] if isinstance(t, int) else v[:, bass.ds(t, 1)]

        def rows(v, t):
            return v[t * P:(t + 1) * P, :] if isinstance(t, int) else v[bass.ds(t * P, P), :]

        def tile(v, t):
            return v[t, :, :] if isinstance(t, int) else v[bass.ds(t, 1), :, :].rearrange("a p c -> (a p) c")

        def at(v, t):
            return v[:, t, :] if isinstance(t, int) else v[:, bass.ds(t, 1), :].rearrange("p a c -> p (a c)")

        def span(v, start, n):
            return v[:, start:start + n] if isinstance(start, int) else v[:, bass.ds(start, n)]

        def windows(eng, first, n):
            _, ws = nc.values_load_multi_w_load_instructions(
                span(win, first, n), engines=[eng.engine], min_val=0, max_val=NT - 1,
                skip_runtime_bounds_check_because="a target is below N, so its window is below NT")
            return list(ws)

        def gather_bodies(eng):
            yield 0, 0, None
            with eng.Fori(1, NT - 1) as m:
                yield m, m, None
            yield NT - 1, NT - 1, None
            yield NT, None, None
            yield NT + 1, None, 0
            with eng.Fori(1, NT - 1) as m:
                yield m + (NT + 1), None, m
            yield 2 * NT, None, NT - 1
            for i in range(2 * NT + 1, T // BODY):
                yield i, None, None

        def between(i):
            return isinstance(i, int) and i == NT

        def staged(eng):
            def stages(u):
                return [(u - k, (u - k) % 2, (u - k) // 2) if 0 <= u - k < NT else (None, None, None) for k in range(3)]

            for u in range(4):
                yield stages(u)
            with eng.Fori(2, NT // 2) as i:
                yield [(2 * i, 0, i), (2 * i - 1, 1, i - 1), (2 * i - 2, 0, i - 1)]
                yield [(2 * i + 1, 1, i), (2 * i, 0, i), (2 * i - 1, 1, i - 1)]
            for u in range(NT - 1, NT + 2):
                yield stages(u)

        def target_windows(eng):
            yield 0
            with eng.Fori(1, NT) as w:
                yield w

        def copy_indices(act, pre, g, h, again):
            if due(again):
                act.wait_ge(*upto(f"{pre}_rows{h}", 16 * GRP * again))
            act.activation(idx_s[:, GRP * h:GRP * h + GRP], span(idx_t, g * GRP, GRP), ACT.Copy).then_inc(sem(f"{pre}_idx"), 1)

        def gather_rows(pool, pre, table):
            for i in bodies(pool):
                for h in range(BPB):
                    g = i * BPB + h
                    pool.wait_ge(*upto(f"{pre}_idx", g + 1))
                    alone(pool)
                    if due(i):
                        pool.wait_ge(*upto(f"{pre}_sum_mm", 2 * (g - BPB + 1)))
                        alone(pool)
                    for j in range(GRP):
                        k = GRP * h + j
                        pool.indirect_dma_start(
                            out=ring[k], out_offset=None, in_=table,
                            in_offset=bass.IndirectOffsetOnAxis(ap=idx_s[:, k:k + 1], axis=0),
                        ).then_inc(sem(f"{pre}_rows{h}"), 16)

        heads = lambda v, h=8: v.rearrange("p (h g) -> p h g", h=h)
        block = ctx.enter_context(nc.Block())

        @block.sync
        def _(sp):
            sp.dma_start(e_dst, dst.rearrange("(p c) -> p c", p=EROWS)).then_inc(sem("edges_in"), 16)
            sp.dma_start(e_src, src.rearrange("(p c) -> p c", p=EROWS)).then_inc(sem("edges_in"), 16)
            sp.dma_start(e_typ, etype.rearrange("(p c) -> p c", p=EROWS)).then_inc(sem("edges_in"), 16)
            sp.wait_ge(*upto("words_packed", 2))
            sp.dma_start(words[0:E, :].rearrange("(p c) o -> p (c o)", p=EROWS), e_dst).then_inc(sem("words_out"), 16)
            sp.dma_start(words[E:E + PAD, :].rearrange("(p c) o -> p (c o)", p=PROWS), e_pad).then_inc(sem("words_out"), 16)
            sp.wait_ge(*upto("words_final", 1))
            full = words[0:TB * P * P, :].rearrange("(b t e) o -> t b (e o)", t=P, e=P)
            sp.dma_start(r_word.rearrange("t (b e) -> t b e", b=TB), full).then_inc(sem("rows_in"), 16)
            nxt = words[P:P + TB * P * P, :].rearrange("(b t e) o -> t b (e o)", t=P, e=P)[:, :, 0:1]
            sp.dma_start(r_next.rearrange("t (b e) -> t b e", e=1), nxt, allow_slow_non_contiguous=True).then_inc(sem("rows_in"), 16)
            if phase_end(sp):
                return
            for n_, (d_, s_) in enumerate([
                    (w_all, gnn0_w.rearrange("(k p) n -> p k n", p=P)),
                    (w_root, gnn0_root.rearrange("(k p) n -> p k n", p=P)),
                    (w_k0, mix_wqkv[:, C:2 * C].rearrange("(k p) n -> p k n", p=P)),
                    (w_v0, mix_wqkv[:, 2 * C:3 * C].rearrange("(k p) n -> p k n", p=P)),
                    (wg1_raw, mix_wg1.rearrange("(k p) n -> p k n", p=P)),
                    (lng, mix_ln_g),
                    (lnb, mix_ln_b),
                    (bg1_b, mix_bg1.partition_broadcast(P)),
                    (bias0_b, gnn0_bias.partition_broadcast(P))]):
                sp.dma_start(d_, s_).then_inc(sem("w0_in"), 16)
            for t, s, n in node_tiles(sp):
                r = rows_of(t)
                if due(t - 1):
                    sp.wait_ge(*upto("n0_xn", t - 1))
                    alone(sp)
                source = x[(NT - 1) * P:N, :] if is_last(t) else rows(x, t)
                sp.dma_start(xin[s][0:r, :], source).then_inc(sem(f"n0_in{s}"), 16)
            if phase_end(sp):
                return
            if phase_end(sp):
                return
            for d_, s_ in [(w_qt, mix_wq_t.rearrange("(k p) n -> p k n", p=P)),
                           (w_proj, mix_wproj.rearrange("(k p) n -> p k n", p=P)),
                           (bproj_b, mix_bproj.partition_broadcast(P)),
                           (wg2, mix_wg2), (bg2, mix_bg2.rearrange("(a n) -> a n", a=1))]:
                sp.dma_start(d_, s_).then_inc(sem("w_mix_in"), 16)
            for t, s, n in node_tiles(sp):
                if due(t):
                    sp.wait_ge(*upto("m1_v_mm", t))
                    alone(sp)
                sp.dma_start(m_xnt, tile(xnt_d, t)).then_inc(sem("m1_in"), 16)
            sp.wait_ge(*upto("m1_v_mm", NT))
            for t, s, n in node_tiles(sp):
                r = rows_of(t)
                if due(t):
                    sp.wait_ge(*upto("m2_g_mm", t))
                    alone(sp)
                    sp.wait_ge(*upto("m2_xb", t))
                    alone(sp)
                sp.dma_start(m_xnt, tile(xnt_d, t)).then_inc(sem("m2_in"), 16)
                sp.dma_start(m_hgt, tile(hgt_d, t)).then_inc(sem("m2_in"), 16)
                source = x[(NT - 1) * P:N, :] if is_last(t) else rows(x, t)
                sp.dma_start(m_x[0:r, :], source).then_inc(sem("m2_in"), 16)
                if due(t):
                    sp.wait_ge(*upto("m2_out", t))
                    alone(sp)
                    sp.dma_start(rows(xm_d, t - 1), m_out).then_inc(sem("m2_st"), 16)
            sp.wait_ge(*upto("m2_out", NT))
            sp.dma_start(rows(xm_d, NT - 1), m_out).then_inc(sem("m2_st"), 16)
            sp.wait_ge(*upto("m2_st", 16 * NT))
            if phase_end(sp):
                return
            for d_, s_ in [(wx_t, ffn_wx_t.rearrange("(j p) n -> p j n", p=P)),
                           (w_fx, ffn_wfx.rearrange("(k p) n -> p k n", p=P)),
                           (w_out, ffn_wout.rearrange("(j p) n -> p j n", p=P)),
                           (bx_c, ffn_bx),
                           (temp_c, ffn_temp),
                           (bfx_b, ffn_bfx.partition_broadcast(P)),
                           (bout_r, ffn_bout.rearrange("(a n) -> a n", a=1))]:
                sp.dma_start(d_, s_).then_inc(sem("w_ffn_in"), 16)
            sp.wait_ge(*upto("bd_zeroed", 4))
            for d_, s_ in [(wsl_bd, ffn_wslice), (wq_bd, ffn_wq), (wk_bd, ffn_wk), (wv_bd, ffn_wv)]:
                for b_ in range(2):
                    sp.dma_start(d_[64 * b_:64 * b_ + 64, 64 * b_:64 * b_ + 64], s_).then_inc(sem("w_ffn_in"), 16)
            for h in range(8):
                sp.dma_start(bslice8[0:1, 64 * h:64 * h + 64], ffn_bslice.rearrange("(a n) -> a n", a=1)).then_inc(sem("w_ffn_in"), 16)
            for t, s, n in node_tiles(sp):
                if due(t - 1):
                    sp.wait_ge(*upto("f1_x1", t - 1))
                    alone(sp)
                sp.dma_start(a_xin[s], rows(xm_d, t)).then_inc(sem(f"f1_in{s}"), 16)
            if phase_end(sp):
                return
            def store2(t, s):
                sp.wait_ge(*upto("f2_x2", t + 1))
                alone(sp)
                sp.dma_start(rows(x2_d, t), k_x2[s]).then_inc(sem(f"f2_x2_out{s}"), 16)
                sp.wait_ge(*upto("f2_xn", t + 1))
                alone(sp)

            for t, s, n in node_tiles(sp):
                if due(t - 1):
                    sp.wait_ge(*upto("f2_o_mm", t - 1))
                    alone(sp)
                    sp.wait_ge(*upto("f2_x2", t - 1))
                    alone(sp)
                sp.dma_start(k_swt[s], tile(swt_d, t)).then_inc(sem(f"f2_in{s}"), 16)
                sp.dma_start(k_x1[s], rows(x1_d, t)).then_inc(sem(f"f2_in{s}"), 16)
                if due(t - 1):
                    store2(t - 2, s)
                    sp.dma_start(rows(xn3_d, t - 2), a_xn[s][:, 0:C]).then_inc(sem(f"f2_xn_out{s}"), 16)
            for t in (NT - 2, NT - 1):
                store2(t, t % 2)
                sp.dma_start(rows(xn3_d, t), a_xn[t % 2][:, 0:C]).then_inc(sem(f"f2_xn_out{t % 2}"), 16)
            for s in range(2):
                for name in (f"f2_x2_out{s}", f"f2_xn_out{s}"):
                    sp.wait_ge(*upto(name, 16 * (NT // 2 + 1 - s)))
            if phase_end(sp):
                return
            sp.dma_start(w_kv1, mix1_wkv_t.rearrange("(k p) n -> p k n", p=P)).then_inc(sem("w_kv_in"), 16)
            for d_, s_ in [(w_q1, mix1_wqkv[0:512, :].rearrange("(j p) n -> p j n", p=P)),
                           (w_o1t, mix1_wout_t.rearrange("(j p) n -> p j n", p=P)),
                           (w_neigh, gnn1_wneigh_t.rearrange("(k p) n -> p k n", p=P)),
                           (w_self, gnn1_wself_t.rearrange("(k p) n -> p k n", p=P)),
                           (w_rt, router_t.rearrange("(k p) n -> p k n", p=P)),
                           (b_self, gnn1_bself.rearrange("(a n) -> a n", a=1)),
                           (b_out1, mix1_bout.rearrange("(a n) -> a n", a=1))]:
                sp.dma_start(d_, s_).then_inc(sem("w_l1_in"), 16)
            for t, s, n in node_tiles(sp):
                if due(t):
                    sp.wait_ge(*upto("kv_v_mm", t))
                    alone(sp)
                sp.dma_start(k_xnt, tile(xnt3_d, t)).then_inc(sem("kv_in"), 16)
            if phase_end(sp):
                return
            for t, s, n in node_tiles(sp):
                if due(t - 1):
                    sp.wait_ge(*upto("c_x_mm", t - 1))
                    alone(sp)
                if due(t - 1):
                    sp.wait_ge(*upto("c_x3", t - 1))
                    alone(sp)
                sp.dma_start(c_xnt[s], tile(xnt3_d, t)).then_inc(sem(f"c_in{s}"), 16)
                sp.dma_start(c_x2[s], rows(x2_d, t)).then_inc(sem(f"c_in{s}"), 16)
            if phase_end(sp):
                return
            sp.dma_start(w1_sb, w1.rearrange("e (k p) n -> p e k n", p=P)).then_inc(sem("w_moe_in"), 16)
            sp.dma_start(w2_sb, w2.rearrange("e (k p) n -> p e k n", p=P)).then_inc(sem("w_moe_in"), 16)
            sp.dma_start(b1_c, b1.rearrange("p (e k) -> p e k", k=KC)).then_inc(sem("w_moe_in"), 16)
            sp.dma_start(b2_sb, b2).then_inc(sem("w_moe_in"), 16)
            for g, s, n, m in expert_groups(sp):
                if due(16 * (g - 1)):
                    sp.wait_ge(*upto("s_h_mm", 16 * (g - 1)))
                    alone(sp)
                if due(16 * n):
                    sp.wait_ge(*upto(f"s_out{s}", 16 * n))
                    alone(sp)
                if m == 4:
                    xs = xnt4_d[4 * g:4 * g + 4, :, :] if isinstance(g, int) else xnt4_d[bass.ds(g * 4, 4), :, :]
                    os_ = x34_d[512 * g:512 * g + 512, :] if isinstance(g, int) else x34_d[bass.ds(g * 512, 512), :]
                else:
                    xs, os_ = xnt4_d[NT - 1:NT, :, :], x34_d[(NT - 1) * P:NP, :]
                sp.dma_start(s_xt[s][:, 0:m, :, :].rearrange("p j k n -> p j (k n)"),
                             xs.rearrange("j p c -> p j c")).then_inc(sem(f"s_in{s}"), 16)
                sp.dma_start(s_o[s][:, 0:m, :], os_.rearrange("(j p) c -> p j c", p=P)).then_inc(sem(f"s_in{s}"), 16)
            phase_end(sp)

        @block.gpsimd
        def _(pool):
            pool.iota(iota_i, pattern=[[1, P]], base=0, channel_multiplier=0).then_inc(sem("iotas"), 1)
            pool.iota(col_i, pattern=[[0, 1]], base=0, channel_multiplier=1).then_inc(sem("iotas"), 1)
            pool.memset(ones[:, :], 1.0).then_inc(sem("const"), 1)
            pool.memset(mhalf[:, :], -0.5).then_inc(sem("const"), 1)
            pool.memset(e_pad, PAD_DST << 16).then_inc(sem("words_packed"), 1)
            for v in (idx_t, dl_t):
                pool.memset(v[:, ET + NT - 1:TW], 0 if v is idx_t else -1.0).then_inc(sem("table_pad"), 1)
            pool.memset(win[:, ET + NT - 1:TW], NT - 1).then_inc(sem("table_pad"), 1)
            pool.wait_ge(*upto("q_flag", 1))
            unsorted = pool.value_load(q_flag, min_val=0, max_val=1)
            pool.wait_ge(*upto("words_out", 32))
            with pool.If(unsorted > 0):
                pool.wait_ge(*upto("q_posi", 1))
                with pool.Fori(0, ECOLS // SCAT) as i:
                    pool.tensor_copy(q_islot, span(q_posi, i * SCAT, SCAT)).then_inc(sem("q_slots"), 1)
                    pool.tensor_copy(q_wslot, span(e_dst, i * SCAT, SCAT)).then_inc(sem("q_slots"), 1)
                    pool.wait_ge(*upto("q_slots", 2 * i + 2))
                    alone(pool)
                    for k in range(SCAT):
                        pool.indirect_dma_start(
                            out=words[0:E, :], out_offset=bass.IndirectOffsetOnAxis(ap=q_islot[:, k:k + 1], axis=0),
                            in_=q_wslot[:, k:k + 1], in_offset=None).then_inc(sem("q_scattered"), 16)
                    pool.wait_ge(*upto("q_scattered", 16 * SCAT * (i + 1)))
                    alone(pool)
            pool.nop().then_inc(sem("words_final"), 1)
            if phase_end(pool):
                return
            for t, s, n in skewed(pool):
                if t[0] is not None:
                    t_, s_, n_ = t
                    pool.wait_ge(*upto("n0_var", t_ + 1))
                    alone(pool)
                    pool.tensor_tensor(rstd[s_][:, 0:1], veps[s_][:, 0:1], mhalf[:, 0:1], ALU.pow).then_inc(sem("n0_rstd"), 1)
                    pool.wait_ge(*upto("n0_gvar", t_ + 1))
                    alone(pool)
                    pool.tensor_tensor(grstd[s_], gveps[s_], mhalf[:, 0:1], ALU.pow).then_inc(sem("n0_grstd"), 1)
                if s[0] is not None:
                    t_, s_, n_ = s
                    pool.wait_ge(*upto("n0_xnt", t_ + 1))
                    alone(pool)
                    pool.dma_start(tile(xnt_d, t_), xnt[s_]).then_inc(sem(f"n0_xnt_out{s_}"), 16)
                    pool.wait_ge(*upto("n0_y_act", 2 * t_ + 2))
                    alone(pool)
                    pool.wait_ge(*upto("n0_y_dve", 2 * t_ + 2))
                    alone(pool)
                    pool.dma_start(rows(y_rows, t_), ysb[s_]).then_inc(sem(f"n0_y_out{s_}"), 16)
                    pool.wait_ge(*upto("n0_hgt", t_ + 1))
                    alone(pool)
                    pool.dma_start(tile(hgt_d, t_), hgt[s_]).then_inc(sem(f"n0_hgt_out{s_}"), 16)
            for s in range(2):
                v = NT // 2 + 1 - s
                for name in (f"n0_xnt_out{s}", f"n0_y_out{s}", f"n0_hgt_out{s}"):
                    pool.wait_ge(*upto(name, 16 * v))
            if phase_end(pool):
                return
            if phase_end(pool):
                return
            gather_rows(pool, "g0", y_table)
            if phase_end(pool):
                return
            for v in (wsl_bd, wq_bd, wk_bd, wv_bd):
                pool.memset(v, 0.0).then_inc(sem("bd_zeroed"), 1)
            for s in range(2):
                pool.memset(a_xn[s][:, C:C + 1], 1.0).then_inc(sem("a_ones"), 1)
            for t, s, n in skewed(pool):
                if t[0] is not None:
                    t_, s_, n_ = t
                    pool.wait_ge(*upto("f1_var", t_ + 1))
                    alone(pool)
                    pool.tensor_tensor(a_rstd[s_], a_veps[s_], mhalf[:, 0:1], ALU.pow).then_inc(sem("f1_rstd"), 1)
                    pool.dma_start(rows(x1_d, t_), a_x1[s_]).then_inc(sem(f"f1_x1_out{s_}"), 16)
                if s[0] is not None:
                    t_, s_, n_ = s
                    pool.wait_ge(*upto("f1_swt", t_ + 1))
                    alone(pool)
                    pool.dma_start(tile(swt_d, t_), a_swt[s_]).then_inc(sem(f"f1_swt_out{s_}"), 16)
            for s in range(2):
                if due(16 * (NT // 2 + 1 - s)):
                    pool.wait_ge(*upto(f"f1_x1_out{s}", 16 * (NT // 2 + 1 - s)))
                    alone(pool)
                if due(16 * (NT // 2 + 1 - s)):
                    pool.wait_ge(*upto(f"f1_swt_out{s}", 16 * (NT // 2 + 1 - s)))
                    alone(pool)
            if phase_end(pool):
                return
            for t, s, n in node_tiles(pool):
                pool.wait_ge(*upto("f2_var", t + 1))
                alone(pool)
                pool.tensor_tensor(a_rstd[s], a_veps[s], mhalf[:, 0:1], ALU.pow).then_inc(sem("f2_rstd"), 1)
            if phase_end(pool):
                return
            gather_rows(pool, "g1", xn3_d)
            if phase_end(pool):
                return
            for t_, s_, n_ in node_tiles(pool):
                    pool.wait_ge(*upto("c_var", t_ + 1))
                    alone(pool)
                    pool.tensor_tensor(c_rstd[s_], c_veps[s_], mhalf[:, 0:1], ALU.pow).then_inc(sem("c_rstd"), 1)
                    pool.wait_ge(*upto("c_x34", t_ + 1))
                    alone(pool)
                    pool.dma_start(rows(x34_d, t_), c_x34[s_]).then_inc(sem(f"c_x34_out{s_}"), 16)
                    pool.wait_ge(*upto("c_x4t", t_ + 1))
                    alone(pool)
                    pool.dma_start(tile(xnt4_d, t_), c_x4t[s_]).then_inc(sem(f"c_x4t_out{s_}"), 16)
            for s in range(2):
                if due(16 * (NT // 2 + 1 - s)):
                    pool.wait_ge(*upto(f"c_x34_out{s}", 16 * (NT // 2 + 1 - s)))
                    alone(pool)
                if due(16 * (NT // 2 + 1 - s)):
                    pool.wait_ge(*upto(f"c_x4t_out{s}", 16 * (NT // 2 + 1 - s)))
                    alone(pool)
            if phase_end(pool):
                return
            for g, s, n, m in expert_groups(pool):
                pool.wait_ge(*upto("s_acc", 32 * (g + 1) if m == 4 else 32 * g + 8))
                alone(pool)
                if m == 4:
                    o_ = out[512 * g:512 * g + 512, :] if isinstance(g, int) else out[bass.ds(g * 512, 512), :]
                    pool.dma_start(o_.rearrange("(j p) c -> p j c", p=P), s_o[s]).then_inc(sem(f"s_out{s}"), 16)
                else:
                    pool.dma_start(out[(NT - 1) * P:N, :], s_o[s][0:LAST, 0, :]).then_inc(sem(f"s_out{s}"), 16)
            pool.wait_ge(*upto("s_out0", 16 * (NT // 8 + 1)))
            pool.wait_ge(*upto("s_out1", 16 * (NT // 8)))
            phase_end(pool)

        @block.scalar
        def _(act):
            if phase_end(act):
                return
            for t, s, n in skewed(act):
                if t[0] is not None:
                    t_, s_, n_ = t
                    act.wait_ge(*upto("n0_t", t_ + 1))
                    if due(t_ - 1):
                        act.wait_ge(*upto("n0_km_mm", t_ - 1))
                    if due(16 * n_):
                        act.wait_ge(*upto(f"n0_xnt_out{s_}", 16 * n_))
                    act.activation(xnt[s_], bank[4][:, 0:C], ACT.Copy).then_inc(sem("n0_xnt"), 1)
                if s[0] is not None:
                    t_, s_, n_ = s
                    if due(16 * n_):
                        act.wait_ge(*upto(f"n0_y_out{s_}", 16 * n_))
                    for b_ in (0, 2):
                        act.wait_ge(*upto(f"n0_y_mm{b_}", t_ + 1))
                        act.activation(ysb[s_][:, 512 * b_:512 * b_ + 512], bank[b_][:, :], ACT.Copy).then_inc(sem("n0_y_act"), 1)
                    act.wait_ge(*upto("n0_gate", t_ + 1))
                    if due(t_ - 1):
                        act.wait_ge(*upto("n0_hg_t", t_ - 1))
                    act.activation(hg[s_], g_b[s_], ACT.Gelu, scale=-1.0).then_inc(sem("n0_hg"), 1)
                    act.wait_ge(*upto("n0_hg_t", t_ + 1))
                    if due(16 * n_):
                        act.wait_ge(*upto(f"n0_hgt_out{s_}", 16 * n_))
                    act.activation(hgt[s_], bank[7][0:64, 0:P], ACT.Copy).then_inc(sem("n0_hgt"), 1)
            if phase_end(act):
                return
            if phase_end(act):
                return
            def copy_oht(g, b_):
                act.wait_ge(*upto("g0_oht_mm", g + 1))
                if due(g - 1):
                    act.wait_ge(*upto("g0_look_mm", g - 1))
                act.activation(oht[b_], bank[6][:, :], ACT.Copy).then_inc(sem("g0_oht"), 1)

            for g in range(BPB):
                copy_indices(act, "g0", g, g, 0)
            for g in range(2):
                copy_oht(g, g)
            for i, m1, m2 in gather_bodies(act):
                for h in range(BPB):
                    g = i * BPB + h
                    copy_oht(g + 2, h % 2)
                    copy_indices(act, "g0", g + BPB, h, i + 1)
                    if m1 is not None and h == 1:
                        act.wait_ge(*upto("m1_k_mm", m1 + 1))
                        if due(m1):
                            act.wait_ge(*upto("m1_ctx_mm", m1))
                        act.activation(m_ek, bank[4][:, 0:C], ACT.Exp).then_inc(sem("m1_ek"), 1)
                    if m2 is not None and h == 0:
                        act.wait_ge(*upto("m2_g_mm", m2 + 1))
                        if due(m2):
                            act.wait_ge(*upto("m2_pr", m2))
                        act.activation(m_sig, bank[5][:, 0:C], ACT.Sigmoid).then_inc(sem("m2_sig"), 1)
                    if m2 is not None and h == 2:
                        act.wait_ge(*upto("m2_prt_mm", m2 + 1))
                        if due(m2):
                            act.wait_ge(*upto("m2_f_mm", m2))
                        act.activation(m_prt, bank[2][:, 0:C], ACT.Copy).then_inc(sem("m2_prt"), 1)
            if phase_end(act):
                return
            for t, s, n in skewed(act):
                if t[0] is not None:
                    t_, s_, n_ = t
                    act.wait_ge(*upto("f1_t", t_ + 1))
                    if due(t_ - 1):
                        act.wait_ge(*upto("f1_l_mm", t_ - 1))
                    act.activation(a_xnt[s_], bank[0][:, 0:C], ACT.Copy).then_inc(sem("f1_xnt"), 1)
                if s[0] is not None:
                    t_, s_, n_ = s
                    act.wait_ge(*upto("f1_lg", t_ + 1))
                    if due(t_ - 1):
                        act.wait_ge(*upto("f1_sw", t_ - 1))
                    act.activation(a_ex[s_], a_lg[s_], ACT.Exp).then_inc(sem("f1_ex"), 1)
                    act.wait_ge(*upto("f1_swt_mm", t_ + 1))
                    if due(16 * n_):
                        act.wait_ge(*upto(f"f1_swt_out{s_}", 16 * n_))
                    act.activation(a_swt[s_], bank[3][:, :], ACT.Copy).then_inc(sem("f1_swt"), 1)
            for j in range(4):
                act.wait_ge(*upto("fs_max", j + 1))
                act.activation(f_s2[:, P * j:P * j + P], f_s[:, P * j:P * j + P], ACT.Exp, bias=f_max[:, j:j + 1],
                               scale=1.0, accum_out=f_sum[:, j:j + 1]).then_inc(sem("fs_exp"), 1)
            if phase_end(act):
                return
            for t_, s_, n_ in node_tiles(act):
                act.wait_ge(*upto("f2_t", t_ + 1))
                if due(16 * n_):
                    act.wait_ge(*upto(f"f2_xnt_out{s_}", 16 * n_))
                act.activation(a_xnt[s_], bank[2][:, 0:C], ACT.Copy).then_inc(sem("f2_xnt"), 1)
                act.wait_ge(*upto("f2_xnt", t_ + 1))
                alone(act)
                act.dma_start(tile(xnt3_d, t_), a_xnt[s_]).then_inc(sem(f"f2_xnt_out{s_}"), 16)
            for s in range(2):
                act.wait_ge(*upto(f"f2_xnt_out{s}", 16 * (NT // 2 + 1 - s)))
            if phase_end(act):
                return
            for g in range(BPB):
                copy_indices(act, "g1", g, g, 0)
            for i, m1, m2 in gather_bodies(act):
                for h in range(BPB):
                    copy_indices(act, "g1", (i + 1) * BPB + h, h, i + 1)
                    if m1 is not None and h == 0:
                        act.wait_ge(*upto("kv_k_mm", m1 + 1))
                        if due(m1):
                            act.wait_ge(*upto("kv_ss", m1))
                        act.activation(k_sq[:, 0:512], bank[2][:, :], ACT.Square).then_inc(sem("kv_sqk"), 1)
                        act.wait_ge(*upto("kv_v_mm", m1 + 1))
                        act.activation(k_sq[:, 512:1024], bank[3][:, :], ACT.Square).then_inc(sem("kv_sqv"), 1)
                        if due(m1):
                            act.wait_ge(*upto("kv_dots_mm", m1))
                        act.activation(k_v, bank[3][:, :], ACT.Copy).then_inc(sem("kv_v"), 1)
                    if m1 is not None and h == 1:
                        act.wait_ge(*upto("kv_pv", m1 + 1))
                        if due(m1):
                            act.wait_ge(*upto("kv_inv", m1))
                        act.activation(k_root, k_pv, ACT.Sqrt).then_inc(sem("kv_root"), 1)
            if phase_end(act):
                return
            for t, s, n in skewed(act):
                if t[0] is not None:
                    t_, s_, n_ = t
                    act.wait_ge(*upto("c_hn_t", t_ + 1))
                    if due(t_ - 1):
                        act.wait_ge(*upto("c_x_mm", t_ - 1))
                    act.activation(c_hnt[s_], bank[0][:, 0:C], ACT.Copy).then_inc(sem("c_hnt"), 1)
                if s[0] is not None:
                    t_, s_, n_ = s
                    act.wait_ge(*upto("c_x4_t", t_ + 1))
                    if due(t_ - 1):
                        act.wait_ge(*upto("c_r_mm", t_ - 1))
                    if due(16 * n_):
                        act.wait_ge(*upto(f"c_x4t_out{s_}", 16 * n_))
                    act.activation(c_x4t[s_], bank[2][:, 0:C], ACT.Copy).then_inc(sem("c_x4t"), 1)
            act.wait_ge(*upto("r_exp_in", 1))
            act.activation(ra[1], ra[0], ACT.Exp).then_inc(sem("r_exp"), 1)
            if phase_end(act):
                return
            for g, s, n, m in expert_groups(act):
                act.wait_ge(*upto("s_ct_mm", g + 1))
                if due(g - 1):
                    act.wait_ge(*upto("s_cb_mm", g - 1))
                act.activation(s_ct[s][:, 0:m * P], bank[6][0:8, 0:m * P], ACT.Copy).then_inc(sem("s_ct"), 1)
                act.wait_ge(*upto("w_moe_in", 64))
                for e in range(8):
                    for f in range(KC):
                        k = 16 * g + 2 * e + f
                        act.wait_ge(*upto("s_h_mm", k + 1))
                        if due(8 * g + e - 1):
                            act.wait_ge(*upto("s_y_mm", 8 * g + e - 1))
                        act.activation(s_h[e % 2][f][:, 0:m * P], bank[2 * (e % 2) + f][:, 0:m * P], ACT.Gelu,
                                       bias=b1_c[:, e, f:f + 1]).then_inc(sem("s_h"), 1)
            phase_end(act)

        @block.vector
        def _(dve):
            step = [0]

            def chain(ins):
                step[0] += 1
                ins.then_inc(sem("dve_chain"), 1)
                dve.wait_ge(sem("dve_chain"), step[0])

            dve.wait_ge(*upto("iotas", 2))
            chain(dve.tensor_copy(iota[:, :], iota_i))
            chain(dve.tensor_copy(blk_f[:, 0:1], col_i))
            chain(dve.tensor_scalar(ident[:, :], iota[:, :], blk_f[:, 0:1], None, ALU.is_equal))
            chain(dve.tensor_copy(identb[:, :], ident[:, :]))
            for bd, sh in ((bd32, 5), (bd64, 6)):
                chain(dve.tensor_scalar(row_bi, iota_i, sh, None, ALU.arith_shift_right))
                chain(dve.tensor_copy(row_b, row_bi))
                chain(dve.tensor_scalar(blk_i[:, 0:1], col_i, sh, None, ALU.arith_shift_right))
                chain(dve.tensor_copy(blk_f[:, 1:2], blk_i[:, 0:1]))
                chain(dve.tensor_scalar(bd[:, :], row_b, blk_f[:, 1:2], None, ALU.is_equal))
            chain(dve.tensor_scalar(off64[:, :], bd64[:, :], -1.0, 1e30, ALU.add, ALU.mult))
            dve.wait_ge(*upto("edges_in", 48))
            chain(dve.scalar_tensor_tensor(e_src, e_src, 3, e_typ, ALU.logical_shift_left, ALU.bitwise_or))
            dve.scalar_tensor_tensor(e_dst, e_dst, 16, e_src, ALU.logical_shift_left, ALU.bitwise_or).then_inc(sem("words_packed"), 1)
            dve.wait_ge(*upto("words_packed", 2))
            chain(dve.tensor_scalar(q_posi, e_dst, 23, None, ALU.logical_shift_right))
            chain(dve.tensor_copy(e_win, q_posi))
            chain(dve.tensor_tensor(q_mask[:, 0:ECOLS - 1], e_win[:, 0:ECOLS - 1], e_win[:, 1:ECOLS], ALU.is_gt))
            dve.tensor_reduce(q_viol, q_mask[:, 0:ECOLS - 1], AX, ALU.add).then_inc(sem("q_viol"), 1)
            dve.wait_ge(*upto("q_rows_mm", 1))
            chain(dve.tensor_copy(q_row, bank[5][0:1, 0:3 * EROWS]))
            chain(dve.tensor_tensor(q_row[:, 0:EROWS - 1], q_row[:, EROWS:2 * EROWS - 1], q_row[:, 1:EROWS], ALU.is_gt))
            chain(dve.tensor_tensor(q_row[:, 0:EROWS - 1], q_row[:, 0:EROWS - 1], q_row[:, 2 * EROWS:3 * EROWS - 1], ALU.add))
            chain(dve.tensor_reduce(q_one[:, 0:1], q_row[:, 0:EROWS - 1], AX, ALU.add))
            chain(dve.tensor_tensor(q_one[:, 0:1], q_one[:, 0:1], q_row[:, 3 * EROWS - 1:3 * EROWS], ALU.add))
            chain(dve.tensor_scalar(q_one[:, 1:2], q_one[:, 0:1], 1.0, None, ALU.min))
            dve.tensor_copy(q_flag, q_one[:, 1:2]).then_inc(sem("q_flag"), 1)
            dve.wait_ge(*upto("q_flag", 1))
            unsorted = dve.value_load(q_flag, min_val=0, max_val=1)
            with dve.If(unsorted > 0):
                dve.tensor_scalar(q_tri, iota[0:EROWS, 0:EROWS], blk_f[0:EROWS, 0:1], None, ALU.is_gt).then_inc(sem("q_start"), 1)
                dve.memset(q_base, -1.0).then_inc(sem("q_start"), 1)
                dve.memset(q_pos, 0.0).then_inc(sem("q_start"), 1)
                dve.wait_ge(*upto("q_start", 3))
                for w in target_windows(dve):
                    if due(w):
                        dve.wait_ge(*upto("q_pos", w))
                    dve.tensor_scalar(q_mask, e_win, col(iota[0:EROWS, :], w), None, ALU.is_equal).then_inc(sem("q_mask"), 1)
                    dve.wait_ge(*upto("q_mask", w + 1))
                    dve.tensor_tensor_scan(q_pre, q_mask, q_mask, 0.0, ALU.add, ALU.max).then_inc(sem("q_pre"), 1)
                    dve.wait_ge(*upto("q_offs_mm", w + 1))
                    dve.tensor_tensor(q_offs, bank[5][0:EROWS, 0:1], q_base, ALU.add).then_inc(sem("q_offs"), 1)
                    dve.wait_ge(*upto("q_offs", w + 1))
                    dve.tensor_tensor(q_base, q_base, bank[5][0:EROWS, 1:2], ALU.add).then_inc(sem("q_base"), 1)
                    dve.scalar_tensor_tensor(q_pre, q_pre, q_offs, q_mask, ALU.add, ALU.mult).then_inc(sem("q_part"), 1)
                    dve.wait_ge(*upto("q_part", w + 1))
                    dve.wait_ge(*upto("q_base", w + 1))
                    dve.tensor_tensor(q_pos, q_pos, q_pre, ALU.add).then_inc(sem("q_pos"), 1)
                dve.wait_ge(*upto("q_pos", NT))
                dve.tensor_copy(q_posi, q_pos).then_inc(sem("q_posi"), 1)
            dve.wait_ge(*upto("rows_in", 32))
            chain(dve.tensor_scalar(r_int, r_word, 16, None, ALU.logical_shift_right))
            chain(dve.tensor_copy(r_dst, r_int))
            r_first = r_int.rearrange("t (b e) -> t b e", b=TB)[:, :, 0]
            chain(dve.tensor_scalar(r_w0i, r_first, 7, None, ALU.logical_shift_right))
            chain(dve.tensor_copy(r_w0, r_w0i))
            chain(dve.tensor_scalar(r_w1i, r_next, 23, None, ALU.logical_shift_right))
            chain(dve.tensor_copy(r_w1, r_w1i))
            chain(dve.tensor_scalar(r_int, r_word, 0xFFFF, None, ALU.bitwise_and))
            chain(dve.tensor_copy(r_idx, r_int))
            for b_ in range(TB):
                cols = slice(P * b_, P * b_ + P)
                chain(dve.tensor_scalar(r_dl[:, cols], r_w0[:, b_:b_ + 1].broadcast_to([P, P]), -float(P), None, ALU.mult))
                chain(dve.tensor_tensor(r_dl[:, cols], r_dl[:, cols], r_dst[:, cols], ALU.add))
                sc = slice((NT - 1) * b_, (NT - 1) * (b_ + 1))
                dve.tensor_scalar(r_sel[:, sc], iota[:, 1:NT], r_w0[:, b_:b_ + 1], None, ALU.is_gt).then_inc(sem("sel"), 1)
                dve.tensor_scalar(r_sel2[:, sc], iota[:, 1:NT], r_w1[:, b_:b_ + 1], None, ALU.is_gt).then_inc(sem("sel"), 1)
            dve.wait_ge(*upto("sel", 2 * TB))
            dve.tensor_tensor(r_sel, r_sel, r_sel2, ALU.subtract).then_inc(sem("rows_ready"), 1)
            dve.tensor_scalar(x_base, iota[:, 1:NT], float(P), None, ALU.mult).then_inc(sem("x_base"), 1)
            for b_ in range(TB):
                n_ = min(P, ET - P * b_)
                cols = slice(P * b_, P * b_ + n_)
                if due(3 * b_ + 3):
                    dve.wait_ge(*upto("tables_mm", 3 * b_ + 3))
                dve.tensor_copy(dl_t[:, cols], bank[b_ % 2][:, 0:n_]).then_inc(sem("tables"), 1)
                dve.tensor_copy(idx_t[:, cols], bank[b_ % 2][:, P:P + n_]).then_inc(sem("tables"), 1)
                dve.tensor_copy(win[:, cols], bank[b_ % 2][0:1, 2 * P:2 * P + n_]).then_inc(sem("tables"), 1)
            cols = slice(ET, ET + NT - 1)
            dve.wait_ge(*upto("extra_mm", 2))
            dve.wait_ge(*upto("x_base", 1))
            dve.tensor_tensor(dl_t[:, cols], bank[2][:, 0:NT - 1], x_base, ALU.subtract).then_inc(sem("tables"), 1)
            dve.tensor_copy(idx_t[:, cols], bank[3][:, 0:NT - 1]).then_inc(sem("tables"), 1)
            dve.tensor_copy(win[:, cols], iota[0:1, 1:NT]).then_inc(sem("tables"), 1)
            dve.wait_ge(*upto("tables", 3 * TB + 3))
            dve.wait_ge(*upto("table_pad", 3))
            ti = typ_t[:, :].bitcast(I32)
            chain(dve.tensor_scalar(ti, idx_t[:, :], 7, None, ALU.bitwise_and))
            chain(dve.tensor_copy(typ_t[:, :], ti))
            if phase_end(dve):
                return
            dve.wait_ge(*upto("w0_in", 16 * 9))
            for k in range(KC):
                dve.tensor_scalar(wg1[:, k, :], wg1_raw[:, k, :], lng[:, k:k + 1], None, ALU.mult).then_inc(sem("gate_w"), 1)
                dve.tensor_copy(lnb_b[:, k, :], lnb[:, k:k + 1].broadcast_to([P, P])).then_inc(sem("gate_w"), 1)
            dve.wait_ge(*upto("gate_w_mm", 2))
            chain(dve.tensor_copy(wg1_sum, bank[7][:, 0:64]))
            dve.tensor_tensor(gate_b, bank[6][:, 0:64], bg1_b, ALU.add).then_inc(sem("gate_b"), 1)
            dve.wait_ge(*upto("gate_b", 1))

            def variance(pre, src_, st, mv_, ve, t, ready):
                dve.wait_ge(*upto(*ready))
                dve.bn_stats(st, src_).then_inc(sem(pre + "_st"), 1)
                dve.wait_ge(*upto(pre + "_st", t + 1))
                alone(dve)
                dve.bn_aggr(mv_, st).then_inc(sem(pre + "_ag"), 1)
                dve.wait_ge(*upto(pre + "_ag", t + 1))
                dve.tensor_scalar(ve, mv_[:, 1:2], EPS, None, ALU.add).then_inc(sem(pre + "_var"), 1)

            def norm(pre, src_, dst_, st, mv_, ve, rs, t, ready, free):
                dve.wait_ge(*upto(*ready))
                dve.bn_stats(st, src_).then_inc(sem(pre + "_st"), 1)
                dve.wait_ge(*upto(pre + "_st", t + 1))
                alone(dve)
                dve.bn_aggr(mv_, st).then_inc(sem(pre + "_ag"), 1)
                dve.wait_ge(*upto(pre + "_ag", t + 1))
                dve.tensor_scalar(ve, mv_[:, 1:2], EPS, None, ALU.add).then_inc(sem(pre + "_var"), 1)
                dve.wait_ge(*upto(pre + "_rstd", t + 1))
                for f_ in free:
                    if due(f_[1]):
                        dve.wait_ge(*upto(*f_))
                dve.tensor_scalar(dst_, src_, mv_[:, 0:1], rs, ALU.subtract, ALU.mult).then_inc(sem(pre + "_xn"), 1)

            for t, s, n in skewed(dve):
                if t[0] is not None:
                    t_, s_, n_ = t
                    norm("n0", xin[s_], xn[s_][:, 0:C], stats[s_], mv[s_], veps[s_][:, 0:1], rstd[s_][:, 0:1], t_,
                         (f"n0_in{s_}", 16 * (n_ + 1)), [("n0_t", t_ - 1)])
                    dve.wait_ge(*upto("n0_xn", t_ + 1))
                    dve.bn_stats(gstats[s_], xn[s_][:, 0:C]).then_inc(sem("n0_gst"), 1)
                    dve.wait_ge(*upto("n0_gst", t_ + 1))
                    alone(dve)
                    dve.bn_aggr(gmv[s_], gstats[s_]).then_inc(sem("n0_gag"), 1)
                    dve.wait_ge(*upto("n0_gag", t_ + 1))
                    dve.tensor_scalar(gveps[s_], gmv[s_][:, 1:2], EPS, None, ALU.add).then_inc(sem("n0_gvar"), 1)
                if s[0] is not None:
                    t_, s_, n_ = s
                    if due(16 * n_):
                        dve.wait_ge(*upto(f"n0_y_out{s_}", 16 * n_))
                    for b_ in (1, 3):
                        dve.wait_ge(*upto(f"n0_y_mm{b_}", t_ + 1))
                        dve.tensor_copy(ysb[s_][:, 512 * b_:512 * b_ + 512], bank[b_][:, :]).then_inc(sem("n0_y_dve"), 1)
                    dve.wait_ge(*upto("n0_root_mm", t_ + 1))
                    dve.tensor_tensor(at(acc, t_), bank[5][:, 0:C], bias0_b, ALU.add).then_inc(sem("n0_root"), 1)
                    dve.wait_ge(*upto("n0_grstd", t_ + 1))
                    dve.scalar_tensor_tensor(g_a[s_], wg1_sum, gmv[s_][:, 0:1], bank[5][:, C:C + 64], ALU.mult, ALU.subtract).then_inc(sem("n0_ga"), 1)
                    dve.wait_ge(*upto("n0_ga", t_ + 1))
                    if due(t_ - 1):
                        dve.wait_ge(*upto("n0_hg", t_ - 1))
                    dve.scalar_tensor_tensor(g_b[s_], g_a[s_], grstd[s_], gate_b, ALU.mult, ALU.subtract).then_inc(sem("n0_gate"), 1)
                    dve.wait_ge(*upto("n0_km_mm", t_ + 1))
                    dve.tensor_reduce(at(kmax, t_), bank[6][:, 0:C].rearrange("p (k n) -> p k n", k=KC)[:, :, 0:rows_of(t_)],
                                      AX, ALU.max).then_inc(sem("n0_km"), 1)
            dve.wait_ge(*upto("n0_km", NT))
            dve.tensor_reduce(kmax1, kmax.rearrange("p t k -> p k t"), AX, ALU.max).then_inc(sem("kmax"), 1)
            dve.wait_ge(*upto("kmax_mm", 1))
            dve.tensor_scalar(negmax, bank[0][0:1, 0:C], -1.0, None, ALU.mult).then_inc(sem("negmax"), 1)
            if phase_end(dve):
                return

            def one_hots(v, wide, values, g):
                return dve.tensor_tensor(v, iota[:, 0:wide].unsqueeze(1).broadcast_to([P, GRP, wide]),
                                         span(values, g * GRP, GRP).unsqueeze(2).broadcast_to([P, GRP, wide]), ALU.is_equal)

            dve.memset(zerob, 0.0).then_inc(sem("zerob"), 1)
            for i in bodies(dve):
                for h in range(BPB):
                    g = i * BPB + h
                    if due(g - BPB + 1):
                        dve.wait_ge(*upto("ct_mm", g - BPB + 1))
                    one_hots(ohb[h], P, dl_t, g).then_inc(sem("ct_oh"), 1)
                    one_hots(tohb[h], R, typ_t, g).then_inc(sem("ct_oh"), 1)
            dve.wait_ge(*upto("ct_mm", NG))
            chain(dve.tensor_copy(cnt[:, :, :], bank[7][:, 0:NT * R].rearrange("p (w r) -> p w r", r=R)))
            chain(dve.tensor_reduce(rdeg[:, :], cnt[:, :, :], AX, ALU.add))
            chain(dve.tensor_scalar(rdeg[:, :], rdeg[:, :], 1.0, None, ALU.max))
            chain(dve.reciprocal(rdeg[:, :], rdeg[:, :]))
            chain(dve.tensor_scalar(cnt[:, :, :], cnt[:, :, :], 1.0, None, ALU.max))
            chain(dve.reciprocal(cnt[:, :, :], cnt[:, :, :]))
            rest = cnt[:, :, :]
            for k in range(3):
                part = rc3[:, :, R * k:R * k + R]
                chain(dve.tensor_copy(part, rest))
                if k < 2:
                    chain(dve.tensor_copy(rc_part, part))
                    chain(dve.tensor_tensor(rc_rest, rest, rc_part, ALU.subtract))
                    rest = rc_rest
            if phase_end(dve):
                return

            def add_sums(pre, g, ws):
                for j in range(GRP):
                    if j % 2 == 0:
                        dve.wait_ge(*upto(pre + "_sum_mm", 2 * g + 1 + j // 2))
                    if due(g * GRP + j):
                        dve.wait_ge(*upto(pre + "_add", g * GRP + j))
                    dve.tensor_tensor(at(acc, ws[j]), at(acc, ws[j]), bank[j // 2][:, C * (j % 2):C * (j % 2) + C],
                                      ALU.add).then_inc(sem(pre + "_add"), 1)

            def sum_windows(i):
                if isinstance(i, int) and i == 0:
                    return [None] * GRP + windows(dve, 0, BODY - GRP)
                return windows(dve, i * BODY - GRP, BODY)

            def targets(g, h):
                if due(g - BPB + 1):
                    dve.wait_ge(*upto("g0_oht_mm", g - BPB + 1))
                    dve.wait_ge(*upto("g0_woh", g - BPB + 1))
                one_hots(ohb[h], P, dl_t, g).then_inc(sem("g0_oh"), 1)
                one_hots(tohb[h], R, typ_t, g).then_inc(sem("g0_toh"), 1)

            def weights(g, h):
                b_ = h % 2
                dve.wait_ge(*upto("g0_toh", g + 1))
                dve.wait_ge(*upto("g0_look_mm", g + 1))
                if due(g - 1):
                    dve.wait_ge(*upto("g0_wgt", g - 1))
                dve.tensor_tensor(wsel[b_], tohb[h].unsqueeze(2).broadcast_to([P, GRP, 3, R]),
                                  bank[7][:, 0:GRP * 3 * R].rearrange("p (j k n) -> p j k n", j=GRP, k=3), ALU.mult).then_inc(sem("g0_wsel"), 1)
                dve.wait_ge(*upto("g0_wsel", g + 1))
                dve.tensor_reduce(wgt[b_], wsel[b_].rearrange("p j k n -> p j (k n)"), AX, ALU.add).then_inc(sem("g0_wgt"), 1)
                dve.wait_ge(*upto("g0_wgt", g + 1))
                if due(g - 1):
                    dve.wait_ge(*upto("g0_sum_mm", 2 * (g - 1)))
                dve.tensor_tensor(woh[b_], ohb[h], wgt[b_].unsqueeze(2).broadcast_to([P, GRP, P]), ALU.mult).then_inc(sem("g0_woh"), 1)

            for g in range(3):
                targets(g, g)
            weights(0, 0)
            def mixer_keys(m, h):
                if h == 1:
                    dve.wait_ge(*upto("m1_v_mm", m + 1))
                    if due(m):
                        dve.wait_ge(*upto("m1_ctx_mm", m))
                    dve.tensor_copy(m_v.rearrange("p (k n) -> p k n", k=KC)[:, :, 0:P],
                                    bank[5][:, 0:C].rearrange("p (k n) -> p k n", k=KC)).then_inc(sem("m1_v"), 1)

            def mixer_context(h):
                if h == 0:
                    dve.wait_ge(*upto("m1_ctx_mm", NT))
                    for k in range(KC):
                        chain(dve.reciprocal(cden[:, k:k + 1], bank[2 + k][:, P:P + 1]))
                        chain(dve.tensor_scalar(bdc[:, k, :], bank[2 + k][:, 0:P], cden[:, k:k + 1], None, ALU.mult))
                        dve.tensor_tensor(bdc[:, k, :], bdc[:, k, :], bd32[:, :], ALU.mult).then_inc(sem("m_bdc"), 1)
                if h == 2:
                    dve.wait_ge(*upto("m_qc_mm", 2))
                    for k in range(KC):
                        dve.tensor_copy(w_qc[:, k, :], bank[4 + k][:, 0:C]).then_inc(sem("m_qc"), 1)

            def mixer_queries(m, h):
                r = rows_of(m)
                if h == 0:
                    dve.wait_ge(*upto("m2_in", 48 * (m + 1)))
                    if due(m):
                        dve.wait_ge(*upto("m2_out", m))
                    dve.tensor_tensor(m_xb[0:r, :], m_x[0:r, :], bproj_b[0:r, :], ALU.add).then_inc(sem("m2_xb"), 1)
                if h == 1:
                    dve.wait_ge(*upto("m2_sig", m + 1))
                    if due(m):
                        dve.wait_ge(*upto("m2_prt_mm", m))
                    dve.tensor_tensor(m_pr, m_sig, bank[4][:, 0:C], ALU.mult).then_inc(sem("m2_pr"), 1)
                if h == 3:
                    dve.wait_ge(*upto("m2_f_mm", m + 1))
                    dve.wait_ge(*upto("m2_xb", m + 1))
                    if due(m):
                        dve.wait_ge(*upto("m2_st", 16 * m))
                    dve.tensor_tensor(m_out, m_xb, bank[3][:, 0:C], ALU.add).then_inc(sem("m2_out"), 1)

            for k in range(KC):
                c_ = (P + 1) * k + P
                dve.memset(m_v[:, c_:c_ + 1], 1.0).then_inc(sem("m1_ones"), 1)
            for i, m1, m2 in gather_bodies(dve):
                ws = sum_windows(i)
                for h in range(BPB):
                    g = i * BPB + h
                    if due(g):
                        add_sums("g0", g - 1, ws[GRP * h:GRP * h + GRP])
                    targets(g + 3, (h + 3) % BPB)
                    weights(g + 1, (h + 1) % BPB)
                    if m1 is not None:
                        mixer_keys(m1, h)
                    if between(i):
                        mixer_context(h)
                    if m2 is not None:
                        if h == 0:
                            dve.wait_ge(*upto("w_mix_in", 80))
                        mixer_queries(m2, h)
            add_sums("g0", NG - 1, windows(dve, T - GRP, GRP))
            dve.wait_ge(*upto("g0_idx", NG + BPB))
            chain(dve.tensor_scalar(idx_t[:, :], idx_t[:, :], 3, None, ALU.logical_shift_right))
            if phase_end(dve):
                return
            dve.wait_ge(*upto("w_ffn_in", 16 * 23))
            chain(dve.tensor_scalar(rtemp_r, temp_c, 0.1, 5.0, ALU.max, ALU.min))
            dve.reciprocal(rtemp_r, rtemp_r).then_inc(sem("rtemp"), 1)
            dve.wait_ge(*upto("rtemp", 1))
            dve.wait_ge(*upto("wl_mm", 4))
            chain(dve.tensor_copy(rtemp_b, bank[2][:, 0:8]))
            for k in range(KC):
                dve.tensor_tensor(heads(w_log[:, k, :]), heads(bank[k][:, :]), rtemp_b.unsqueeze(2).broadcast_to([P, 8, 64]), ALU.mult).then_inc(sem("w_log"), 1)
            chain(dve.tensor_tensor(b_log, bank[3][0:1, :], bslice8, ALU.add))
            dve.tensor_tensor(heads(b_log), heads(b_log), rtemp_r.unsqueeze(2).broadcast_to([1, 8, 64]), ALU.mult).then_inc(sem("w_log"), 1)
            for t, s, n in skewed(dve):
                if t[0] is not None:
                    t_, s_, n_ = t
                    dve.wait_ge(*upto(f"f1_in{s_}", 16 * (n_ + 1)))
                    if due(16 * n_):
                        dve.wait_ge(*upto(f"f1_x1_out{s_}", 16 * n_))
                    dve.scalar_tensor_tensor(a_x1[s_], at(acc, t_), 0.0, a_xin[s_], ALU.max, ALU.add).then_inc(sem("f1_x1"), 1)
                    norm("f1", a_x1[s_], a_xn[s_][:, 0:C], a_stats[s_], a_mv[s_], a_veps[s_], a_rstd[s_], t_,
                         ("f1_x1", t_ + 1), [("f1_t", t_ - 1), ("f1_u_mm", t_ - 1)])
                if s[0] is not None:
                    t_, s_, n_ = s
                    lg = bank[1 + s_]
                    dve.wait_ge(*upto("f1_l_mm", t_ + 1))
                    dve.tensor_reduce(a_max[s_], heads(lg[:, :]), AX, ALU.max).then_inc(sem("f1_mx"), 1)
                    dve.wait_ge(*upto("f1_mx", t_ + 1))
                    if due(t_ - 1):
                        dve.wait_ge(*upto("f1_ex", t_ - 1))
                    dve.tensor_tensor(heads(a_lg[s_]), heads(lg[:, :]), a_max[s_].unsqueeze(2).broadcast_to([P, 8, 64]), ALU.subtract).then_inc(sem("f1_lg"), 1)
                    dve.wait_ge(*upto("f1_ex", t_ + 1))
                    dve.tensor_reduce(a_sum[s_], heads(a_ex[s_]), AX, ALU.add).then_inc(sem("f1_sm"), 1)
                    dve.wait_ge(*upto("f1_sm", t_ + 1))
                    dve.reciprocal(a_rsum[s_], a_sum[s_]).then_inc(sem("f1_rs"), 1)
                    dve.wait_ge(*upto("f1_rs", t_ + 1))
                    if due(t_ - 1):
                        dve.wait_ge(*upto("f1_swt_mm", t_ - 1))
                    if due(t_ - 1):
                        dve.wait_ge(*upto("f1_u_mm", t_ - 1))
                    dve.tensor_tensor(heads(a_sw[s_]), heads(a_ex[s_]), a_rsum[s_].unsqueeze(2).broadcast_to([P, 8, 64]), ALU.mult).then_inc(sem("f1_sw"), 1)
            four = range(4)
            blk = lambda v, j: v[:, P * j:P * j + P]
            dve.wait_ge(*upto("f1_u_mm", NT))
            for j in four:
                dve.tensor_copy(f_u[:, j, :], bank[4 + j][:, 0:257]).then_inc(sem("fs_u"), 1)
            dve.wait_ge(*upto("fs_u", 4))
            chain(dve.tensor_scalar(f_den, f_u[:, :, 256], EPS, None, ALU.add))
            chain(dve.reciprocal(f_rden, f_den))
            dve.wait_ge(*upto("fs_ut_mm", 2))
            for k in range(KC):
                dve.tensor_copy(f_ut[:, k, :], bank[k][:, :]).then_inc(sem("fs_ut"), 1)
            dve.wait_ge(*upto("fs_tok_mm", 1))
            for j in four:
                chain(dve.scalar_tensor_tensor(blk(f_tok, j), blk(bfx_b, j), f_u[:, j, 256:257], blk(bank[2], j), ALU.mult, ALU.add))
                dve.scalar_tensor_tensor(blk(f_tok2, j), blk(f_tok, j), f_rden[:, j:j + 1], bd64[:, :], ALU.mult, ALU.mult).then_inc(sem("fs_tok"), 1)
            dve.wait_ge(*upto("fs_tokt_mm", 1))
            dve.tensor_copy(f_tokt, bank[0][:, :]).then_inc(sem("fs_tokt"), 1)
            dve.wait_ge(*upto("fs_qkv_mm", 3))
            for v, b_ in ((f_qt, 1), (f_kt, 2), (f_v, 4)):
                dve.tensor_copy(v, bank[b_][:, :]).then_inc(sem("fs_qkv"), 1)
            dve.wait_ge(*upto("fs_s_mm", 1))
            for j in four:
                chain(dve.scalar_tensor_tensor(blk(f_s, j), blk(bank[5], j), 64 ** -0.5, off64[:, :], ALU.mult, ALU.add))
                dve.tensor_reduce(f_max[:, j:j + 1], blk(f_s, j), AX, ALU.max, negate=True).then_inc(sem("fs_max"), 1)
            dve.wait_ge(*upto("fs_exp", 4))
            chain(dve.reciprocal(f_rsum, f_sum))
            for j in four:
                dve.tensor_scalar(blk(f_s, j), blk(f_s2, j), f_rsum[:, j:j + 1], None, ALU.mult).then_inc(sem("fs_a"), 1)
            dve.wait_ge(*upto("fs_at_mm", 1))
            dve.tensor_copy(f_at, bank[0][:, :]).then_inc(sem("fs_at"), 1)
            dve.wait_ge(*upto("fs_ost_mm", 1))
            dve.tensor_copy(f_ost, bank[1][:, :]).then_inc(sem("fs_ost"), 1)
            dve.wait_ge(*upto("fs_m_mm", 4))
            for j in four:
                dve.tensor_copy(f_m[:, j, :], bank[4 + j][:, 0:C]).then_inc(sem("fs_m"), 1)
            dve.wait_ge(*upto("fs_m", 4))
            if phase_end(dve):
                return
            for (t, s, n), (t_, s_, n_), _ in staged(dve):
                if t is not None:
                    dve.wait_ge(*upto(f"f2_in{s}", 32 * (n + 1)))
                    dve.wait_ge(*upto("f2_o_mm", t + 1))
                    if due(16 * n):
                        dve.wait_ge(*upto(f"f2_x2_out{s}", 16 * n))
                        dve.wait_ge(*upto("f2_xn", t - 1))
                    dve.tensor_tensor(k_x2[s], k_x1[s], bank[s][:, 0:C], ALU.add).then_inc(sem("f2_x2"), 1)
                    variance("f2", k_x2[s], a_stats[s], a_mv[s], a_veps[s], t, ("f2_x2", t + 1))
                if t_ is not None:
                    dve.wait_ge(*upto("f2_rstd", t_ + 1))
                    if due(t_ - 1):
                        dve.wait_ge(*upto("f2_t", t_ - 1))
                        dve.wait_ge(*upto(f"f2_xn_out{s_}", 16 * n_))
                    dve.tensor_scalar(a_xn[s_][:, 0:C], k_x2[s_], a_mv[s_][:, 0:1], a_rstd[s_], ALU.subtract, ALU.mult).then_inc(sem("f2_xn"), 1)
            dve.memset(acc[:, :, :], 0.0)
            if phase_end(dve):
                return
            def targets1(g, h):
                if due(g - 1):
                    dve.wait_ge(*upto("g1_sum_mm", 2 * (g - 1)))
                one_hots(oh[h % 2], P, dl_t, g).then_inc(sem("g1_oh"), 1)

            targets1(0, 0)
            dve.wait_ge(*upto("w_kv_in", 16))
            for k in range(KC):
                chain(dve.tensor_reduce(kv_mean[:, k, :], heads(w_kv1[:, k, :], 16), AX, ALU.add))
                chain(dve.tensor_scalar(kv_mean[:, k, :], kv_mean[:, k, :], 1.0 / 64, None, ALU.mult))
                dve.tensor_tensor(heads(w_kv1[:, k, :], 16), heads(w_kv1[:, k, :], 16),
                                  kv_mean[:, k, :].unsqueeze(2).broadcast_to([P, 16, 64]), ALU.subtract).then_inc(sem("w_kv"), 1)

            def keys_values(m, h):
                if h == 1:
                    dve.wait_ge(*upto("kv_sqk", m + 1))
                    dve.wait_ge(*upto("kv_sqv", m + 1))
                    if due(m):
                        dve.wait_ge(*upto("kv_v1", m))
                    dve.tensor_reduce(k_ss, heads(k_sq, 16), AX, ALU.add).then_inc(sem("kv_ss"), 1)
                    dve.wait_ge(*upto("kv_ss", m + 1))
                    if due(m):
                        dve.wait_ge(*upto("kv_pv", m))
                    dve.tensor_scalar(k_v1, k_ss, 1.0 / 64, EPS, ALU.mult, ALU.add).then_inc(sem("kv_v1"), 1)
                    dve.wait_ge(*upto("kv_v1", m + 1))
                    if due(m):
                        dve.wait_ge(*upto("kv_n2", m))
                        dve.wait_ge(*upto("kv_root", m))
                    dve.tensor_tensor(k_pv, k_v1[:, 0:8], k_v1[:, 8:16], ALU.mult).then_inc(sem("kv_pv"), 1)
                if h == 2:
                    dve.wait_ge(*upto("kv_root", m + 1))
                    if due(m):
                        dve.wait_ge(*upto("kv_krs", m))
                    dve.reciprocal(k_inv, k_root).then_inc(sem("kv_inv"), 1)
                    dve.wait_ge(*upto("kv_inv", m + 1))
                    dve.tensor_tensor(k_n[0], k_inv, k_inv, ALU.mult).then_inc(sem("kv_n1"), 1)
                    dve.wait_ge(*upto("kv_n1", m + 1))
                    dve.tensor_tensor(k_n[1], k_n[0], k_pv, ALU.mult).then_inc(sem("kv_n2"), 1)
                    dve.wait_ge(*upto("kv_n2", m + 1))
                    dve.tensor_scalar(k_n[2], k_n[1], -0.5, 1.5, ALU.mult, ALU.add).then_inc(sem("kv_n3"), 1)
                    dve.wait_ge(*upto("kv_n3", m + 1))
                    if due(m):
                        dve.wait_ge(*upto("kv_kn", m))
                    dve.tensor_tensor(k_rs, k_inv, k_n[2], ALU.mult).then_inc(sem("kv_krs"), 1)
                    dve.wait_ge(*upto("kv_krs", m + 1))
                    if due(m):
                        dve.wait_ge(*upto("kv_dots_mm", m))
                    dve.tensor_tensor(heads(k_kn), heads(bank[2][:, :]), k_rs.unsqueeze(2).broadcast_to([P, 8, 64]), ALU.mult).then_inc(sem("kv_kn"), 1)

            for i, m1, m2 in gather_bodies(dve):
                ws = sum_windows(i)
                for h in range(BPB):
                    g = i * BPB + h
                    if due(g):
                        add_sums("g1", g - 1, ws[GRP * h:GRP * h + GRP])
                    targets1(g + 1, h + 1)
                    if m1 is not None:
                        keys_values(m1, h)
            add_sums("g1", NG - 1, windows(dve, T - GRP, GRP))
            dve.wait_ge(*upto("w_l1_in", 16 * 7))
            dve.tensor_tensor(b_comb, b_self, b_out1, ALU.add).then_inc(sem("b_comb"), 1)
            for j in four:
                chain(dve.tensor_tensor(blk(d_bd, j), bank[4 + j][:, 0:P], bd64[:, :], ALU.mult))
            dve.tensor_scalar(d_bd, d_bd, 1.0 / N, None, ALU.mult).then_inc(sem("d_bd"), 1)
            dve.wait_ge(*upto("d_t1_mm", 4))
            for j in four:
                dve.tensor_copy(d_t1[:, j, :], bank[j][:, 0:C]).then_inc(sem("d_t1"), 1)
            dve.wait_ge(*upto("d_f_mm", 2))
            for k in range(KC):
                dve.tensor_tensor(w_comb[:, k, :], bank[4 + k][:, 0:C], w_self[:, k, :], ALU.add).then_inc(sem("w_comb"), 1)
            if phase_end(dve):
                return
            for t, s, n in skewed(dve):
                if t[0] is not None:
                    t_, s_, n_ = t
                    if due(t_ - 1):
                        dve.wait_ge(*upto("c_hn_t", t_ - 1))
                    dve.tensor_scalar(c_hn[s_], at(acc, t_), col(rdeg, t_), None, ALU.mult).then_inc(sem("c_hn"), 1)
                if s[0] is not None:
                    t_, s_, n_ = s
                    dve.wait_ge(*upto(f"c_in{s_}", 32 * (n_ + 1)))
                    dve.wait_ge(*upto("c_x_mm", t_ + 1))
                    dve.tensor_tensor(c_x3[s_], c_x2[s_], bank[1][:, 0:C], ALU.add).then_inc(sem("c_x3"), 1)
                    norm("c", c_x3[s_], c_xn[s_], c_stats[s_], c_mv[s_], c_veps[s_], c_rstd[s_], t_,
                         ("c_x3", t_ + 1), [("c_x4_t", t_ - 1)])
                    dve.wait_ge(*upto("c_xn", t_ + 1))
                    if due(16 * n_):
                        dve.wait_ge(*upto(f"c_x34_out{s_}", 16 * n_))
                    dve.tensor_tensor(c_x34[s_], c_x3[s_], c_xn[s_], ALU.add).then_inc(sem("c_x34"), 1)
                    dve.wait_ge(*upto("c_r_mm", t_ + 1))
                    dve.tensor_copy(at(logits, t_), bank[3][:, 0:8]).then_inc(sem("c_r"), 1)
            dve.wait_ge(*upto("c_r", NT))
            big = [P, NT, 8]
            m_, s_, i_ = rb[0], rb[1], rb[2]
            iota8 = iota[:, 0:8].unsqueeze(1).broadcast_to(big)
            each = lambda v: v.unsqueeze(2).broadcast_to(big)
            chain(dve.tensor_reduce(m_, logits, AX, ALU.max))
            dve.tensor_tensor(ra[0], logits, each(m_), ALU.subtract).then_inc(sem("r_exp_in"), 1)
            dve.wait_ge(*upto("r_exp", 1))
            chain(dve.tensor_reduce(s_, ra[1], AX, ALU.add))
            chain(dve.reciprocal(s_, s_))
            chain(dve.tensor_tensor(ra[0], ra[1], each(s_), ALU.mult))
            chain(dve.tensor_copy(ra[1], ra[0]))
            for pick in range(2):
                chain(dve.tensor_reduce(rb[3 + pick], ra[1], AX, ALU.max))
                chain(dve.tensor_tensor(ra[2], ra[1], each(rb[3 + pick]), ALU.is_ge))
                chain(dve.tensor_scalar(ra[3], iota8, -1.0, 8.0, ALU.mult, ALU.add))
                chain(dve.tensor_tensor(ra[2], ra[2], ra[3], ALU.mult))
                chain(dve.tensor_reduce(i_, ra[2], AX, ALU.max))
                chain(dve.tensor_tensor(ra[2], ra[3], each(i_), ALU.is_equal))
                if pick == 0:
                    chain(dve.tensor_copy(comb, ra[2]))
                    chain(dve.scalar_tensor_tensor(ra[1], ra[2], -2.0, ra[1], ALU.mult, ALU.add))
                else:
                    chain(dve.tensor_tensor(comb, comb, ra[2], ALU.add))
            chain(dve.tensor_tensor(rb[5], rb[3], rb[4], ALU.add))
            chain(dve.tensor_scalar(rb[5], rb[5], 1e-12, None, ALU.max))
            chain(dve.reciprocal(rb[5], rb[5]))
            chain(dve.tensor_tensor(comb, comb, ra[0], ALU.mult))
            chain(dve.tensor_tensor(comb, comb, each(rb[5]), ALU.mult))
            if phase_end(dve):
                return
            for g, s, n, m in expert_groups(dve):
                cf = comb.rearrange("p t e -> p (t e)")
                if due(g - 1):
                    dve.wait_ge(*upto("s_ct_mm", g - 1))
                dve.tensor_copy(s_cg[s][:, 0:8 * m], span(cf, 32 * g if isinstance(g, int) else g * 32, 8 * m)).then_inc(sem("s_cg"), 1)
                dve.wait_ge(*upto(f"s_in{s}", 32 * (n + 1)))
                dve.wait_ge(*upto("s_cb_mm", g + 1))
                for j in range(m):
                    dve.tensor_tensor(s_o[s][:, j, :], s_o[s][:, j, :], bank[4 + j // 2][:, C * (j % 2):C * (j % 2) + C], ALU.add).then_inc(sem("s_base"), 1)
                dve.wait_ge(*upto("s_base", 4 * g + m))
                for e in range(8):
                    dve.wait_ge(*upto("s_y_mm", 8 * g + e + 1))
                    for j in range(m):
                        if due(32 * g + m * e + j - m + 1 if e else 0):
                            dve.wait_ge(*upto("s_acc", 32 * g + m * e + j - m + 1 if e else 0))
                        c_ = s_cg[s][:, 8 * j + e:8 * j + e + 1]
                        dve.scalar_tensor_tensor(s_o[s][:, j, :], bank[4 + j // 2][:, C * (j % 2):C * (j % 2) + C], c_,
                                                 s_o[s][:, j, :], ALU.mult, ALU.add).then_inc(sem("s_acc"), 1)
            phase_end(dve)

        @block.tensor
        def _(pe):
            mm = pe.matmul

            def transposes(dst_, src_, n_=KC):
                for k in range(n_):
                    last = pe.transpose(dst_[:, P * k:P * k + P], src_[:, P * k:P * k + P], ident[:, :])
                return last

            pe.wait_ge(*upto("q_viol", 1))
            for k, v in enumerate((e_win[:, 0:1], e_win[:, ECOLS - 1:ECOLS], q_viol)):
                last = mm(bank[5][0:1, EROWS * k:EROWS * (k + 1)], v, ident[0:EROWS, 0:EROWS], start=True, stop=True)
            last.then_inc(sem("q_rows_mm"), 1)
            pe.wait_ge(*upto("q_flag", 1))
            unsorted = pe.value_load(q_flag, min_val=0, max_val=1)
            with pe.If(unsorted > 0):
                pe.wait_ge(*upto("q_start", 3))
                for w in target_windows(pe):
                    pe.wait_ge(*upto("q_pre", w + 1))
                    if due(w):
                        pe.wait_ge(*upto("q_base", w))
                    total = q_pre[:, ECOLS - 1:ECOLS]
                    mm(bank[5][0:EROWS, 0:1], q_tri, total, start=True, stop=True)
                    mm(bank[5][0:EROWS, 1:2], ones[0:EROWS, 0:EROWS], total, start=True, stop=True).then_inc(sem("q_offs_mm"), 1)
            pe.wait_ge(*upto("rows_ready", 1))
            for b_ in range(TB):
                cols = slice(P * b_, P * b_ + P)
                if due(3 * (b_ - 1)):
                    pe.wait_ge(*upto("tables", 3 * (b_ - 1)))
                mm(bank[b_ % 2][:, 0:P], r_dl[:, cols], ident[:, :], start=True, stop=True).then_inc(sem("tables_mm"), 1)
                mm(bank[b_ % 2][:, P:2 * P], r_idx[:, cols], ident[:, :], start=True, stop=True).then_inc(sem("tables_mm"), 1)
                mm(bank[b_ % 2][0:1, 2 * P:3 * P], r_w0[:, b_:b_ + 1], ident[:, :], start=True, stop=True).then_inc(sem("tables_mm"), 1)
            for v, b2_ in ((r_dst, 2), (r_idx, 3)):
                for b_ in range(TB):
                    last = mm(bank[b2_][:, 0:NT - 1], v[:, P * b_:P * b_ + P], r_sel[:, (NT - 1) * b_:(NT - 1) * (b_ + 1)],
                              start=b_ == 0, stop=b_ == TB - 1)
                last.then_inc(sem("extra_mm"), 1)
            if phase_end(pe):
                return
            pe.wait_ge(*upto("gate_w", 4))
            for k in range(KC):
                last = mm(bank[7][:, 0:64], ones[:, :], wg1[:, k, :], start=k == 0, stop=k == KC - 1)
            last.then_inc(sem("gate_w_mm"), 1)
            for k in range(KC):
                last = mm(bank[6][:, 0:64], lnb_b[:, k, :], wg1_raw[:, k, :], start=k == 0, stop=k == KC - 1)
            last.then_inc(sem("gate_w_mm"), 1)
            pe.wait_ge(*upto("gate_b", 1))
            for t, s, n in skewed(pe):
                if t[0] is not None:
                    t_, s_, n_ = t
                    pe.wait_ge(*upto("n0_xn", t_ + 1))
                    if due(t_):
                        pe.wait_ge(*upto("n0_xnt", t_))
                    transposes(bank[4], xn[s_]).then_inc(sem("n0_t"), 1)
                if s[0] is not None:
                    t_, s_, n_ = s
                    pe.wait_ge(*upto("n0_xnt", t_ + 1))
                    for b_ in range(4):
                        if b_ % 2:
                            if due(2 * t_ - 1 + b_ // 2):
                                pe.wait_ge(*upto("n0_y_dve", 2 * t_ - 1 + b_ // 2))
                        else:
                            if due(2 * t_ - 1 + b_ // 2):
                                pe.wait_ge(*upto("n0_y_act", 2 * t_ - 1 + b_ // 2))
                        for k in range(KC):
                            last = mm(bank[b_][:, :], xnt[s_][:, P * k:P * k + P], w_all[:, k, 512 * b_:512 * b_ + 512], start=k == 0, stop=k == KC - 1)
                        last.then_inc(sem(f"n0_y_mm{b_}"), 1)
                    if due(t_):
                        pe.wait_ge(*upto("n0_ga", t_))
                    for k in range(KC):
                        mm(bank[5][:, 0:C], xnt[s_][:, P * k:P * k + P], w_root[:, k, :], start=k == 0, stop=k == KC - 1)
                    for k in range(KC):
                        last = mm(bank[5][:, C:C + 64], xnt[s_][:, P * k:P * k + P], wg1[:, k, :], start=k == 0, stop=k == KC - 1)
                    last.then_inc(sem("n0_root_mm"), 1)
                    if due(t_):
                        pe.wait_ge(*upto("n0_km", t_))
                    for m in range(KC):
                        for k in range(KC):
                            last = mm(bank[6][:, P * m:P * m + P], w_k0[:, k, P * m:P * m + P], xnt[s_][:, P * k:P * k + P], start=k == 0, stop=k == KC - 1)
                    last.then_inc(sem("n0_km_mm"), 1)
                    pe.wait_ge(*upto("n0_hg", t_ + 1))
                    if due(t_):
                        pe.wait_ge(*upto("n0_hgt", t_))
                    alone(pe)
                    pe.transpose(bank[7][0:64, 0:P], hg[s_], ident[:, :]).then_inc(sem("n0_hg_t"), 1)
            pe.wait_ge(*upto("kmax", 1))
            pe.wait_ge(*upto("n0_y_act", 2 * NT))
            for k in range(KC):
                last = mm(bank[0][0:1, P * k:P * k + P], kmax1[:, k:k + 1], ident[:, :], start=True, stop=True)
            last.then_inc(sem("kmax_mm"), 1)
            if phase_end(pe):
                return
            pe.wait_ge(*upto("zerob", 1))
            mm(bank[7][:, :], zerob[:, 0:P], zerob, start=True, stop=False, skip_group_check=True)
            for i in bodies(pe):
                ws = windows(pe, i * BODY, BODY)
                for h in range(BPB):
                    g = i * BPB + h
                    pe.wait_ge(*upto("ct_oh", 2 * g + 2))
                    for j in range(GRP):
                        last = mm(bank[7][:, bass.ds(ws[GRP * h + j] * R, R)], ohb[h][:, j, :], tohb[h][:, j, :],
                                  start=False, stop=False, skip_group_check=True)
                    last.then_inc(sem("ct_mm"), 1)
            if phase_end(pe):
                return

            def sum_rows(pre, g, again, lhs, h):
                pe.wait_ge(*upto(f"{pre}_rows{h}", 16 * GRP * (again + 1)))
                for j in range(GRP):
                    if j % 2 == 0 and due(g):
                        pe.wait_ge(*upto(pre + "_add", GRP * (g - 1) + j + 2))
                    last = mm(bank[j // 2][:, C * (j % 2):C * (j % 2) + C], lhs[:, j, :], ring[GRP * h + j], start=True, stop=True)
                    if j % 2:
                        last.then_inc(sem(pre + "_sum_mm"), 1)

            def turn(g, h):
                pe.wait_ge(*upto("g0_oh", g + 1))
                if due(g):
                    pe.wait_ge(*upto("g0_oht", g))
                for j in range(GRP):
                    last = mm(bank[6][:, P * j:P * j + P], ohb[h][:, j, :], identb[:, :], start=True, stop=True)
                last.then_inc(sem("g0_oht_mm"), 1)

            def look(g, h, ws):
                pe.wait_ge(*upto("g0_oht", g + 1))
                if due(g):
                    pe.wait_ge(*upto("g0_wsel", g))
                for j in range(GRP):
                    last = mm(bank[7][:, 3 * R * j:3 * R * (j + 1)], oht[h % 2][:, P * j:P * j + P], at(rc3, ws[j]), start=True, stop=True)
                last.then_inc(sem("g0_look_mm"), 1)

            ws = windows(pe, 0, 2 * GRP)
            for g in range(2):
                turn(g, g)
                look(g, g, ws[GRP * g:GRP * g + GRP])
            def mixer_keys(m, h):
                if h == 0:
                    pe.wait_ge(*upto("m1_in", 16 * (m + 1)))
                    if due(m):
                        pe.wait_ge(*upto("m1_ek", m))
                    mm(bank[4][:, 0:C], ones[0:1, :], negmax, start=True, stop=False)
                    for k in range(KC):
                        last = mm(bank[4][:, 0:C], m_xnt[:, P * k:P * k + P], w_k0[:, k, :], start=False, stop=k == KC - 1)
                    last.then_inc(sem("m1_k_mm"), 1)
                    if due(m):
                        pe.wait_ge(*upto("m1_v", m))
                    for k in range(KC):
                        last = mm(bank[5][:, 0:C], m_xnt[:, P * k:P * k + P], w_v0[:, k, :], start=k == 0, stop=k == KC - 1)
                    last.then_inc(sem("m1_v_mm"), 1)
                if h == 2:
                    r = rows_of(m)
                    pe.wait_ge(*upto("m1_ek", m + 1))
                    pe.wait_ge(*upto("m1_v", m + 1))
                    pe.wait_ge(*upto("m1_ones", KC))
                    for k in range(KC):
                        last = mm(bank[2 + k][:, 0:P + 1], m_ek[0:r, P * k:P * k + P], m_v[0:r, (P + 1) * k:(P + 1) * (k + 1)],
                                  start=isinstance(m, int) and m == 0, stop=is_last(m), skip_group_check=True)
                    last.then_inc(sem("m1_ctx_mm"), 1)

            def mixer_context(h):
                if h == 1:
                    pe.wait_ge(*upto("w_mix_in", 80))
                    pe.wait_ge(*upto("m_bdc", KC))
                    pe.wait_ge(*upto("m1_v", NT))
                    for i_ in range(KC):
                        for j in range(KC):
                            last = mm(bank[4 + i_][:, P * j:P * j + P], w_qt[:, j, P * i_:P * i_ + P], bdc[:, j, :], start=True, stop=True)
                        last.then_inc(sem("m_qc_mm"), 1)

            def mixer_queries(m, h):
                if h == 0:
                    pe.wait_ge(*upto("m2_in", 48 * (m + 1)))
                    if not due(m):
                        pe.wait_ge(*upto("m_qc", KC))
                    if due(m):
                        pe.wait_ge(*upto("m2_pr", m))
                        pe.wait_ge(*upto("m2_sig", m))
                    for k in range(KC):
                        mm(bank[4][:, 0:C], m_xnt[:, P * k:P * k + P], w_qc[:, k, :], start=k == 0, stop=k == KC - 1)
                    mm(bank[5][:, 0:C], ones[0:1, :], bg2, start=True, stop=False)
                    mm(bank[5][:, 0:C], m_hgt, wg2, start=False, stop=True).then_inc(sem("m2_g_mm"), 1)
                if h == 2:
                    pe.wait_ge(*upto("m2_pr", m + 1))
                    if due(m):
                        pe.wait_ge(*upto("m2_prt", m))
                    transposes(bank[2], m_pr).then_inc(sem("m2_prt_mm"), 1)
                if h == 3:
                    pe.wait_ge(*upto("m2_prt", m + 1))
                    if due(m):
                        pe.wait_ge(*upto("m2_out", m))
                    for k in range(KC):
                        last = mm(bank[3][:, 0:C], m_prt[:, P * k:P * k + P], w_proj[:, k, :], start=k == 0, stop=k == KC - 1)
                    last.then_inc(sem("m2_f_mm"), 1)

            for i, m1, m2 in gather_bodies(pe):
                ws = windows(pe, i * BODY + 2 * GRP, BODY)
                for h in range(BPB):
                    g = i * BPB + h
                    turn(g + 2, (h + 2) % BPB)
                    pe.wait_ge(*upto("g0_woh", g + 1))
                    sum_rows("g0", g, i, woh[h % 2], h)
                    look(g + 2, h, ws[GRP * h:GRP * h + GRP])
                    if m1 is not None:
                        mixer_keys(m1, h)
                    if between(i):
                        mixer_context(h)
                    if m2 is not None:
                        mixer_queries(m2, h)
            if phase_end(pe):
                return
            pe.wait_ge(*upto("w_ffn_in", 16 * 23))
            pe.wait_ge(*upto("rtemp", 1))
            for i in range(KC):
                for j in range(4):
                    last = mm(bank[i][:, P * j:P * j + P], wx_t[:, j, P * i:P * i + P], wsl_bd, start=True, stop=True)
                last.then_inc(sem("wl_mm"), 1)
            mm(bank[2][:, 0:8], ones[0:1, :], rtemp_r, start=True, stop=True).then_inc(sem("wl_mm"), 1)
            for j in range(4):
                last = mm(bank[3][0:1, P * j:P * j + P], bx_c[:, j:j + 1], wsl_bd, start=True, stop=True)
            last.then_inc(sem("wl_mm"), 1)
            pe.wait_ge(*upto("w_log", 3))
            pe.wait_ge(*upto("a_ones", 2))
            for t, s, n in skewed(pe):
                if t[0] is not None:
                    t_, s_, n_ = t
                    pe.wait_ge(*upto("f1_xn", t_ + 1))
                    if due(t_):
                        pe.wait_ge(*upto("f1_xnt", t_))
                    transposes(bank[0], a_xn[s_]).then_inc(sem("f1_t"), 1)
                if s[0] is not None:
                    t_, s_, n_ = s
                    r = rows_of(t_)
                    pe.wait_ge(*upto("f1_xnt", t_ + 1))
                    if due(t_ - 1):
                        pe.wait_ge(*upto("f1_lg", t_ - 1))
                    mm(bank[1 + s_][:, :], ones[0:1, :], b_log, start=True, stop=False)
                    for k in range(KC):
                        last = mm(bank[1 + s_][:, :], a_xnt[s_][:, P * k:P * k + P], w_log[:, k, :], start=False, stop=k == KC - 1)
                    last.then_inc(sem("f1_l_mm"), 1)
                    pe.wait_ge(*upto("f1_sw", t_ + 1))
                    if due(t_):
                        pe.wait_ge(*upto("f1_swt", t_))
                    for j in range(4):
                        last = pe.transpose(bank[3][:, P * j:P * j + P], a_sw[s_][:, P * j:P * j + P], ident[:, :])
                    last.then_inc(sem("f1_swt_mm"), 1)
                    for j in range(4):
                        last = mm(bank[4 + j][:, 0:257], a_sw[s_][0:r, P * j:P * j + P], a_xn[s_][0:r, :],
                                  start=isinstance(t_, int) and t_ == 0, stop=is_last(t_), skip_group_check=True)
                    last.then_inc(sem("f1_u_mm"), 1)
            blk = lambda v, j: v[:, P * j:P * j + P]
            pe.wait_ge(*upto("fs_u", 4))
            for k in range(KC):
                for j in range(4):
                    last = pe.transpose(bank[k][:, P * j:P * j + P], f_u[:, j, P * k:P * k + P], ident[:, :])
                last.then_inc(sem("fs_ut_mm"), 1)
            pe.wait_ge(*upto("fs_ut", 2))
            for j in range(4):
                for k in range(KC):
                    last = mm(blk(bank[2], j), f_ut[:, k, P * j:P * j + P], w_fx[:, k, P * j:P * j + P], start=k == 0, stop=k == KC - 1)
            last.then_inc(sem("fs_tok_mm"), 1)
            pe.wait_ge(*upto("fs_tok", 4))
            for j in range(4):
                last = pe.transpose(blk(bank[0], j), blk(f_tok2, j), ident[:, :])
            last.then_inc(sem("fs_tokt_mm"), 1)
            pe.wait_ge(*upto("fs_tokt", 1))
            for w_, b_ in ((wq_bd, 1), (wk_bd, 2)):
                last = mm(bank[b_][:, :], w_, f_tokt, start=True, stop=True)
                last.then_inc(sem("fs_qkv_mm"), 1)
            for j in range(4):
                last = mm(blk(bank[4], j), blk(f_tokt, j), wv_bd, start=True, stop=True)
            last.then_inc(sem("fs_qkv_mm"), 1)
            pe.wait_ge(*upto("fs_qkv", 3))
            for j in range(4):
                last = mm(blk(bank[5], j), blk(f_qt, j), blk(f_kt, j), start=True, stop=True)
            last.then_inc(sem("fs_s_mm"), 1)
            pe.wait_ge(*upto("fs_a", 4))
            for j in range(4):
                last = pe.transpose(blk(bank[0], j), blk(f_s, j), ident[:, :])
            last.then_inc(sem("fs_at_mm"), 1)
            pe.wait_ge(*upto("fs_at", 1))
            for j in range(4):
                last = mm(blk(bank[1], j), blk(f_v, j), blk(f_at, j), start=True, stop=True)
            last.then_inc(sem("fs_ost_mm"), 1)
            pe.wait_ge(*upto("fs_ost", 1))
            for j in range(4):
                mm(bank[4 + j][:, 0:C], blk(f_ost, j), w_out[:, j, :], start=True, stop=True).then_inc(sem("fs_m_mm"), 1)
            if phase_end(pe):
                return
            for (t, s, n), (t_, s_, n_), _ in staged(pe):
                if t is not None:
                    pe.wait_ge(*upto(f"f2_in{s}", 32 * (n + 1)))
                    if due(t - 1):
                        pe.wait_ge(*upto("f2_x2", t - 1))
                    mm(bank[s][:, 0:C], ones[0:1, :], bout_r, start=True, stop=False)
                    for j in range(4):
                        last = mm(bank[s][:, 0:C], k_swt[s][:, P * j:P * j + P], f_m[:, j, :], start=False, stop=j == 3)
                    last.then_inc(sem("f2_o_mm"), 1)
                if t_ is not None:
                    pe.wait_ge(*upto("f2_xn", t_ + 1))
                    if due(t_):
                        pe.wait_ge(*upto("f2_xnt", t_))
                    transposes(bank[2], a_xn[s_]).then_inc(sem("f2_t"), 1)
            if phase_end(pe):
                return
            def keys_values(m, h):
                if h == 0:
                    pe.wait_ge(*upto("kv_in", 16 * (m + 1)))
                    if not due(m):
                        pe.wait_ge(*upto("w_kv", KC))
                    if due(m):
                        pe.wait_ge(*upto("kv_kn", m))
                    for k in range(KC):
                        last = mm(bank[2][:, :], k_xnt[:, P * k:P * k + P], w_kv1[:, k, 0:512], start=k == 0, stop=k == KC - 1)
                    last.then_inc(sem("kv_k_mm"), 1)
                    if due(m):
                        pe.wait_ge(*upto("kv_v", m))
                    for k in range(KC):
                        last = mm(bank[3][:, :], k_xnt[:, P * k:P * k + P], w_kv1[:, k, 512:1024], start=k == 0, stop=k == KC - 1)
                    last.then_inc(sem("kv_v_mm"), 1)
                if h == 3:
                    r = rows_of(m)
                    pe.wait_ge(*upto("kv_kn", m + 1))
                    pe.wait_ge(*upto("kv_v", m + 1))
                    for j in range(4):
                        last = mm(bank[4 + j][:, 0:P], k_v[0:r, P * j:P * j + P], k_kn[0:r, P * j:P * j + P],
                                  start=isinstance(m, int) and m == 0, stop=is_last(m), skip_group_check=True)
                    last.then_inc(sem("kv_dots_mm"), 1)

            for i, m1, m2 in gather_bodies(pe):
                for h in range(BPB):
                    g = i * BPB + h
                    pe.wait_ge(*upto("g1_oh", g + 1))
                    sum_rows("g1", g, i, oh[h % 2], h)
                    if m1 is not None:
                        keys_values(m1, h)
            pe.wait_ge(*upto("g1_add", T))
            pe.wait_ge(*upto("d_bd", 1))
            for j in range(4):
                mm(bank[j][:, 0:C], blk(d_bd, j), w_o1t[:, j, :], start=True, stop=True).then_inc(sem("d_t1_mm"), 1)
            pe.wait_ge(*upto("d_t1", 4))
            for k in range(KC):
                for j in range(4):
                    last = mm(bank[4 + k][:, 0:C], w_q1[:, j, P * k:P * k + P], d_t1[:, j, :], start=j == 0, stop=j == 3)
                last.then_inc(sem("d_f_mm"), 1)
            if phase_end(pe):
                return
            for t, s, n in skewed(pe):
                if t[0] is not None:
                    t_, s_, n_ = t
                    pe.wait_ge(*upto("c_hn", t_ + 1))
                    if due(t_):
                        pe.wait_ge(*upto("c_hnt", t_))
                    transposes(bank[0], c_hn[s_]).then_inc(sem("c_hn_t"), 1)
                if s[0] is not None:
                    t_, s_, n_ = s
                    pe.wait_ge(*upto("c_hnt", t_ + 1))
                    pe.wait_ge(*upto(f"c_in{s_}", 32 * (n_ + 1)))
                    if due(t_):
                        pe.wait_ge(*upto("c_x3", t_))
                    mm(bank[1][:, 0:C], ones[0:1, :], b_comb, start=True, stop=False)
                    for k in range(KC):
                        mm(bank[1][:, 0:C], c_hnt[s_][:, P * k:P * k + P], w_neigh[:, k, :], start=False, stop=False)
                    for k in range(KC):
                        last = mm(bank[1][:, 0:C], c_xnt[s_][:, P * k:P * k + P], w_comb[:, k, :], start=False, stop=k == KC - 1)
                    last.then_inc(sem("c_x_mm"), 1)
                    pe.wait_ge(*upto("c_xn", t_ + 1))
                    if due(t_):
                        pe.wait_ge(*upto("c_x4t", t_))
                    transposes(bank[2], c_xn[s_]).then_inc(sem("c_x4_t"), 1)
                    pe.wait_ge(*upto("c_x4t", t_ + 1))
                    if due(t_):
                        pe.wait_ge(*upto("c_r", t_))
                    for k in range(KC):
                        last = mm(bank[3][:, 0:8], c_x4t[s_][:, P * k:P * k + P], w_rt[:, k, :], start=k == 0, stop=k == KC - 1)
                    last.then_inc(sem("c_r_mm"), 1)
            if phase_end(pe):
                return
            pe.wait_ge(*upto("w_moe_in", 64))
            for g, s, n, m in expert_groups(pe):
                pe.wait_ge(*upto(f"s_in{s}", 32 * (n + 1)))
                if due(g):
                    pe.wait_ge(*upto("s_ct", g))
                pe.wait_ge(*upto("s_cg", g + 1))
                for j in range(m):
                    last = pe.transpose(bank[6][0:8, P * j:P * j + P], s_cg[s][:, 8 * j:8 * j + 8], ident[:, :])
                last.then_inc(sem("s_ct_mm"), 1)
                pe.wait_ge(*upto("s_ct", g + 1))
                if due(32 * g):
                    pe.wait_ge(*upto("s_acc", 32 * g))
                for j in range(m):
                    last = mm(bank[4 + j // 2][:, C * (j % 2):C * (j % 2) + C], s_ct[s][:, P * j:P * j + P], b2_sb, start=True, stop=True)
                last.then_inc(sem("s_cb_mm"), 1)

                def hidden(e):
                    for f in range(KC):
                        if due(16 * g + 2 * e + f - 3):
                            pe.wait_ge(*upto("s_h", 16 * g + 2 * e + f - 3))
                        for k in range(KC):
                            last = mm(bank[2 * (e % 2) + f][:, 0:m * P], w1_sb[:, e, k, P * f:P * f + P], s_xt[s][:, 0:m, k, :], start=k == 0, stop=k == KC - 1)
                        last.then_inc(sem("s_h_mm"), 1)

                hidden(0)
                for e in range(8):
                    if e < 7:
                        hidden(e + 1)
                    pe.wait_ge(*upto("s_h", 16 * g + 2 * e + 2))
                    pe.wait_ge(*upto("s_base", 4 * g + m))
                    if due(32 * g + m * e):
                        pe.wait_ge(*upto("s_acc", 32 * g + m * e))
                    for j in range(m):
                        for f in range(KC):
                            last = mm(bank[4 + j // 2][:, C * (j % 2):C * (j % 2) + C], s_h[e % 2][f][:, P * j:P * j + P], w2_sb[:, e, f, :], start=f == 0, stop=f == KC - 1)
                    last.then_inc(sem("s_y_mm"), 1)
            phase_end(pe)



def kernel(x, src, dst, edge_type_8, L0_gnn_W, L0_gnn_W_root, L0_gnn_bias, L0_mix_Wqkv, L0_mix_Wproj, L0_mix_bproj,
           L0_mix_ln_g, L0_mix_ln_b, L0_mix_Wg1, L0_mix_bg1, L0_mix_Wg2, L0_mix_bg2, L0_ffn_W_fx, L0_ffn_b_fx,
           L0_ffn_W_x, L0_ffn_b_x, L0_ffn_W_slice, L0_ffn_b_slice, L0_ffn_W_q, L0_ffn_W_k, L0_ffn_W_v, L0_ffn_W_out,
           L0_ffn_b_out, L0_ffn_temperature, L1_gnn_w_neigh, L1_gnn_w_self, L1_gnn_b_self, L1_mix_Wqkv, L1_mix_Wout,
           L1_mix_bout, L1_ffn_router_w, L1_ffn_w1, L1_ffn_b1, L1_ffn_w2, L1_ffn_b2):
    import numpy as np
    import concourse.bacc as bacc
    from concourse.bass_utils import run_bass_kernel_spmd

    a = np.asarray
    arrays = {
        "x": a(x), "src": a(src), "dst": a(dst), "etype": a(edge_type_8),
        "gnn0_w": a(L0_gnn_W).transpose(1, 0, 2).reshape(C, R * C), "gnn0_root": a(L0_gnn_W_root),
        "gnn0_bias": a(L0_gnn_bias), "mix_wqkv": a(L0_mix_Wqkv), "mix_wq_t": a(L0_mix_Wqkv)[:, 0:C].T,
        "mix_wproj": a(L0_mix_Wproj), "mix_bproj": a(L0_mix_bproj), "mix_ln_g": a(L0_mix_ln_g).reshape(KC, P).T,
        "mix_ln_b": a(L0_mix_ln_b).reshape(KC, P).T, "mix_wg1": a(L0_mix_Wg1), "mix_bg1": a(L0_mix_bg1), "mix_wg2": a(L0_mix_Wg2),
        "mix_bg2": a(L0_mix_bg2), "ffn_wfx": a(L0_ffn_W_fx), "ffn_bfx": a(L0_ffn_b_fx), "ffn_wx_t": a(L0_ffn_W_x).T,
        "ffn_bx": a(L0_ffn_b_x).reshape(4, P).T, "ffn_wslice": a(L0_ffn_W_slice), "ffn_bslice": a(L0_ffn_b_slice),
        "ffn_wq": a(L0_ffn_W_q), "ffn_wk": a(L0_ffn_W_k), "ffn_wv": a(L0_ffn_W_v), "ffn_wout": a(L0_ffn_W_out),
        "ffn_bout": a(L0_ffn_b_out), "ffn_temp": a(L0_ffn_temperature).reshape(1, 8),
        "gnn1_wneigh_t": a(L1_gnn_w_neigh).T, "gnn1_wself_t": a(L1_gnn_w_self).T, "gnn1_bself": a(L1_gnn_b_self),
        "mix1_wqkv": a(L1_mix_Wqkv), "mix1_wkv_t": a(L1_mix_Wqkv)[512:1536, :].T, "mix1_wout_t": a(L1_mix_Wout).T,
        "mix1_bout": a(L1_mix_bout), "router_t": a(L1_ffn_router_w).T, "w1": a(L1_ffn_w1), "b1": a(L1_ffn_b1).reshape(8 * KC, P).T,
        "w2": a(L1_ffn_w2), "b2": a(L1_ffn_b2),
    }
    nc = bacc.Bacc("TRN2", target_bir_lowering=False, num_devices=1)
    given, args = {}, {}
    for name, v in arrays.items():
        given[f"in_{name}"] = v = np.ascontiguousarray(v)
        args[name] = nc.dram_tensor(f"in_{name}", v.shape, mybir.dt.from_np(v.dtype), kind="ExternalInput").ap()
    args["out"] = nc.dram_tensor("out_x", (N, C), FP32, kind="ExternalOutput").ap()
    build(nc, **args)
    r = run_bass_kernel_spmd(nc, [given], core_ids=[0])
    return r.results[0]["out_x"]
```

```python
import concourse.bass as bass
from concourse import mybir
from contextlib import ExitStack

FP32 = mybir.dt.float32
BF16 = mybir.dt.bfloat16
I32 = mybir.dt.int32
ALU = mybir.AluOpType
ACT = mybir.ActivationFunctionType
AX = mybir.AxisListType.X

P = 128
N = 6250
C = 256
KC = C // P
NT = -(-N // P)
NP = NT * P
LAST = N - (NT - 1) * P
E = 200000
R = 8
ET = -(-E // P)
GRP = 4
BODY = 16
T = -(-(ET + NT - 1) // BODY) * BODY
NG = T // GRP
BPB = BODY // GRP
CPT = 8
TW = T + BODY
TB = -(-ET // P)
EROWS, ECOLS = 80, E // 80
PAD = TB * P * P + P - E
PROWS = 80
SCAT = 20
PAD_DST = 8191
EPS = 1e-5


def build(nc, x, src, dst, etype, gnn0_w, gnn0_root, gnn0_bias, mix_wqkv, mix_wq_t, mix_wproj, mix_bproj,
          mix_ln_g, mix_ln_b, mix_wg1, mix_bg1, mix_wg2, mix_bg2, ffn_wfx, ffn_bfx, ffn_wx_t, ffn_bx,
          ffn_wslice, ffn_bslice, ffn_wq, ffn_wk, ffn_wv, ffn_wout, ffn_bout, ffn_temp,
          gnn1_wneigh_t, gnn1_wself_t, gnn1_bself, mix1_wqkv, mix1_wkv_t, mix1_wout_t, mix1_bout,
          router_t, w1, b1, w2, b2, out, stop_after=99):
    ctx = ExitStack()
    with ctx:
        sems = {}

        share = {}
        ended = {}

        def take_turns(lane, step, count):
            share[step] = (lane, ended.get(lane, 0))
            ended[lane] = ended.get(lane, 0) + count

        for steps in (
                "n0_t n0_xnt n0_xn n0_var n0_rstd n0_gvar n0_grstd n0_gst n0_gag n0_st n0_ag n0_km n0_km_mm n0_root "
                "n0_root_mm n0_ga n0_gate n0_hg n0_hg_t n0_hgt n0_y_mm0 n0_y_mm1 n0_y_mm2 n0_y_mm3",
                "m1_k_mm m1_v_mm m1_ek m1_v m1_ctx_mm m2_xb m2_g_mm m2_sig m2_pr m2_prt_mm m2_prt m2_f_mm m2_out",
                "f1_x1 f1_st f1_ag f1_var f1_rstd f1_xn f1_t f1_xnt f1_l_mm f1_mx f1_lg f1_ex f1_sm f1_rs f1_sw "
                "f1_swt_mm f1_swt f1_u_mm",
                "f2_o_mm f2_x2 f2_st f2_ag f2_var f2_rstd f2_xn f2_t f2_xnt",
                "kv_k_mm kv_v_mm kv_sqk kv_sqv kv_v kv_ss kv_v1 kv_pv kv_root kv_inv kv_n1 kv_n2 kv_n3 kv_krs kv_kn "
                "kv_dots_mm",
                "c_hn c_hn_t c_hnt c_x_mm c_x3 c_st c_ag c_var c_rstd c_xn c_x4_t c_x4t c_x34 c_r c_r_mm"):
            for n_, step_ in enumerate(steps.split()):
                take_turns(f"tile_step_{n_}", step_, NT)
        for lane, steps in (
                ("load", [("n0_in", 1), ("f1_in", 1), ("f2_in", 2), ("c_in", 2)]),
                ("store_a", [("f1_x1_out", 1), ("c_x34_out", 1)]),
                ("store_b", [("n0_y_out", 1), ("f2_xn_out", 1)]), ("store_c", [("f2_x2_out", 1)]),
                ("store_d", [("n0_xnt_out", 1), ("f1_swt_out", 1), ("f2_xnt_out", 1), ("c_x4t_out", 1)]),
                ("store_e", [("n0_hgt_out", 1)])):
            for step_, dmas in steps:
                for s in range(2):
                    take_turns(f"{lane}_{s}", f"{step_}{s}", 16 * dmas * (NT // 2 + 1 - s))

        for lane, steps in (
                ("sum_mm", [("g0_sum_mm", 2 * NG), ("g1_sum_mm", 2 * NG)]),
                ("add", [("g0_add", T), ("g1_add", T)]),
                ("oh", [("g0_oh", NG + 3), ("g1_oh", NG + 1)]),
                ("idx", [("g0_idx", NG + BPB), ("g1_idx", NG + BPB)]),
                ("once_0", [("fs_u", 4), ("d_bd", 1)]),
                ("once_1", [("fs_ut_mm", KC), ("d_t1_mm", 4)]),
                ("once_2", [("fs_ut", KC), ("d_t1", 4)]),
                ("once_3", [("fs_tok_mm", 1), ("d_f_mm", KC)]),
                ("once_4", [("fs_tok", 4), ("w_comb", KC)]),
                ("once_5", [("fs_tokt_mm", 1), ("b_comb", 1)])):
            for step_, count_ in steps:
                take_turns(lane, step_, count_)
        for step_ in ("g0", "g1"):
            for h in range(BPB):
                take_turns(f"rows{h}", f"{step_}_rows{h}", 16 * GRP * (T // BODY))

        def sem(name):
            name = share.get(name, (name, 0))[0]
            if name not in sems:
                sems[name] = ctx.enter_context(nc.semaphore(name))
            return sems[name]

        def dram(name, shape, dt=FP32):
            return nc.dram_tensor(name, shape, dt, kind="Internal").ap()

        def sb(name, shape, dt=FP32):
            return ctx.enter_context(nc.sbuf_tensor(name, shape, dt))

        words = dram("edge_words", (E + PAD, 1), I32)
        y_table = dram("y_table", (NP * R, C))
        y_rows = y_table.rearrange("(n r) c -> n (r c)", r=R)
        xnt_d = dram("xn_t", (NT, P, C))
        hgt_d = dram("hgate_t", (NT, 64, P))
        xm_d = dram("x_mixed", (NP, C))
        x1_d = dram("x_1", (NP, C))
        swt_d = dram("slice_weights_t", (NT, P, 512))
        x2_d = dram("x_2", (NP, C))
        xn3_d = dram("xn_3", (NP, C))
        xnt3_d = dram("xn_3_t", (NT, P, C))
        x34_d = dram("x_3_plus_xn_4", (NP, C))
        xnt4_d = dram("xn_4_t", (NT, P, C))

        acc = sb("acc", [P, NT, C])
        idx_t = sb("idx_t", [P, TW], I32)
        dl_t = sb("dl_t", [P, TW])
        typ_t = sb("typ_t", [P, TW])
        win = sb("win", [1, TW], I32)
        cnt_at = sb("cnt_at", [1, TW], I32)
        cnt = sb("cnt", [P, NT, R])
        rdeg = sb("rdeg", [P, NT])
        rc3 = sb("rc3", [P, NT, 3 * R], BF16)
        ident = sb("ident", [P, P])
        identb = sb("identb", [P, P], BF16)
        iota = sb("iota", [P, P])
        ones = sb("ones", [P, P])
        bd32 = sb("bd32", [P, P])
        bd64 = sb("bd64", [P, P])
        off64 = sb("off64", [P, P])
        mhalf = sb("mhalf", [P, 16])
        arena = sb("arena", [P, 30000])
        bank = [ctx.enter_context(nc.psum_tensor(f"bank{i}", [P, 512], FP32)) for i in range(8)]

        class Arena:
            def __init__(self, at=0):
                self.at = at

            def take(self, cols, dt=FP32, parts=P):
                words_ = cols if dt != BF16 else -(-cols // 2)
                a = arena[0:parts, self.at:self.at + words_]
                self.at += words_
                assert self.at <= 30000, self.at
                return a if dt == FP32 else a.bitcast(dt)

        ar = Arena()
        e_src = ar.take(ECOLS, I32, EROWS)
        e_dst = ar.take(ECOLS, I32, EROWS)
        e_typ = ar.take(ECOLS, I32, EROWS)
        e_pad = ar.take(PAD // PROWS, I32, PROWS)
        r_word = ar.take(TB * P, I32)
        r_int = ar.take(TB * P, I32)
        r_dst = ar.take(TB * P)
        r_idx = ar.take(TB * P)
        r_dl = ar.take(TB * P)
        r_next = ar.take(TB, I32)
        r_w0i = ar.take(TB, I32)
        r_w0 = ar.take(TB)
        r_w1i = ar.take(TB, I32)
        r_w1 = ar.take(TB)
        r_sel = ar.take(TB * (NT - 1))
        r_sel2 = ar.take(TB * (NT - 1))
        x_base = ar.take(NT - 1)
        e_win = e_typ.bitcast(FP32)
        q_mask = ar.take(ECOLS, FP32, EROWS)
        q_pre = ar.take(ECOLS, FP32, EROWS)
        q_pos = ar.take(ECOLS, FP32, EROWS)
        q_posi = e_src
        q_offs = ar.take(1, FP32, EROWS)
        q_base = ar.take(1, FP32, EROWS)
        q_viol = ar.take(1, FP32, EROWS)
        q_row = ar.take(3 * EROWS, FP32, 1)
        q_one = ar.take(2, FP32, 1)
        q_flag = ar.take(1, I32, 1)
        q_tri = ar.take(EROWS, FP32, EROWS)
        q_islot = ar.take(SCAT, I32, EROWS)
        q_wslot = ar.take(SCAT, I32, EROWS)
        iota_i = ar.take(P, I32)
        col_i = ar.take(1, I32)
        blk_i = ar.take(2, I32)
        blk_f = ar.take(2)
        row_b = ar.take(P)
        row_bi = ar.take(P, I32)

        ar = Arena()
        w_all = ar.take(KC * R * C).rearrange("p (k n) -> p k n", k=KC)
        w_root = ar.take(KC * C).rearrange("p (k n) -> p k n", k=KC)
        w_k0 = ar.take(KC * C).rearrange("p (k n) -> p k n", k=KC)
        w_v0 = ar.take(KC * C).rearrange("p (k n) -> p k n", k=KC)
        wg1_raw = ar.take(KC * 64).rearrange("p (k n) -> p k n", k=KC)
        wg1 = ar.take(KC * 64).rearrange("p (k n) -> p k n", k=KC)
        lng = ar.take(KC)
        lnb = ar.take(KC)
        lnb_b = ar.take(KC * P).rearrange("p (k n) -> p k n", k=KC)
        bg1_b = ar.take(64)
        wg1_sum = ar.take(64)
        gate_b = ar.take(64)
        bias0_b = ar.take(C)
        kmax = ar.take(NT * KC).rearrange("p (t k) -> p t k", k=KC)
        kmax1 = ar.take(KC)
        negmax = ar.take(C, FP32, 1)
        after_weights0 = ar.at
        xin = [ar.take(C) for _ in range(2)]
        xn = [ar.take(C + 1) for _ in range(2)]
        stats = [ar.take(6) for _ in range(2)]
        mv = [ar.take(2) for _ in range(2)]
        veps = [ar.take(16) for _ in range(2)]
        rstd = [ar.take(16) for _ in range(2)]
        gstats = [ar.take(6) for _ in range(2)]
        gmv = [ar.take(2) for _ in range(2)]
        gveps = [ar.take(1) for _ in range(2)]
        grstd = [ar.take(1) for _ in range(2)]
        xnt = [ar.take(C) for _ in range(2)]
        ysb = [ar.take(R * C) for _ in range(2)]
        g_a = [ar.take(64) for _ in range(2)]
        g_b = [ar.take(64) for _ in range(2)]
        hg = [ar.take(64) for _ in range(2)]
        hgt = [ar.take(P, FP32, 64) for _ in range(2)]
        after_norm0 = ar.at

        ar = Arena(after_norm0)
        c_oh = [ar.take(GRP * P, BF16).rearrange("p (j n) -> p j n", j=GRP) for _ in range(CPT)]
        c_toh = [ar.take(GRP * R, BF16).rearrange("p (j n) -> p j n", j=GRP) for _ in range(CPT)]
        zerob = ar.take(512, BF16)
        ar = Arena(after_norm0)
        ring = [ar.take(C) for _ in range(BODY)]
        idx_s = ar.take(BODY, I32)
        oh = [ar.take(GRP * P).rearrange("p (j n) -> p j n", j=GRP) for _ in range(2)]
        woh = [ar.take(GRP * P).rearrange("p (j n) -> p j n", j=GRP) for _ in range(2)]
        ohb = [ar.take(GRP * P, BF16).rearrange("p (j n) -> p j n", j=GRP) for _ in range(BPB)]
        tohb = [ar.take(GRP * R, BF16).rearrange("p (j n) -> p j n", j=GRP) for _ in range(BPB)]
        oht = [ar.take(GRP * P, BF16) for _ in range(2)]
        wsel = [ar.take(GRP * 3 * R).rearrange("p (j k n) -> p j k n", j=GRP, k=3) for _ in range(2)]
        wgt = [ar.take(GRP) for _ in range(2)]
        rc_rest = ar.take(NT * R).rearrange("p (w r) -> p w r", r=R)
        rc_part = ar.take(NT * R).rearrange("p (w r) -> p w r", r=R)

        ar = Arena(0)
        w_qt = ar.take(KC * C).rearrange("p (k n) -> p k n", k=KC)
        w_qc = ar.take(KC * C).rearrange("p (k n) -> p k n", k=KC)
        w_proj = ar.take(KC * C).rearrange("p (k n) -> p k n", k=KC)
        bproj_b = ar.take(C)
        wg2 = ar.take(C, FP32, 64)
        bg2 = ar.take(C, FP32, 1)
        bdc = ar.take(KC * P).rearrange("p (k n) -> p k n", k=KC)
        cden = ar.take(KC)
        assert ar.at <= KC * R * C
        ar = Arena(after_weights0)
        m_xnt = ar.take(C)
        m_ek = ar.take(C)
        m_v = ar.take(2 * (P + 1))
        m_hgt = ar.take(P, FP32, 64)
        m_x = ar.take(C)
        m_sig = ar.take(C)
        m_pr = ar.take(C)
        m_prt = ar.take(C)
        m_xb = ar.take(C)
        m_out = ar.take(C)
        assert ar.at <= after_norm0

        ar = Arena()
        wx_t = ar.take(4 * C).rearrange("p (j n) -> p j n", j=4)
        w_fx = ar.take(KC * 512).rearrange("p (k n) -> p k n", k=KC)
        w_out = ar.take(4 * C).rearrange("p (j n) -> p j n", j=4)
        w_log = ar.take(KC * 512).rearrange("p (k n) -> p k n", k=KC)
        b_log = ar.take(512, FP32, 1)
        bslice8 = ar.take(512, FP32, 1)
        bx_c = ar.take(4)
        temp_c = ar.take(8, FP32, 1)
        rtemp_r = ar.take(8, FP32, 1)
        rtemp_b = ar.take(8)
        bfx_b = ar.take(512)
        wsl_bd = ar.take(P)
        wq_bd = ar.take(P)
        wk_bd = ar.take(P)
        wv_bd = ar.take(P)
        bout_r = ar.take(C, FP32, 1)
        f_m = ar.take(4 * C).rearrange("p (j n) -> p j n", j=4)
        after_ffn_w = ar.at
        f_u = ar.take(4 * 257).rearrange("p (j n) -> p j n", j=4)
        f_ut = ar.take(KC * 512).rearrange("p (k n) -> p k n", k=KC)
        f_den = ar.take(4)
        f_rden = ar.take(4)
        f_tok = ar.take(512)
        f_tok2 = ar.take(512)
        f_tokt = ar.take(512)
        f_qt = ar.take(512)
        f_kt = ar.take(512)
        f_v = ar.take(512)
        f_s = ar.take(512)
        f_s2 = ar.take(512)
        f_max = ar.take(4)
        f_sum = ar.take(4)
        f_rsum = ar.take(4)
        f_at = ar.take(512)
        f_ost = ar.take(512)
        a_x1 = [ar.take(C) for _ in range(2)]
        a_xin = [ar.take(C) for _ in range(2)]
        a_xn = [ar.take(C + 1) for _ in range(2)]
        a_xnt = [ar.take(C) for _ in range(2)]
        a_stats = [ar.take(6) for _ in range(2)]
        a_mv = [ar.take(2) for _ in range(2)]
        a_veps = [ar.take(1) for _ in range(2)]
        a_rstd = [ar.take(1) for _ in range(2)]
        a_max = [ar.take(8) for _ in range(2)]
        a_sum = [ar.take(8) for _ in range(2)]
        a_rsum = [ar.take(8) for _ in range(2)]
        a_lg = [ar.take(512) for _ in range(2)]
        a_ex = [ar.take(512) for _ in range(2)]
        a_sw = [ar.take(512) for _ in range(2)]
        a_swt = [ar.take(512) for _ in range(2)]
        after_a = ar.at
        ar = Arena(after_a)
        k_swt = [ar.take(512) for _ in range(2)]
        k_x1 = [ar.take(C) for _ in range(2)]
        k_x2 = [ar.take(C) for _ in range(2)]
        ar = Arena()
        w_q1 = ar.take(4 * C).rearrange("p (j n) -> p j n", j=4)
        w_o1t = ar.take(4 * C).rearrange("p (j n) -> p j n", j=4)
        w_neigh = ar.take(KC * C).rearrange("p (k n) -> p k n", k=KC)
        w_self = ar.take(KC * C).rearrange("p (k n) -> p k n", k=KC)
        w_comb = ar.take(KC * C).rearrange("p (k n) -> p k n", k=KC)
        w_rt = ar.take(KC * 8).rearrange("p (k n) -> p k n", k=KC)
        b_self = ar.take(C, FP32, 1)
        b_out1 = ar.take(C, FP32, 1)
        b_comb = ar.take(C, FP32, 1)
        d_bd = ar.take(512)
        d_t1 = ar.take(4 * C).rearrange("p (j n) -> p j n", j=4)
        logits = ar.take(NT * 8).rearrange("p (t e) -> p t e", e=8)
        comb = ar.take(NT * 8).rearrange("p (t e) -> p t e", e=8)
        ra = [ar.take(NT * 8).rearrange("p (t e) -> p t e", e=8) for _ in range(4)]
        rb = [ar.take(NT) for _ in range(6)]
        after_c = ar.at
        w_kv1 = ar.take(KC * 1024).rearrange("p (k n) -> p k n", k=KC)
        kv_mean = ar.take(KC * 16).rearrange("p (k n) -> p k n", k=KC)
        k_xnt = ar.take(C)
        k_sq = ar.take(1024)
        k_ss = ar.take(16)
        k_v1 = ar.take(16)
        k_pv = ar.take(8)
        k_root = ar.take(8)
        k_inv = ar.take(8)
        k_n = [ar.take(8) for _ in range(3)]
        k_rs = ar.take(8)
        k_kn = ar.take(512)
        k_v = ar.take(512)
        assert ar.at <= after_norm0, (ar.at, after_norm0)
        ar = Arena(after_c)
        c_hn = [ar.take(C) for _ in range(2)]
        c_hnt = [ar.take(C) for _ in range(2)]
        c_xnt = [ar.take(C) for _ in range(2)]
        c_x2 = [ar.take(C) for _ in range(2)]
        c_x3 = [ar.take(C) for _ in range(2)]
        c_xn = [ar.take(C) for _ in range(2)]
        c_x34 = [ar.take(C) for _ in range(2)]
        c_x4t = [ar.take(C) for _ in range(2)]
        c_stats = [ar.take(6) for _ in range(2)]
        c_mv = [ar.take(2) for _ in range(2)]
        c_veps = [ar.take(1) for _ in range(2)]
        c_rstd = [ar.take(1) for _ in range(2)]
        assert ar.at < after_norm0
        ar = Arena(after_norm0)
        w1_sb = ar.take(8 * KC * C).rearrange("p (e k n) -> p e k n", e=8, k=KC)
        w2_sb = ar.take(8 * KC * C).rearrange("p (e k n) -> p e k n", e=8, k=KC)
        b1_c = ar.take(16).rearrange("p (e k) -> p e k", k=KC)
        b2_sb = ar.take(C, FP32, 8)
        s_xt = [ar.take(4 * C).rearrange("p (j k n) -> p j k n", j=4, k=KC) for _ in range(2)]
        s_o = [ar.take(4 * C).rearrange("p (j n) -> p j n", j=4) for _ in range(2)]
        s_ct = [ar.take(512, FP32, 8) for _ in range(2)]
        s_cg = [ar.take(32) for _ in range(2)]
        s_h = [[ar.take(512) for _ in range(KC)] for _ in range(2)]

        def upto(step, value):
            return sem(step), value + share.get(step, (step, 0))[1]

        def due(value):
            return not isinstance(value, int) or value > 0

        def alone(eng):
            eng.nop(nofuse=True)

        def node_tiles(eng):
            yield 0, 0, 0
            yield 1, 1, 0
            with eng.Fori(1, NT // 2) as i:
                yield 2 * i, 0, i
                yield 2 * i + 1, 1, i
            yield NT - 1, 0, NT // 2

        def expert_groups(eng):
            yield 0, 0, 0, 4
            yield 1, 1, 0, 4
            with eng.Fori(1, NT // 8) as i:
                yield 2 * i, 0, i, 4
                yield 2 * i + 1, 1, i, 4
            yield NT // 4, 0, NT // 8, 1

        def following(t, s, n):
            return t + 1, 1 - s, n + s

        def skewed(eng):
            none = (None, None, None)
            yield (0, 0, 0), none, None
            for t, s, n in node_tiles(eng):
                if is_last(t):
                    yield none, (t, s, n), None
                else:
                    yield following(t, s, n), (t, s, n), None

        def is_last(t):
            return isinstance(t, int) and t == NT - 1

        def rows_of(t):
            return LAST if is_last(t) else P

        def bodies(eng):
            yield 0
            with eng.Fori(1, T // BODY) as i:
                yield i

        phase = {}

        def phase_end(eng):
            k = phase[eng.engine] = phase.get(eng.engine, 0) + 1
            eng.drain().then_inc(sem("phase_ended"), 1)
            eng.wait_ge(sem("phase_ended"), 5 * k)
            return k >= stop_after

        def col(v, t):
            return v[:, t:t + 1] if isinstance(t, int) else v[:, bass.ds(t, 1)]

        def rows(v, t):
            return v[t * P:(t + 1) * P, :] if isinstance(t, int) else v[bass.ds(t * P, P), :]

        def tile(v, t):
            return v[t, :, :] if isinstance(t, int) else v[bass.ds(t, 1), :, :].rearrange("a p c -> (a p) c")

        def at(v, t):
            return v[:, t, :] if isinstance(t, int) else v[:, bass.ds(t, 1), :].rearrange("p a c -> p (a c)")

        def span(v, start, n):
            return v[:, start:start + n] if isinstance(start, int) else v[:, bass.ds(start, n)]

        def windows(eng, first, n, table=win, most=NT - 1):
            _, ws = nc.values_load_multi_w_load_instructions(
                span(table, first, n), engines=[eng.engine], min_val=0, max_val=most,
                skip_runtime_bounds_check_because="a target is below N, so its window is below NT")
            return list(ws)

        def gather_bodies(eng):
            yield 0, 0, None
            with eng.Fori(1, NT - 1) as m:
                yield m, m, None
            yield NT - 1, NT - 1, None
            yield NT, None, None
            yield NT + 1, None, 0
            with eng.Fori(1, NT - 1) as m:
                yield m + (NT + 1), None, m
            yield 2 * NT, None, NT - 1
            for i in range(2 * NT + 1, T // BODY):
                yield i, None, None

        def between(i):
            return isinstance(i, int) and i == NT

        def staged(eng):
            def stages(u):
                return [(u - k, (u - k) % 2, (u - k) // 2) if 0 <= u - k < NT else (None, None, None) for k in range(3)]

            for u in range(4):
                yield stages(u)
            with eng.Fori(2, NT // 2) as i:
                yield [(2 * i, 0, i), (2 * i - 1, 1, i - 1), (2 * i - 2, 0, i - 1)]
                yield [(2 * i + 1, 1, i), (2 * i, 0, i), (2 * i - 1, 1, i - 1)]
            for u in range(NT - 1, NT + 2):
                yield stages(u)

        def target_windows(eng):
            yield 0
            with eng.Fori(1, NT) as w:
                yield w

        def copy_indices(act, pre, g, h, again):
            if due(again):
                act.wait_ge(*upto(f"{pre}_rows{h}", 16 * GRP * again))
            act.activation(idx_s[:, GRP * h:GRP * h + GRP], span(idx_t, g * GRP, GRP), ACT.Copy).then_inc(sem(f"{pre}_idx"), 1)

        def gather_rows(pool, pre, table):
            for i in bodies(pool):
                for h in range(BPB):
                    g = i * BPB + h
                    pool.wait_ge(*upto(f"{pre}_idx", g + 1))
                    alone(pool)
                    if due(i):
                        pool.wait_ge(*upto(f"{pre}_sum_mm", 2 * (g - BPB + 1)))
                        alone(pool)
                    for j in range(GRP):
                        k = GRP * h + j
                        pool.indirect_dma_start(
                            out=ring[k], out_offset=None, in_=table,
                            in_offset=bass.IndirectOffsetOnAxis(ap=idx_s[:, k:k + 1], axis=0),
                        ).then_inc(sem(f"{pre}_rows{h}"), 16)

        heads = lambda v, h=8: v.rearrange("p (h g) -> p h g", h=h)
        block = ctx.enter_context(nc.Block())

        @block.sync
        def _(sp):
            sp.dma_start(e_dst, dst.rearrange("(p c) -> p c", p=EROWS)).then_inc(sem("edges_in"), 16)
            sp.dma_start(e_src, src.rearrange("(p c) -> p c", p=EROWS)).then_inc(sem("edges_in"), 16)
            sp.dma_start(e_typ, etype.rearrange("(p c) -> p c", p=EROWS)).then_inc(sem("edges_in"), 16)
            sp.wait_ge(*upto("words_packed", 2))
            sp.dma_start(words[0:E, :].rearrange("(p c) o -> p (c o)", p=EROWS), e_dst).then_inc(sem("words_out"), 16)
            sp.dma_start(words[E:E + PAD, :].rearrange("(p c) o -> p (c o)", p=PROWS), e_pad).then_inc(sem("words_out"), 16)
            sp.wait_ge(*upto("words_final", 1))
            full = words[0:TB * P * P, :].rearrange("(b t e) o -> t b (e o)", t=P, e=P)
            sp.dma_start(r_word.rearrange("t (b e) -> t b e", b=TB), full).then_inc(sem("rows_in"), 16)
            nxt = words[P:P + TB * P * P, :].rearrange("(b t e) o -> t b (e o)", t=P, e=P)[:, :, 0:1]
            sp.dma_start(r_next.rearrange("t (b e) -> t b e", e=1), nxt, allow_slow_non_contiguous=True).then_inc(sem("rows_in"), 16)
            if phase_end(sp):
                return
            for n_, (d_, s_) in enumerate([
                    (w_all, gnn0_w.rearrange("(k p) n -> p k n", p=P)),
                    (w_root, gnn0_root.rearrange("(k p) n -> p k n", p=P)),
                    (w_k0, mix_wqkv[:, C:2 * C].rearrange("(k p) n -> p k n", p=P)),
                    (w_v0, mix_wqkv[:, 2 * C:3 * C].rearrange("(k p) n -> p k n", p=P)),
                    (wg1_raw, mix_wg1.rearrange("(k p) n -> p k n", p=P)),
                    (lng, mix_ln_g),
                    (lnb, mix_ln_b),
                    (bg1_b, mix_bg1.partition_broadcast(P)),
                    (bias0_b, gnn0_bias.partition_broadcast(P))]):
                sp.dma_start(d_, s_).then_inc(sem("w0_in"), 16)
            for t, s, n in node_tiles(sp):
                r = rows_of(t)
                if due(t - 1):
                    sp.wait_ge(*upto("n0_xn", t - 1))
                    alone(sp)
                source = x[(NT - 1) * P:N, :] if is_last(t) else rows(x, t)
                sp.dma_start(xin[s][0:r, :], source).then_inc(sem(f"n0_in{s}"), 16)
                if due(t - 1):
                    sp.wait_ge(*upto("n0_y_act", 2 * (t - 1)))
                    alone(sp)
                    sp.wait_ge(*upto("n0_y_dve", 2 * (t - 1)))
                    alone(sp)
                    sp.dma_start(rows(y_rows, t - 2), ysb[s]).then_inc(sem(f"n0_y_out{s}"), 16)
            for t in (NT - 2, NT - 1):
                sp.wait_ge(*upto("n0_y_act", 2 * (t + 1)))
                sp.wait_ge(*upto("n0_y_dve", 2 * (t + 1)))
                sp.dma_start(rows(y_rows, t), ysb[t % 2]).then_inc(sem(f"n0_y_out{t % 2}"), 16)
            for s in range(2):
                sp.wait_ge(*upto(f"n0_y_out{s}", 16 * (NT // 2 + 1 - s)))
            if phase_end(sp):
                return
            for d_, s_ in [(w_qt, mix_wq_t.rearrange("(k p) n -> p k n", p=P)),
                           (w_proj, mix_wproj.rearrange("(k p) n -> p k n", p=P)),
                           (bproj_b, mix_bproj.partition_broadcast(P)),
                           (wg2, mix_wg2), (bg2, mix_bg2.rearrange("(a n) -> a n", a=1))]:
                sp.dma_start(d_, s_).then_inc(sem("w_mix_in"), 16)
            for t, s, n in node_tiles(sp):
                if due(t):
                    sp.wait_ge(*upto("m1_v_mm", t))
                    alone(sp)
                sp.dma_start(m_xnt, tile(xnt_d, t)).then_inc(sem("m1_in"), 16)
            sp.wait_ge(*upto("m1_v_mm", NT))
            for t, s, n in node_tiles(sp):
                r = rows_of(t)
                if due(t):
                    sp.wait_ge(*upto("m2_g_mm", t))
                    alone(sp)
                    sp.wait_ge(*upto("m2_xb", t))
                    alone(sp)
                sp.dma_start(m_xnt, tile(xnt_d, t)).then_inc(sem("m2_in"), 16)
                sp.dma_start(m_hgt, tile(hgt_d, t)).then_inc(sem("m2_in"), 16)
                source = x[(NT - 1) * P:N, :] if is_last(t) else rows(x, t)
                sp.dma_start(m_x[0:r, :], source).then_inc(sem("m2_in"), 16)
                if due(t):
                    sp.wait_ge(*upto("m2_out", t))
                    alone(sp)
                    sp.dma_start(rows(xm_d, t - 1), m_out).then_inc(sem("m2_st"), 16)
            sp.wait_ge(*upto("m2_out", NT))
            sp.dma_start(rows(xm_d, NT - 1), m_out).then_inc(sem("m2_st"), 16)
            sp.wait_ge(*upto("m2_st", 16 * NT))
            if phase_end(sp):
                return
            for d_, s_ in [(wx_t, ffn_wx_t.rearrange("(j p) n -> p j n", p=P)),
                           (w_fx, ffn_wfx.rearrange("(k p) n -> p k n", p=P)),
                           (w_out, ffn_wout.rearrange("(j p) n -> p j n", p=P)),
                           (bx_c, ffn_bx),
                           (temp_c, ffn_temp),
                           (bfx_b, ffn_bfx.partition_broadcast(P)),
                           (bout_r, ffn_bout.rearrange("(a n) -> a n", a=1))]:
                sp.dma_start(d_, s_).then_inc(sem("w_ffn_in"), 16)
            sp.wait_ge(*upto("bd_zeroed", 4))
            for d_, s_ in [(wsl_bd, ffn_wslice), (wq_bd, ffn_wq), (wk_bd, ffn_wk), (wv_bd, ffn_wv)]:
                for b_ in range(2):
                    sp.dma_start(d_[64 * b_:64 * b_ + 64, 64 * b_:64 * b_ + 64], s_).then_inc(sem("w_ffn_in"), 16)
            for h in range(8):
                sp.dma_start(bslice8[0:1, 64 * h:64 * h + 64], ffn_bslice.rearrange("(a n) -> a n", a=1)).then_inc(sem("w_ffn_in"), 16)
            for t, s, n in node_tiles(sp):
                if due(t - 1):
                    sp.wait_ge(*upto("f1_x1", t - 1))
                    alone(sp)
                sp.dma_start(a_xin[s], rows(xm_d, t)).then_inc(sem(f"f1_in{s}"), 16)
            if phase_end(sp):
                return
            def store2(t, s):
                sp.wait_ge(*upto("f2_x2", t + 1))
                alone(sp)
                sp.dma_start(rows(x2_d, t), k_x2[s]).then_inc(sem(f"f2_x2_out{s}"), 16)
                sp.wait_ge(*upto("f2_xn", t + 1))
                alone(sp)

            for t, s, n in node_tiles(sp):
                if due(t - 1):
                    sp.wait_ge(*upto("f2_o_mm", t - 1))
                    alone(sp)
                    sp.wait_ge(*upto("f2_x2", t - 1))
                    alone(sp)
                sp.dma_start(k_swt[s], tile(swt_d, t)).then_inc(sem(f"f2_in{s}"), 16)
                sp.dma_start(k_x1[s], rows(x1_d, t)).then_inc(sem(f"f2_in{s}"), 16)
                if due(t - 1):
                    store2(t - 2, s)
                    sp.dma_start(rows(xn3_d, t - 2), a_xn[s][:, 0:C]).then_inc(sem(f"f2_xn_out{s}"), 16)
            for t in (NT - 2, NT - 1):
                store2(t, t % 2)
                sp.dma_start(rows(xn3_d, t), a_xn[t % 2][:, 0:C]).then_inc(sem(f"f2_xn_out{t % 2}"), 16)
            for s in range(2):
                for name in (f"f2_x2_out{s}", f"f2_xn_out{s}"):
                    sp.wait_ge(*upto(name, 16 * (NT // 2 + 1 - s)))
            if phase_end(sp):
                return
            sp.dma_start(w_kv1, mix1_wkv_t.rearrange("(k p) n -> p k n", p=P)).then_inc(sem("w_kv_in"), 16)
            for d_, s_ in [(w_q1, mix1_wqkv[0:512, :].rearrange("(j p) n -> p j n", p=P)),
                           (w_o1t, mix1_wout_t.rearrange("(j p) n -> p j n", p=P)),
                           (w_neigh, gnn1_wneigh_t.rearrange("(k p) n -> p k n", p=P)),
                           (w_self, gnn1_wself_t.rearrange("(k p) n -> p k n", p=P)),
                           (w_rt, router_t.rearrange("(k p) n -> p k n", p=P)),
                           (b_self, gnn1_bself.rearrange("(a n) -> a n", a=1)),
                           (b_out1, mix1_bout.rearrange("(a n) -> a n", a=1))]:
                sp.dma_start(d_, s_).then_inc(sem("w_l1_in"), 16)
            for t, s, n in node_tiles(sp):
                if due(t):
                    sp.wait_ge(*upto("kv_v_mm", t))
                    alone(sp)
                sp.dma_start(k_xnt, tile(xnt3_d, t)).then_inc(sem("kv_in"), 16)
            if phase_end(sp):
                return
            for t, s, n in node_tiles(sp):
                if due(t - 1):
                    sp.wait_ge(*upto("c_x_mm", t - 1))
                    alone(sp)
                if due(t - 1):
                    sp.wait_ge(*upto("c_x3", t - 1))
                    alone(sp)
                sp.dma_start(c_xnt[s], tile(xnt3_d, t)).then_inc(sem(f"c_in{s}"), 16)
                sp.dma_start(c_x2[s], rows(x2_d, t)).then_inc(sem(f"c_in{s}"), 16)
            sp.dma_start(w1_sb, w1.rearrange("e (k p) n -> p e k n", p=P)).then_inc(sem("w_moe_in"), 16)
            sp.dma_start(w2_sb, w2.rearrange("e (k p) n -> p e k n", p=P)).then_inc(sem("w_moe_in"), 16)
            sp.dma_start(b1_c, b1.rearrange("p (e k) -> p e k", k=KC)).then_inc(sem("w_moe_in"), 16)
            sp.dma_start(b2_sb, b2).then_inc(sem("w_moe_in"), 16)
            if phase_end(sp):
                return
            for g, s, n, m in expert_groups(sp):
                if due(16 * (g - 1)):
                    sp.wait_ge(*upto("s_h_mm", 16 * (g - 1)))
                    alone(sp)
                if due(16 * n):
                    sp.wait_ge(*upto(f"s_out{s}", 16 * n))
                    alone(sp)
                if m == 4:
                    xs = xnt4_d[4 * g:4 * g + 4, :, :] if isinstance(g, int) else xnt4_d[bass.ds(g * 4, 4), :, :]
                    os_ = x34_d[512 * g:512 * g + 512, :] if isinstance(g, int) else x34_d[bass.ds(g * 512, 512), :]
                else:
                    xs, os_ = xnt4_d[NT - 1:NT, :, :], x34_d[(NT - 1) * P:NP, :]
                sp.dma_start(s_xt[s][:, 0:m, :, :].rearrange("p j k n -> p j (k n)"),
                             xs.rearrange("j p c -> p j c")).then_inc(sem(f"s_in{s}"), 16)
                sp.dma_start(s_o[s][:, 0:m, :], os_.rearrange("(j p) c -> p j c", p=P)).then_inc(sem(f"s_in{s}"), 16)
            phase_end(sp)

        @block.gpsimd
        def _(pool):
            pool.iota(iota_i, pattern=[[1, P]], base=0, channel_multiplier=0).then_inc(sem("iotas"), 1)
            pool.iota(col_i, pattern=[[0, 1]], base=0, channel_multiplier=1).then_inc(sem("iotas"), 1)
            pool.memset(ones[:, :], 1.0).then_inc(sem("const"), 1)
            pool.memset(mhalf[:, :], -0.5).then_inc(sem("const"), 1)
            pool.memset(e_pad, PAD_DST << 16).then_inc(sem("words_packed"), 1)
            for v in (idx_t, dl_t):
                pool.memset(v[:, ET + NT - 1:TW], 0 if v is idx_t else -1.0).then_inc(sem("table_pad"), 1)
            pool.memset(win[:, ET + NT - 1:TW], NT - 1).then_inc(sem("table_pad"), 1)
            pool.wait_ge(*upto("q_flag", 1))
            unsorted = pool.value_load(q_flag, min_val=0, max_val=1)
            pool.wait_ge(*upto("words_out", 32))
            with pool.If(unsorted > 0):
                pool.wait_ge(*upto("q_posi", 1))
                with pool.Fori(0, ECOLS // SCAT) as i:
                    pool.tensor_copy(q_islot, span(q_posi, i * SCAT, SCAT)).then_inc(sem("q_slots"), 1)
                    pool.tensor_copy(q_wslot, span(e_dst, i * SCAT, SCAT)).then_inc(sem("q_slots"), 1)
                    pool.wait_ge(*upto("q_slots", 2 * i + 2))
                    alone(pool)
                    for k in range(SCAT):
                        pool.indirect_dma_start(
                            out=words[0:E, :], out_offset=bass.IndirectOffsetOnAxis(ap=q_islot[:, k:k + 1], axis=0),
                            in_=q_wslot[:, k:k + 1], in_offset=None).then_inc(sem("q_scattered"), 16)
                    pool.wait_ge(*upto("q_scattered", 16 * SCAT * (i + 1)))
                    alone(pool)
            pool.nop().then_inc(sem("words_final"), 1)
            if phase_end(pool):
                return
            for t, s, n in node_tiles(pool):
                pool.wait_ge(*upto("n0_var", t + 1))
                alone(pool)
                pool.tensor_tensor(rstd[s][:, 0:1], veps[s][:, 0:1], mhalf[:, 0:1], ALU.pow).then_inc(sem("n0_rstd"), 1)
                pool.wait_ge(*upto("n0_gvar", t + 1))
                alone(pool)
                pool.tensor_tensor(grstd[s], gveps[s], mhalf[:, 0:1], ALU.pow).then_inc(sem("n0_grstd"), 1)
            if phase_end(pool):
                return
            gather_rows(pool, "g0", y_table)
            if phase_end(pool):
                return
            for v in (wsl_bd, wq_bd, wk_bd, wv_bd):
                pool.memset(v, 0.0).then_inc(sem("bd_zeroed"), 1)
            for s in range(2):
                pool.memset(a_xn[s][:, C:C + 1], 1.0).then_inc(sem("a_ones"), 1)
            for t, s, n in node_tiles(pool):
                pool.wait_ge(*upto("f1_var", t + 1))
                alone(pool)
                pool.tensor_tensor(a_rstd[s], a_veps[s], mhalf[:, 0:1], ALU.pow).then_inc(sem("f1_rstd"), 1)
                pool.dma_start(rows(x1_d, t), a_x1[s]).then_inc(sem(f"f1_x1_out{s}"), 16)
            for s in range(2):
                pool.wait_ge(*upto(f"f1_x1_out{s}", 16 * (NT // 2 + 1 - s)))
            if phase_end(pool):
                return
            for t, s, n in node_tiles(pool):
                pool.wait_ge(*upto("f2_var", t + 1))
                alone(pool)
                pool.tensor_tensor(a_rstd[s], a_veps[s], mhalf[:, 0:1], ALU.pow).then_inc(sem("f2_rstd"), 1)
            if phase_end(pool):
                return
            gather_rows(pool, "g1", xn3_d)
            if phase_end(pool):
                return
            for _, (t, s, n), (t_, s_, n_) in staged(pool):
                if t_ is not None:
                    pool.wait_ge(*upto("c_x34", t_ + 1))
                    alone(pool)
                    pool.dma_start(rows(x34_d, t_), c_x34[s_]).then_inc(sem(f"c_x34_out{s_}"), 16)
                if t is not None:
                    pool.wait_ge(*upto("c_var", t + 1))
                    alone(pool)
                    pool.tensor_tensor(c_rstd[s], c_veps[s], mhalf[:, 0:1], ALU.pow).then_inc(sem("c_rstd"), 1)
            for s in range(2):
                pool.wait_ge(*upto(f"c_x34_out{s}", 16 * (NT // 2 + 1 - s)))
            if phase_end(pool):
                return
            for g, s, n, m in expert_groups(pool):
                pool.wait_ge(*upto("s_acc", 32 * (g + 1) if m == 4 else 32 * g + 8))
                alone(pool)
                if m == 4:
                    o_ = out[512 * g:512 * g + 512, :] if isinstance(g, int) else out[bass.ds(g * 512, 512), :]
                    pool.dma_start(o_.rearrange("(j p) c -> p j c", p=P), s_o[s]).then_inc(sem(f"s_out{s}"), 16)
                else:
                    pool.dma_start(out[(NT - 1) * P:N, :], s_o[s][0:LAST, 0, :]).then_inc(sem(f"s_out{s}"), 16)
            pool.wait_ge(*upto("s_out0", 16 * (NT // 8 + 1)))
            pool.wait_ge(*upto("s_out1", 16 * (NT // 8)))
            phase_end(pool)

        @block.scalar
        def _(act):
            if phase_end(act):
                return
            for t, s, n in skewed(act):
                if s[0] is not None:
                    t_, s_, n_ = s
                    if due(16 * n_):
                        act.wait_ge(*upto(f"n0_y_out{s_}", 16 * n_))
                    for b_ in (0, 2):
                        act.wait_ge(*upto(f"n0_y_mm{b_}", t_ + 1))
                        act.activation(ysb[s_][:, 512 * b_:512 * b_ + 512], bank[b_][:, :], ACT.Copy).then_inc(sem("n0_y_act"), 1)
                if t[0] is not None:
                    t_, s_, n_ = t
                    act.wait_ge(*upto("n0_t", t_ + 1))
                    if due(t_ - 1):
                        act.wait_ge(*upto("n0_km_mm", t_ - 1))
                    if due(16 * n_):
                        act.wait_ge(*upto(f"n0_xnt_out{s_}", 16 * n_))
                    act.activation(xnt[s_], bank[4][:, 0:C], ACT.Copy).then_inc(sem("n0_xnt"), 1)
                    act.wait_ge(*upto("n0_xnt", t_ + 1))
                    alone(act)
                    act.dma_start(tile(xnt_d, t_), xnt[s_]).then_inc(sem(f"n0_xnt_out{s_}"), 16)
                if s[0] is not None:
                    t_, s_, n_ = s
                    act.wait_ge(*upto("n0_gate", t_ + 1))
                    if due(t_ - 1):
                        act.wait_ge(*upto("n0_hg_t", t_ - 1))
                    act.activation(hg[s_], g_b[s_], ACT.Gelu, scale=-1.0).then_inc(sem("n0_hg"), 1)
                    act.wait_ge(*upto("n0_hg_t", t_ + 1))
                    if due(16 * n_):
                        act.wait_ge(*upto(f"n0_hgt_out{s_}", 16 * n_))
                    act.activation(hgt[s_], bank[4][0:64, C:C + P], ACT.Copy).then_inc(sem("n0_hgt"), 1)
                    act.wait_ge(*upto("n0_hgt", t_ + 1))
                    alone(act)
                    act.dma_start(tile(hgt_d, t_), hgt[s_]).then_inc(sem(f"n0_hgt_out{s_}"), 16)
            for s in range(2):
                for name in (f"n0_xnt_out{s}", f"n0_hgt_out{s}"):
                    act.wait_ge(*upto(name, 16 * (NT // 2 + 1 - s)))
            if phase_end(act):
                return
            def copy_oht(g, b_):
                act.wait_ge(*upto("g0_oht_mm", g + 1))
                if due(g - 1):
                    act.wait_ge(*upto("g0_look_mm", g - 1))
                act.activation(oht[b_], bank[6][:, :], ACT.Copy).then_inc(sem("g0_oht"), 1)

            for g in range(BPB):
                copy_indices(act, "g0", g, g, 0)
            for g in range(2):
                copy_oht(g, g)
            for i, m1, m2 in gather_bodies(act):
                for h in range(BPB):
                    g = i * BPB + h
                    copy_oht(g + 2, h % 2)
                    copy_indices(act, "g0", g + BPB, h, i + 1)
                    if m1 is not None and h == 1:
                        act.wait_ge(*upto("m1_k_mm", m1 + 1))
                        if due(m1):
                            act.wait_ge(*upto("m1_ctx_mm", m1))
                        act.activation(m_ek, bank[4][:, 0:C], ACT.Exp).then_inc(sem("m1_ek"), 1)
                    if m2 is not None and h == 0:
                        act.wait_ge(*upto("m2_g_mm", m2 + 1))
                        if due(m2):
                            act.wait_ge(*upto("m2_pr", m2))
                        act.activation(m_sig, bank[5][:, 0:C], ACT.Sigmoid).then_inc(sem("m2_sig"), 1)
                    if m2 is not None and h == 2:
                        act.wait_ge(*upto("m2_prt_mm", m2 + 1))
                        if due(m2):
                            act.wait_ge(*upto("m2_f_mm", m2))
                        act.activation(m_prt, bank[2][:, 0:C], ACT.Copy).then_inc(sem("m2_prt"), 1)
            if phase_end(act):
                return
            for _, (t, s, n), (t_, s_, n_) in staged(act):
                if t is not None:
                    act.wait_ge(*upto("f1_t", t + 1))
                    if due(t - 1):
                        act.wait_ge(*upto("f1_l_mm", t - 1))
                    act.activation(a_xnt[s], bank[0][:, 0:C], ACT.Copy).then_inc(sem("f1_xnt"), 1)
                if t_ is not None:
                    act.wait_ge(*upto("f1_lg", t_ + 1))
                    if due(t_ - 1):
                        act.wait_ge(*upto("f1_sw", t_ - 1))
                    act.activation(a_ex[s_], a_lg[s_], ACT.Exp).then_inc(sem("f1_ex"), 1)
                    act.wait_ge(*upto("f1_swt_mm", t_ + 1))
                    if due(16 * n_):
                        act.wait_ge(*upto(f"f1_swt_out{s_}", 16 * n_))
                    act.activation(a_swt[s_], bank[3][:, :], ACT.Copy).then_inc(sem("f1_swt"), 1)
                    act.wait_ge(*upto("f1_swt", t_ + 1))
                    alone(act)
                    act.dma_start(tile(swt_d, t_), a_swt[s_]).then_inc(sem(f"f1_swt_out{s_}"), 16)
            for s in range(2):
                act.wait_ge(*upto(f"f1_swt_out{s}", 16 * (NT // 2 + 1 - s)))
            for j in range(4):
                act.wait_ge(*upto("fs_max", j + 1))
                act.activation(f_s2[:, P * j:P * j + P], f_s[:, P * j:P * j + P], ACT.Exp, bias=f_max[:, j:j + 1],
                               scale=1.0, accum_out=f_sum[:, j:j + 1]).then_inc(sem("fs_exp"), 1)
            if phase_end(act):
                return
            for t_, s_, n_ in node_tiles(act):
                act.wait_ge(*upto("f2_t", t_ + 1))
                if due(16 * n_):
                    act.wait_ge(*upto(f"f2_xnt_out{s_}", 16 * n_))
                act.activation(a_xnt[s_], bank[2][:, 0:C], ACT.Copy).then_inc(sem("f2_xnt"), 1)
                act.wait_ge(*upto("f2_xnt", t_ + 1))
                alone(act)
                act.dma_start(tile(xnt3_d, t_), a_xnt[s_]).then_inc(sem(f"f2_xnt_out{s_}"), 16)
            for s in range(2):
                act.wait_ge(*upto(f"f2_xnt_out{s}", 16 * (NT // 2 + 1 - s)))
            if phase_end(act):
                return
            for g in range(BPB):
                copy_indices(act, "g1", g, g, 0)
            for i, m1, m2 in gather_bodies(act):
                for h in range(BPB):
                    copy_indices(act, "g1", (i + 1) * BPB + h, h, i + 1)
                    if m1 is not None and h == 0:
                        act.wait_ge(*upto("kv_k_mm", m1 + 1))
                        if due(m1):
                            act.wait_ge(*upto("kv_ss", m1))
                        act.activation(k_sq[:, 0:512], bank[2][:, :], ACT.Square).then_inc(sem("kv_sqk"), 1)
                        act.wait_ge(*upto("kv_v_mm", m1 + 1))
                        act.activation(k_sq[:, 512:1024], bank[3][:, :], ACT.Square).then_inc(sem("kv_sqv"), 1)
                        if due(m1):
                            act.wait_ge(*upto("kv_dots_mm", m1))
                        act.activation(k_v, bank[3][:, :], ACT.Copy).then_inc(sem("kv_v"), 1)
                    if m1 is not None and h == 2:
                        act.wait_ge(*upto("kv_pv", m1 + 1))
                        if due(m1):
                            act.wait_ge(*upto("kv_inv", m1))
                        act.activation(k_root, k_pv, ACT.Sqrt).then_inc(sem("kv_root"), 1)
            if phase_end(act):
                return
            for (t, s, n), _, (t_, s_, n_) in staged(act):
                if t_ is not None:
                    act.wait_ge(*upto("c_x4_t", t_ + 1))
                    if due(t_ - 1):
                        act.wait_ge(*upto("c_r_mm", t_ - 1))
                    if due(16 * n_):
                        act.wait_ge(*upto(f"c_x4t_out{s_}", 16 * n_))
                    act.activation(c_x4t[s_], bank[2][:, 0:C], ACT.Copy).then_inc(sem("c_x4t"), 1)
                if t is not None:
                    act.wait_ge(*upto("c_hn_t", t + 1))
                    if due(t - 1):
                        act.wait_ge(*upto("c_x_mm", t - 1))
                    act.activation(c_hnt[s], bank[0][:, 0:C], ACT.Copy).then_inc(sem("c_hnt"), 1)
                if t_ is not None:
                    act.wait_ge(*upto("c_x4t", t_ + 1))
                    alone(act)
                    act.dma_start(tile(xnt4_d, t_), c_x4t[s_]).then_inc(sem(f"c_x4t_out{s_}"), 16)
            for s in range(2):
                act.wait_ge(*upto(f"c_x4t_out{s}", 16 * (NT // 2 + 1 - s)))
            act.wait_ge(*upto("r_exp_in", 1))
            act.activation(ra[1], ra[0], ACT.Exp).then_inc(sem("r_exp"), 1)
            if phase_end(act):
                return
            for g, s, n, m in expert_groups(act):
                act.wait_ge(*upto("s_ct_mm", g + 1))
                if due(g - 1):
                    act.wait_ge(*upto("s_cb_mm", g - 1))
                act.activation(s_ct[s][:, 0:m * P], bank[6][0:8, 0:m * P], ACT.Copy).then_inc(sem("s_ct"), 1)
                act.wait_ge(*upto("w_moe_in", 64))
                for e in range(8):
                    for f in range(KC):
                        k = 16 * g + 2 * e + f
                        act.wait_ge(*upto("s_h_mm", k + 1))
                        if due(8 * g + e - 1):
                            act.wait_ge(*upto("s_y_mm", 8 * g + e - 1))
                        act.activation(s_h[e % 2][f][:, 0:m * P], bank[2 * (e % 2) + f][:, 0:m * P], ACT.Gelu,
                                       bias=b1_c[:, e, f:f + 1]).then_inc(sem("s_h"), 1)
            phase_end(act)

        @block.vector
        def _(dve):
            step = [0]

            def chain(ins):
                step[0] += 1
                ins.then_inc(sem("dve_chain"), 1)
                dve.wait_ge(sem("dve_chain"), step[0])

            dve.wait_ge(*upto("iotas", 2))
            chain(dve.tensor_copy(iota[:, :], iota_i))
            chain(dve.tensor_copy(blk_f[:, 0:1], col_i))
            chain(dve.tensor_scalar(ident[:, :], iota[:, :], blk_f[:, 0:1], None, ALU.is_equal))
            chain(dve.tensor_copy(identb[:, :], ident[:, :]))
            for bd, sh in ((bd32, 5), (bd64, 6)):
                chain(dve.tensor_scalar(row_bi, iota_i, sh, None, ALU.arith_shift_right))
                chain(dve.tensor_copy(row_b, row_bi))
                chain(dve.tensor_scalar(blk_i[:, 0:1], col_i, sh, None, ALU.arith_shift_right))
                chain(dve.tensor_copy(blk_f[:, 1:2], blk_i[:, 0:1]))
                chain(dve.tensor_scalar(bd[:, :], row_b, blk_f[:, 1:2], None, ALU.is_equal))
            chain(dve.tensor_scalar(off64[:, :], bd64[:, :], -1.0, 1e30, ALU.add, ALU.mult))
            dve.wait_ge(*upto("edges_in", 48))
            chain(dve.scalar_tensor_tensor(e_src, e_src, 3, e_typ, ALU.logical_shift_left, ALU.bitwise_or))
            dve.scalar_tensor_tensor(e_dst, e_dst, 16, e_src, ALU.logical_shift_left, ALU.bitwise_or).then_inc(sem("words_packed"), 1)
            dve.wait_ge(*upto("words_packed", 2))
            chain(dve.tensor_scalar(q_posi, e_dst, 23, None, ALU.logical_shift_right))
            chain(dve.tensor_copy(e_win, q_posi))
            chain(dve.tensor_tensor(q_mask[:, 0:ECOLS - 1], e_win[:, 0:ECOLS - 1], e_win[:, 1:ECOLS], ALU.is_gt))
            dve.tensor_reduce(q_viol, q_mask[:, 0:ECOLS - 1], AX, ALU.add).then_inc(sem("q_viol"), 1)
            dve.wait_ge(*upto("q_rows_mm", 1))
            chain(dve.tensor_copy(q_row, bank[5][0:1, 0:3 * EROWS]))
            chain(dve.tensor_tensor(q_row[:, 0:EROWS - 1], q_row[:, EROWS:2 * EROWS - 1], q_row[:, 1:EROWS], ALU.is_gt))
            chain(dve.tensor_tensor(q_row[:, 0:EROWS - 1], q_row[:, 0:EROWS - 1], q_row[:, 2 * EROWS:3 * EROWS - 1], ALU.add))
            chain(dve.tensor_reduce(q_one[:, 0:1], q_row[:, 0:EROWS - 1], AX, ALU.add))
            chain(dve.tensor_tensor(q_one[:, 0:1], q_one[:, 0:1], q_row[:, 3 * EROWS - 1:3 * EROWS], ALU.add))
            chain(dve.tensor_scalar(q_one[:, 1:2], q_one[:, 0:1], 1.0, None, ALU.min))
            dve.tensor_copy(q_flag, q_one[:, 1:2]).then_inc(sem("q_flag"), 1)
            dve.wait_ge(*upto("q_flag", 1))
            unsorted = dve.value_load(q_flag, min_val=0, max_val=1)
            with dve.If(unsorted > 0):
                dve.tensor_scalar(q_tri, iota[0:EROWS, 0:EROWS], blk_f[0:EROWS, 0:1], None, ALU.is_gt).then_inc(sem("q_start"), 1)
                dve.memset(q_base, -1.0).then_inc(sem("q_start"), 1)
                dve.memset(q_pos, 0.0).then_inc(sem("q_start"), 1)
                dve.wait_ge(*upto("q_start", 3))
                for w in target_windows(dve):
                    if due(w):
                        dve.wait_ge(*upto("q_pos", w))
                    dve.tensor_scalar(q_mask, e_win, col(iota[0:EROWS, :], w), None, ALU.is_equal).then_inc(sem("q_mask"), 1)
                    dve.wait_ge(*upto("q_mask", w + 1))
                    dve.tensor_tensor_scan(q_pre, q_mask, q_mask, 0.0, ALU.add, ALU.max).then_inc(sem("q_pre"), 1)
                    dve.wait_ge(*upto("q_offs_mm", w + 1))
                    dve.tensor_tensor(q_offs, bank[5][0:EROWS, 0:1], q_base, ALU.add).then_inc(sem("q_offs"), 1)
                    dve.wait_ge(*upto("q_offs", w + 1))
                    dve.tensor_tensor(q_base, q_base, bank[5][0:EROWS, 1:2], ALU.add).then_inc(sem("q_base"), 1)
                    dve.scalar_tensor_tensor(q_pre, q_pre, q_offs, q_mask, ALU.add, ALU.mult).then_inc(sem("q_part"), 1)
                    dve.wait_ge(*upto("q_part", w + 1))
                    dve.wait_ge(*upto("q_base", w + 1))
                    dve.tensor_tensor(q_pos, q_pos, q_pre, ALU.add).then_inc(sem("q_pos"), 1)
                dve.wait_ge(*upto("q_pos", NT))
                dve.tensor_copy(q_posi, q_pos).then_inc(sem("q_posi"), 1)
            dve.wait_ge(*upto("rows_in", 32))
            chain(dve.tensor_scalar(r_int, r_word, 16, None, ALU.logical_shift_right))
            chain(dve.tensor_copy(r_dst, r_int))
            r_first = r_int.rearrange("t (b e) -> t b e", b=TB)[:, :, 0]
            chain(dve.tensor_scalar(r_w0i, r_first, 7, None, ALU.logical_shift_right))
            chain(dve.tensor_copy(r_w0, r_w0i))
            chain(dve.tensor_scalar(r_w1i, r_next, 23, None, ALU.logical_shift_right))
            chain(dve.tensor_copy(r_w1, r_w1i))
            chain(dve.tensor_scalar(r_int, r_word, 0xFFFF, None, ALU.bitwise_and))
            chain(dve.tensor_copy(r_idx, r_int))
            for b_ in range(TB):
                cols = slice(P * b_, P * b_ + P)
                chain(dve.tensor_scalar(r_dl[:, cols], r_w0[:, b_:b_ + 1].broadcast_to([P, P]), -float(P), None, ALU.mult))
                chain(dve.tensor_tensor(r_dl[:, cols], r_dl[:, cols], r_dst[:, cols], ALU.add))
                sc = slice((NT - 1) * b_, (NT - 1) * (b_ + 1))
                dve.tensor_scalar(r_sel[:, sc], iota[:, 1:NT], r_w0[:, b_:b_ + 1], None, ALU.is_gt).then_inc(sem("sel"), 1)
                dve.tensor_scalar(r_sel2[:, sc], iota[:, 1:NT], r_w1[:, b_:b_ + 1], None, ALU.is_gt).then_inc(sem("sel"), 1)
            dve.wait_ge(*upto("sel", 2 * TB))
            dve.tensor_tensor(r_sel, r_sel, r_sel2, ALU.subtract).then_inc(sem("rows_ready"), 1)
            dve.tensor_scalar(x_base, iota[:, 1:NT], float(P), None, ALU.mult).then_inc(sem("x_base"), 1)
            for b_ in range(TB):
                n_ = min(P, ET - P * b_)
                cols = slice(P * b_, P * b_ + n_)
                if due(3 * b_ + 3):
                    dve.wait_ge(*upto("tables_mm", 3 * b_ + 3))
                dve.tensor_copy(dl_t[:, cols], bank[b_ % 2][:, 0:n_]).then_inc(sem("tables"), 1)
                dve.tensor_copy(idx_t[:, cols], bank[b_ % 2][:, P:P + n_]).then_inc(sem("tables"), 1)
                dve.tensor_copy(win[:, cols], bank[b_ % 2][0:1, 2 * P:2 * P + n_]).then_inc(sem("tables"), 1)
            cols = slice(ET, ET + NT - 1)
            dve.wait_ge(*upto("extra_mm", 2))
            dve.wait_ge(*upto("x_base", 1))
            dve.tensor_tensor(dl_t[:, cols], bank[2][:, 0:NT - 1], x_base, ALU.subtract).then_inc(sem("tables"), 1)
            dve.tensor_copy(idx_t[:, cols], bank[3][:, 0:NT - 1]).then_inc(sem("tables"), 1)
            dve.tensor_copy(win[:, cols], iota[0:1, 1:NT]).then_inc(sem("tables"), 1)
            dve.wait_ge(*upto("tables", 3 * TB + 3))
            dve.wait_ge(*upto("table_pad", 3))
            chain(dve.tensor_scalar(cnt_at[:, :], win[:, :], 3, None, ALU.logical_shift_left))
            ti = typ_t[:, :].bitcast(I32)
            chain(dve.tensor_scalar(ti, idx_t[:, :], 7, None, ALU.bitwise_and))
            chain(dve.tensor_copy(typ_t[:, :], ti))
            if phase_end(dve):
                return
            dve.wait_ge(*upto("w0_in", 16 * 9))
            for k in range(KC):
                dve.tensor_scalar(wg1[:, k, :], wg1_raw[:, k, :], lng[:, k:k + 1], None, ALU.mult).then_inc(sem("gate_w"), 1)
                dve.tensor_copy(lnb_b[:, k, :], lnb[:, k:k + 1].broadcast_to([P, P])).then_inc(sem("gate_w"), 1)
            dve.wait_ge(*upto("gate_w_mm", 2))
            chain(dve.tensor_copy(wg1_sum, bank[7][:, 0:64]))
            dve.tensor_tensor(gate_b, bank[6][:, 0:64], bg1_b, ALU.add).then_inc(sem("gate_b"), 1)
            dve.wait_ge(*upto("gate_b", 1))

            def variance(pre, src_, st, mv_, ve, t, ready):
                dve.wait_ge(*upto(*ready))
                dve.bn_stats(st, src_).then_inc(sem(pre + "_st"), 1)
                dve.wait_ge(*upto(pre + "_st", t + 1))
                alone(dve)
                dve.bn_aggr(mv_, st).then_inc(sem(pre + "_ag"), 1)
                dve.wait_ge(*upto(pre + "_ag", t + 1))
                dve.tensor_scalar(ve, mv_[:, 1:2], EPS, None, ALU.add).then_inc(sem(pre + "_var"), 1)

            def one_hots(v, wide, values, g):
                return dve.tensor_tensor(v, iota[:, 0:wide].unsqueeze(1).broadcast_to([P, GRP, wide]),
                                         span(values, g * GRP, GRP).unsqueeze(2).broadcast_to([P, GRP, wide]), ALU.is_equal)

            def to_count(t, ks):
                for k in ks:
                    g = t * CPT + k
                    if due(g - CPT + 1):
                        dve.wait_ge(*upto("ct_mm", g - CPT + 1))
                    one_hots(c_oh[k], P, dl_t, g).then_inc(sem("ct_oh"), 1)
                    one_hots(c_toh[k], R, typ_t, g).then_inc(sem("ct_oh"), 1)

            dve.memset(zerob, 0.0).then_inc(sem("zerob"), 1)
            for t, s, n in skewed(dve):
                if t[0] is not None:
                    t_, s_, n_ = t
                    variance("n0", xin[s_], stats[s_], mv[s_], veps[s_][:, 0:1], t_, (f"n0_in{s_}", 16 * (n_ + 1)))
                    to_count(t_, (0, 1))
                    dve.wait_ge(*upto("n0_rstd", t_ + 1))
                    if due(t_ - 1):
                        dve.wait_ge(*upto("n0_t", t_ - 1))
                    dve.tensor_scalar(xn[s_][:, 0:C], xin[s_], mv[s_][:, 0:1], rstd[s_][:, 0:1], ALU.subtract, ALU.mult).then_inc(sem("n0_xn"), 1)
                    to_count(t_, (2, 3))
                    dve.wait_ge(*upto("n0_xn", t_ + 1))
                    dve.bn_stats(gstats[s_], xn[s_][:, 0:C]).then_inc(sem("n0_gst"), 1)
                    dve.wait_ge(*upto("n0_gst", t_ + 1))
                    alone(dve)
                    dve.bn_aggr(gmv[s_], gstats[s_]).then_inc(sem("n0_gag"), 1)
                    dve.wait_ge(*upto("n0_gag", t_ + 1))
                    dve.tensor_scalar(gveps[s_], gmv[s_][:, 1:2], EPS, None, ALU.add).then_inc(sem("n0_gvar"), 1)
                if s[0] is not None:
                    t_, s_, n_ = s
                    if due(16 * n_):
                        dve.wait_ge(*upto(f"n0_y_out{s_}", 16 * n_))
                    for b_ in (1, 3):
                        dve.wait_ge(*upto(f"n0_y_mm{b_}", t_ + 1))
                        dve.tensor_copy(ysb[s_][:, 512 * b_:512 * b_ + 512], bank[b_][:, :]).then_inc(sem("n0_y_dve"), 1)
                        if b_ == 1 and t[0] is not None:
                            to_count(t[0], (4, 5))
                    dve.wait_ge(*upto("n0_root_mm", t_ + 1))
                    dve.tensor_tensor(at(acc, t_), bank[5][:, 0:C], bias0_b, ALU.add).then_inc(sem("n0_root"), 1)
                    dve.wait_ge(*upto("n0_grstd", t_ + 1))
                    dve.scalar_tensor_tensor(g_a[s_], wg1_sum, gmv[s_][:, 0:1], bank[5][:, C:C + 64], ALU.mult, ALU.subtract).then_inc(sem("n0_ga"), 1)
                    dve.wait_ge(*upto("n0_ga", t_ + 1))
                    if due(t_ - 1):
                        dve.wait_ge(*upto("n0_hg", t_ - 1))
                    dve.scalar_tensor_tensor(g_b[s_], g_a[s_], grstd[s_], gate_b, ALU.mult, ALU.subtract).then_inc(sem("n0_gate"), 1)
                    if t[0] is not None:
                        to_count(t[0], (6, 7))
                    dve.wait_ge(*upto("n0_km_mm", t_ + 1))
                    dve.tensor_reduce(at(kmax, t_), bank[6][:, 0:C].rearrange("p (k n) -> p k n", k=KC)[:, :, 0:rows_of(t_)],
                                      AX, ALU.max).then_inc(sem("n0_km"), 1)
                elif t[0] is not None:
                    to_count(t[0], (4, 5, 6, 7))
            for g in range(NT * CPT, NG):
                to_count(g // CPT, (g % CPT,))
            dve.wait_ge(*upto("n0_km", NT))
            dve.tensor_reduce(kmax1, kmax.rearrange("p t k -> p k t"), AX, ALU.max).then_inc(sem("kmax"), 1)
            dve.wait_ge(*upto("kmax_mm", 1))
            dve.tensor_scalar(negmax, bank[0][0:1, 0:C], -1.0, None, ALU.mult).then_inc(sem("negmax"), 1)
            dve.wait_ge(*upto("ct_mm", NG))
            chain(dve.tensor_copy(cnt[:, :, :], bank[7][:, 0:NT * R].rearrange("p (w r) -> p w r", r=R)))
            chain(dve.tensor_reduce(rdeg[:, :], cnt[:, :, :], AX, ALU.add))
            chain(dve.tensor_scalar(rdeg[:, :], rdeg[:, :], 1.0, None, ALU.max))
            chain(dve.reciprocal(rdeg[:, :], rdeg[:, :]))
            chain(dve.tensor_scalar(cnt[:, :, :], cnt[:, :, :], 1.0, None, ALU.max))
            chain(dve.reciprocal(cnt[:, :, :], cnt[:, :, :]))
            rest = cnt[:, :, :]
            for k in range(3):
                part = rc3[:, :, R * k:R * k + R]
                chain(dve.tensor_copy(part, rest))
                if k < 2:
                    chain(dve.tensor_copy(rc_part, part))
                    chain(dve.tensor_tensor(rc_rest, rest, rc_part, ALU.subtract))
                    rest = rc_rest
            if phase_end(dve):
                return

            def add_sum(pre, g, ws, j):
                if isinstance(g, int) and g < 0:
                    return
                if j % 2 == 0:
                    dve.wait_ge(*upto(pre + "_sum_mm", 2 * g + 1 + j // 2))
                if due(g * GRP + j):
                    dve.wait_ge(*upto(pre + "_add", g * GRP + j))
                dve.tensor_tensor(at(acc, ws[j]), at(acc, ws[j]), bank[j // 2][:, C * (j % 2):C * (j % 2) + C],
                                  ALU.add).then_inc(sem(pre + "_add"), 1)

            def sum_windows(i):
                if isinstance(i, int) and i == 0:
                    return [None] * GRP + windows(dve, 0, BODY - GRP)
                return windows(dve, i * BODY - GRP, BODY)

            def targets(g, h):
                if due(g - BPB + 1):
                    dve.wait_ge(*upto("g0_oht_mm", g - BPB + 1))
                    dve.wait_ge(*upto("g0_woh", g - BPB + 1))
                one_hots(ohb[h], P, dl_t, g).then_inc(sem("g0_oh"), 1)

            def relations(g, h):
                if due(g - BPB + 1):
                    dve.wait_ge(*upto("g0_wsel", g - BPB + 1))
                one_hots(tohb[h], R, typ_t, g).then_inc(sem("g0_toh"), 1)

            def select(g, h):
                b_ = h % 2
                dve.wait_ge(*upto("g0_toh", g + 1))
                dve.wait_ge(*upto("g0_look_mm", g + 1))
                if due(g - 1):
                    dve.wait_ge(*upto("g0_wgt", g - 1))
                dve.tensor_tensor(wsel[b_], tohb[h].unsqueeze(2).broadcast_to([P, GRP, 3, R]),
                                  bank[7][:, 0:GRP * 3 * R].rearrange("p (j k n) -> p j k n", j=GRP, k=3), ALU.mult).then_inc(sem("g0_wsel"), 1)

            def weights(g, h):
                b_ = h % 2
                dve.wait_ge(*upto("g0_wsel", g + 1))
                if due(g - 1):
                    dve.wait_ge(*upto("g0_woh", g - 1))
                dve.tensor_reduce(wgt[b_], wsel[b_].rearrange("p j k n -> p j (k n)"), AX, ALU.add).then_inc(sem("g0_wgt"), 1)
                dve.wait_ge(*upto("g0_wgt", g + 1))
                if due(g - 1):
                    dve.wait_ge(*upto("g0_sum_mm", 2 * (g - 1)))
                dve.tensor_tensor(woh[b_], ohb[h], wgt[b_].unsqueeze(2).broadcast_to([P, GRP, P]), ALU.mult).then_inc(sem("g0_woh"), 1)

            for g in range(3):
                targets(g, g)
                relations(g, g)
            select(0, 0)
            weights(0, 0)

            def mixer_keys(m, h):
                if h == 1:
                    dve.wait_ge(*upto("m1_v_mm", m + 1))
                    if due(m):
                        dve.wait_ge(*upto("m1_ctx_mm", m))
                    dve.tensor_copy(m_v.rearrange("p (k n) -> p k n", k=KC)[:, :, 0:P],
                                    bank[5][:, 0:C].rearrange("p (k n) -> p k n", k=KC)).then_inc(sem("m1_v"), 1)

            def mixer_context(h):
                if h == 0:
                    dve.wait_ge(*upto("m1_ctx_mm", NT))
                    for k in range(KC):
                        chain(dve.reciprocal(cden[:, k:k + 1], bank[2 + k][:, P:P + 1]))
                        chain(dve.tensor_scalar(bdc[:, k, :], bank[2 + k][:, 0:P], cden[:, k:k + 1], None, ALU.mult))
                        dve.tensor_tensor(bdc[:, k, :], bdc[:, k, :], bd32[:, :], ALU.mult).then_inc(sem("m_bdc"), 1)
                if h == 2:
                    dve.wait_ge(*upto("m_qc_mm", 2))
                    for k in range(KC):
                        dve.tensor_copy(w_qc[:, k, :], bank[4 + k][:, 0:C]).then_inc(sem("m_qc"), 1)

            def mixer_queries(m, h):
                r = rows_of(m)
                if h == 0:
                    dve.wait_ge(*upto("m2_in", 48 * (m + 1)))
                    if due(m):
                        dve.wait_ge(*upto("m2_out", m))
                    dve.tensor_tensor(m_xb[0:r, :], m_x[0:r, :], bproj_b[0:r, :], ALU.add).then_inc(sem("m2_xb"), 1)
                if h == 1:
                    dve.wait_ge(*upto("m2_sig", m + 1))
                    if due(m):
                        dve.wait_ge(*upto("m2_prt_mm", m))
                    dve.tensor_tensor(m_pr, m_sig, bank[4][:, 0:C], ALU.mult).then_inc(sem("m2_pr"), 1)
                if h == 3:
                    dve.wait_ge(*upto("m2_f_mm", m + 1))
                    dve.wait_ge(*upto("m2_xb", m + 1))
                    if due(m):
                        dve.wait_ge(*upto("m2_st", 16 * m))
                    dve.tensor_tensor(m_out, m_xb, bank[3][:, 0:C], ALU.add).then_inc(sem("m2_out"), 1)

            for k in range(KC):
                c_ = (P + 1) * k + P
                dve.memset(m_v[:, c_:c_ + 1], 1.0).then_inc(sem("m1_ones"), 1)
            for i, m1, m2 in gather_bodies(dve):
                ws = sum_windows(i)
                for h in range(BPB):
                    g = i * BPB + h
                    w4 = ws[GRP * h:GRP * h + GRP]
                    add_sum("g0", g - 1, w4, 0)
                    relations(g + 3, (h + 3) % BPB)
                    add_sum("g0", g - 1, w4, 1)
                    targets(g + 3, (h + 3) % BPB)
                    add_sum("g0", g - 1, w4, 2)
                    select(g + 1, (h + 1) % BPB)
                    add_sum("g0", g - 1, w4, 3)
                    weights(g + 1, (h + 1) % BPB)
                    if m1 is not None:
                        mixer_keys(m1, h)
                    if between(i):
                        mixer_context(h)
                    if m2 is not None:
                        if h == 0:
                            dve.wait_ge(*upto("w_mix_in", 80))
                        mixer_queries(m2, h)
            w4 = windows(dve, T - GRP, GRP)
            for j in range(GRP):
                add_sum("g0", NG - 1, w4, j)
            dve.wait_ge(*upto("g0_idx", NG + BPB))
            chain(dve.tensor_scalar(idx_t[:, :], idx_t[:, :], 3, None, ALU.logical_shift_right))
            if phase_end(dve):
                return
            dve.wait_ge(*upto("w_ffn_in", 16 * 23))
            chain(dve.tensor_scalar(rtemp_r, temp_c, 0.1, 5.0, ALU.max, ALU.min))
            dve.reciprocal(rtemp_r, rtemp_r).then_inc(sem("rtemp"), 1)
            dve.wait_ge(*upto("rtemp", 1))
            dve.wait_ge(*upto("wl_mm", 4))
            chain(dve.tensor_copy(rtemp_b, bank[2][:, 0:8]))
            for k in range(KC):
                dve.tensor_tensor(heads(w_log[:, k, :]), heads(bank[k][:, :]), rtemp_b.unsqueeze(2).broadcast_to([P, 8, 64]), ALU.mult).then_inc(sem("w_log"), 1)
            chain(dve.tensor_tensor(b_log, bank[3][0:1, :], bslice8, ALU.add))
            dve.tensor_tensor(heads(b_log), heads(b_log), rtemp_r.unsqueeze(2).broadcast_to([1, 8, 64]), ALU.mult).then_inc(sem("w_log"), 1)
            for (t, s, n), (tb, sb_, nb), (t_, s_, n_) in staged(dve):
                if t_ is not None:
                    lg = bank[1 + s_]
                    dve.wait_ge(*upto("f1_l_mm", t_ + 1))
                    if due(t_ - 1):
                        dve.wait_ge(*upto("f1_lg", t_ - 1))
                    dve.tensor_reduce(a_max[s_], heads(lg[:, :]), AX, ALU.max).then_inc(sem("f1_mx"), 1)
                    dve.wait_ge(*upto("f1_mx", t_ + 1))
                    if due(t_ - 1):
                        dve.wait_ge(*upto("f1_ex", t_ - 1))
                    dve.tensor_tensor(heads(a_lg[s_]), heads(lg[:, :]), a_max[s_].unsqueeze(2).broadcast_to([P, 8, 64]), ALU.subtract).then_inc(sem("f1_lg"), 1)
                if tb is not None:
                    dve.wait_ge(*upto("f1_rstd", tb + 1))
                    if due(tb - 1):
                        dve.wait_ge(*upto("f1_t", tb - 1))
                        dve.wait_ge(*upto("f1_u_mm", tb - 1))
                    dve.tensor_scalar(a_xn[sb_][:, 0:C], a_x1[sb_], a_mv[sb_][:, 0:1], a_rstd[sb_], ALU.subtract, ALU.mult).then_inc(sem("f1_xn"), 1)
                if t is not None:
                    dve.wait_ge(*upto(f"f1_in{s}", 16 * (n + 1)))
                    if due(16 * n):
                        dve.wait_ge(*upto(f"f1_x1_out{s}", 16 * n))
                        dve.wait_ge(*upto("f1_xn", t - 1))
                    dve.scalar_tensor_tensor(a_x1[s], at(acc, t), 0.0, a_xin[s], ALU.max, ALU.add).then_inc(sem("f1_x1"), 1)
                    variance("f1", a_x1[s], a_stats[s], a_mv[s], a_veps[s], t, ("f1_x1", t + 1))
                if t_ is not None:
                    dve.wait_ge(*upto("f1_ex", t_ + 1))
                    dve.tensor_reduce(a_sum[s_], heads(a_ex[s_]), AX, ALU.add).then_inc(sem("f1_sm"), 1)
                    dve.wait_ge(*upto("f1_sm", t_ + 1))
                    dve.reciprocal(a_rsum[s_], a_sum[s_]).then_inc(sem("f1_rs"), 1)
                    dve.wait_ge(*upto("f1_rs", t_ + 1))
                    if due(t_ - 1):
                        dve.wait_ge(*upto("f1_swt_mm", t_ - 1))
                        dve.wait_ge(*upto("f1_u_mm", t_ - 1))
                    dve.tensor_tensor(heads(a_sw[s_]), heads(a_ex[s_]), a_rsum[s_].unsqueeze(2).broadcast_to([P, 8, 64]), ALU.mult).then_inc(sem("f1_sw"), 1)
            four = range(4)
            blk = lambda v, j: v[:, P * j:P * j + P]
            dve.wait_ge(*upto("f1_u_mm", NT))
            for j in four:
                dve.tensor_copy(f_u[:, j, :], bank[4 + j][:, 0:257]).then_inc(sem("fs_u"), 1)
            dve.wait_ge(*upto("fs_u", 4))
            chain(dve.tensor_scalar(f_den, f_u[:, :, 256], EPS, None, ALU.add))
            chain(dve.reciprocal(f_rden, f_den))
            dve.wait_ge(*upto("fs_ut_mm", 2))
            for k in range(KC):
                dve.tensor_copy(f_ut[:, k, :], bank[k][:, :]).then_inc(sem("fs_ut"), 1)
            dve.wait_ge(*upto("fs_tok_mm", 1))
            for j in four:
                chain(dve.scalar_tensor_tensor(blk(f_tok, j), blk(bfx_b, j), f_u[:, j, 256:257], blk(bank[2], j), ALU.mult, ALU.add))
                dve.scalar_tensor_tensor(blk(f_tok2, j), blk(f_tok, j), f_rden[:, j:j + 1], bd64[:, :], ALU.mult, ALU.mult).then_inc(sem("fs_tok"), 1)
            dve.wait_ge(*upto("fs_tokt_mm", 1))
            dve.tensor_copy(f_tokt, bank[0][:, :]).then_inc(sem("fs_tokt"), 1)
            dve.wait_ge(*upto("fs_qkv_mm", 3))
            for v, b_ in ((f_qt, 1), (f_kt, 2), (f_v, 4)):
                dve.tensor_copy(v, bank[b_][:, :]).then_inc(sem("fs_qkv"), 1)
            dve.wait_ge(*upto("fs_s_mm", 1))
            for j in four:
                chain(dve.scalar_tensor_tensor(blk(f_s, j), blk(bank[5], j), 64 ** -0.5, off64[:, :], ALU.mult, ALU.add))
                dve.tensor_reduce(f_max[:, j:j + 1], blk(f_s, j), AX, ALU.max, negate=True).then_inc(sem("fs_max"), 1)
            dve.wait_ge(*upto("fs_exp", 4))
            chain(dve.reciprocal(f_rsum, f_sum))
            for j in four:
                dve.tensor_scalar(blk(f_s, j), blk(f_s2, j), f_rsum[:, j:j + 1], None, ALU.mult).then_inc(sem("fs_a"), 1)
            dve.wait_ge(*upto("fs_at_mm", 1))
            dve.tensor_copy(f_at, bank[0][:, :]).then_inc(sem("fs_at"), 1)
            dve.wait_ge(*upto("fs_ost_mm", 1))
            dve.tensor_copy(f_ost, bank[1][:, :]).then_inc(sem("fs_ost"), 1)
            dve.wait_ge(*upto("fs_m_mm", 4))
            for j in four:
                dve.tensor_copy(f_m[:, j, :], bank[4 + j][:, 0:C]).then_inc(sem("fs_m"), 1)
            dve.wait_ge(*upto("fs_m", 4))
            if phase_end(dve):
                return
            for (t, s, n), (t_, s_, n_), _ in staged(dve):
                if t_ is not None:
                    dve.wait_ge(*upto("f2_rstd", t_ + 1))
                    if due(t_ - 1):
                        dve.wait_ge(*upto("f2_t", t_ - 1))
                        dve.wait_ge(*upto(f"f2_xn_out{s_}", 16 * n_))
                    dve.tensor_scalar(a_xn[s_][:, 0:C], k_x2[s_], a_mv[s_][:, 0:1], a_rstd[s_], ALU.subtract, ALU.mult).then_inc(sem("f2_xn"), 1)
                if t is not None:
                    dve.wait_ge(*upto(f"f2_in{s}", 32 * (n + 1)))
                    dve.wait_ge(*upto("f2_o_mm", t + 1))
                    if due(16 * n):
                        dve.wait_ge(*upto(f"f2_x2_out{s}", 16 * n))
                        dve.wait_ge(*upto("f2_xn", t - 1))
                    dve.tensor_tensor(k_x2[s], k_x1[s], bank[s][:, 0:C], ALU.add).then_inc(sem("f2_x2"), 1)
                    variance("f2", k_x2[s], a_stats[s], a_mv[s], a_veps[s], t, ("f2_x2", t + 1))
            dve.memset(acc[:, :, :], 0.0)
            if phase_end(dve):
                return
            def targets1(g, h):
                if due(g - 1):
                    dve.wait_ge(*upto("g1_sum_mm", 2 * (g - 1)))
                one_hots(oh[h % 2], P, dl_t, g).then_inc(sem("g1_oh"), 1)

            targets1(0, 0)
            dve.wait_ge(*upto("w_kv_in", 16))
            for k in range(KC):
                chain(dve.tensor_reduce(kv_mean[:, k, :], heads(w_kv1[:, k, :], 16), AX, ALU.add))
                chain(dve.tensor_scalar(kv_mean[:, k, :], kv_mean[:, k, :], 1.0 / 64, None, ALU.mult))
                dve.tensor_tensor(heads(w_kv1[:, k, :], 16), heads(w_kv1[:, k, :], 16),
                                  kv_mean[:, k, :].unsqueeze(2).broadcast_to([P, 16, 64]), ALU.subtract).then_inc(sem("w_kv"), 1)

            def keys_values(m, h, k):
                if (h, k) == (2, 0):
                    dve.wait_ge(*upto("kv_sqk", m + 1))
                    dve.wait_ge(*upto("kv_sqv", m + 1))
                    if due(m):
                        dve.wait_ge(*upto("kv_v1", m))
                    dve.tensor_reduce(k_ss, heads(k_sq, 16), AX, ALU.add).then_inc(sem("kv_ss"), 1)
                if (h, k) == (2, 1):
                    dve.wait_ge(*upto("kv_ss", m + 1))
                    if due(m):
                        dve.wait_ge(*upto("kv_pv", m))
                    dve.tensor_scalar(k_v1, k_ss, 1.0 / 64, EPS, ALU.mult, ALU.add).then_inc(sem("kv_v1"), 1)
                if (h, k) == (2, 2):
                    dve.wait_ge(*upto("kv_v1", m + 1))
                    if due(m):
                        dve.wait_ge(*upto("kv_n2", m))
                        dve.wait_ge(*upto("kv_root", m))
                    dve.tensor_tensor(k_pv, k_v1[:, 0:8], k_v1[:, 8:16], ALU.mult).then_inc(sem("kv_pv"), 1)
                if (h, k) == (3, 0):
                    dve.wait_ge(*upto("kv_root", m + 1))
                    if due(m):
                        dve.wait_ge(*upto("kv_krs", m))
                    dve.reciprocal(k_inv, k_root).then_inc(sem("kv_inv"), 1)
                if (h, k) == (3, 1):
                    dve.wait_ge(*upto("kv_inv", m + 1))
                    dve.tensor_tensor(k_n[0], k_inv, k_inv, ALU.mult).then_inc(sem("kv_n1"), 1)
                if (h, k) == (3, 2):
                    dve.wait_ge(*upto("kv_n1", m + 1))
                    dve.tensor_tensor(k_n[1], k_n[0], k_pv, ALU.mult).then_inc(sem("kv_n2"), 1)
                if (h, k) == (3, 3):
                    dve.wait_ge(*upto("kv_n2", m + 1))
                    dve.tensor_scalar(k_n[2], k_n[1], -0.5, 1.5, ALU.mult, ALU.add).then_inc(sem("kv_n3"), 1)
                if (h, k) == (3, 4):
                    dve.wait_ge(*upto("kv_n3", m + 1))
                    if due(m):
                        dve.wait_ge(*upto("kv_kn", m))
                    dve.tensor_tensor(k_rs, k_inv, k_n[2], ALU.mult).then_inc(sem("kv_krs"), 1)
                    dve.wait_ge(*upto("kv_krs", m + 1))
                    if due(m):
                        dve.wait_ge(*upto("kv_dots_mm", m))
                    dve.tensor_tensor(heads(k_kn), heads(bank[2][:, :]), k_rs.unsqueeze(2).broadcast_to([P, 8, 64]), ALU.mult).then_inc(sem("kv_kn"), 1)

            for i, m1, m2 in gather_bodies(dve):
                ws = sum_windows(i)
                for h in range(BPB):
                    g = i * BPB + h
                    w4 = ws[GRP * h:GRP * h + GRP]
                    beside = (lambda k: None) if m1 is None else (lambda k: keys_values(m1, h, k))
                    add_sum("g1", g - 1, w4, 0)
                    beside(0)
                    add_sum("g1", g - 1, w4, 1)
                    targets1(g + 1, h + 1)
                    beside(1)
                    add_sum("g1", g - 1, w4, 2)
                    beside(2)
                    add_sum("g1", g - 1, w4, 3)
                    beside(3)
                    beside(4)
            w4 = windows(dve, T - GRP, GRP)
            for j in range(GRP):
                add_sum("g1", NG - 1, w4, j)
            dve.wait_ge(*upto("w_l1_in", 16 * 7))
            dve.tensor_tensor(b_comb, b_self, b_out1, ALU.add).then_inc(sem("b_comb"), 1)
            for j in four:
                chain(dve.tensor_tensor(blk(d_bd, j), bank[4 + j][:, 0:P], bd64[:, :], ALU.mult))
            dve.tensor_scalar(d_bd, d_bd, 1.0 / N, None, ALU.mult).then_inc(sem("d_bd"), 1)
            dve.wait_ge(*upto("d_t1_mm", 4))
            for j in four:
                dve.tensor_copy(d_t1[:, j, :], bank[j][:, 0:C]).then_inc(sem("d_t1"), 1)
            dve.wait_ge(*upto("d_f_mm", 2))
            for k in range(KC):
                dve.tensor_tensor(w_comb[:, k, :], bank[4 + k][:, 0:C], w_self[:, k, :], ALU.add).then_inc(sem("w_comb"), 1)
            if phase_end(dve):
                return
            for (t, s, n), (tb, sb_, nb), (t_, s_, n_) in staged(dve):
                if t_ is not None:
                    dve.wait_ge(*upto("c_rstd", t_ + 1))
                    if due(t_ - 1):
                        dve.wait_ge(*upto("c_x4_t", t_ - 1))
                        dve.wait_ge(*upto("c_x34", t_ - 1))
                    dve.tensor_scalar(c_xn[s_], c_x3[s_], c_mv[s_][:, 0:1], c_rstd[s_], ALU.subtract, ALU.mult).then_inc(sem("c_xn"), 1)
                if t is not None:
                    if due(t - 1):
                        dve.wait_ge(*upto("c_hn_t", t - 1))
                    dve.tensor_scalar(c_hn[s], at(acc, t), col(rdeg, t), None, ALU.mult).then_inc(sem("c_hn"), 1)
                if t_ is not None:
                    dve.wait_ge(*upto("c_xn", t_ + 1))
                    if due(16 * n_):
                        dve.wait_ge(*upto(f"c_x34_out{s_}", 16 * n_))
                    dve.tensor_tensor(c_x34[s_], c_x3[s_], c_xn[s_], ALU.add).then_inc(sem("c_x34"), 1)
                if tb is not None:
                    dve.wait_ge(*upto(f"c_in{sb_}", 32 * (nb + 1)))
                    dve.wait_ge(*upto("c_x_mm", tb + 1))
                    if due(tb - 1):
                        dve.wait_ge(*upto("c_x34", tb - 1))
                    dve.tensor_tensor(c_x3[sb_], c_x2[sb_], bank[1][:, 0:C], ALU.add).then_inc(sem("c_x3"), 1)
                    variance("c", c_x3[sb_], c_stats[sb_], c_mv[sb_], c_veps[sb_], tb, ("c_x3", tb + 1))
                if t_ is not None:
                    dve.wait_ge(*upto("c_r_mm", t_ + 1))
                    dve.tensor_copy(at(logits, t_), bank[3][:, 0:8]).then_inc(sem("c_r"), 1)
            dve.wait_ge(*upto("c_r", NT))
            big = [P, NT, 8]
            m_, s_, i_ = rb[0], rb[1], rb[2]
            iota8 = iota[:, 0:8].unsqueeze(1).broadcast_to(big)
            each = lambda v: v.unsqueeze(2).broadcast_to(big)
            chain(dve.tensor_reduce(m_, logits, AX, ALU.max))
            dve.tensor_tensor(ra[0], logits, each(m_), ALU.subtract).then_inc(sem("r_exp_in"), 1)
            dve.wait_ge(*upto("r_exp", 1))
            chain(dve.tensor_reduce(s_, ra[1], AX, ALU.add))
            chain(dve.reciprocal(s_, s_))
            chain(dve.tensor_tensor(ra[0], ra[1], each(s_), ALU.mult))
            chain(dve.tensor_copy(ra[1], ra[0]))
            for pick in range(2):
                chain(dve.tensor_reduce(rb[3 + pick], ra[1], AX, ALU.max))
                chain(dve.tensor_tensor(ra[2], ra[1], each(rb[3 + pick]), ALU.is_ge))
                chain(dve.tensor_scalar(ra[3], iota8, -1.0, 8.0, ALU.mult, ALU.add))
                chain(dve.tensor_tensor(ra[2], ra[2], ra[3], ALU.mult))
                chain(dve.tensor_reduce(i_, ra[2], AX, ALU.max))
                chain(dve.tensor_tensor(ra[2], ra[3], each(i_), ALU.is_equal))
                if pick == 0:
                    chain(dve.tensor_copy(comb, ra[2]))
                    chain(dve.scalar_tensor_tensor(ra[1], ra[2], -2.0, ra[1], ALU.mult, ALU.add))
                else:
                    chain(dve.tensor_tensor(comb, comb, ra[2], ALU.add))
            chain(dve.tensor_tensor(rb[5], rb[3], rb[4], ALU.add))
            chain(dve.tensor_scalar(rb[5], rb[5], 1e-12, None, ALU.max))
            chain(dve.reciprocal(rb[5], rb[5]))
            chain(dve.tensor_tensor(comb, comb, ra[0], ALU.mult))
            chain(dve.tensor_tensor(comb, comb, each(rb[5]), ALU.mult))
            if phase_end(dve):
                return
            for g, s, n, m in expert_groups(dve):
                cf = comb.rearrange("p t e -> p (t e)")
                if due(g - 1):
                    dve.wait_ge(*upto("s_ct_mm", g - 1))
                dve.tensor_copy(s_cg[s][:, 0:8 * m], span(cf, 32 * g if isinstance(g, int) else g * 32, 8 * m)).then_inc(sem("s_cg"), 1)
                dve.wait_ge(*upto(f"s_in{s}", 32 * (n + 1)))
                dve.wait_ge(*upto("s_cb_mm", g + 1))
                for j in range(m):
                    dve.tensor_tensor(s_o[s][:, j, :], s_o[s][:, j, :], bank[4 + j // 2][:, C * (j % 2):C * (j % 2) + C], ALU.add).then_inc(sem("s_base"), 1)
                dve.wait_ge(*upto("s_base", 4 * g + m))
                for e in range(8):
                    dve.wait_ge(*upto("s_y_mm", 8 * g + e + 1))
                    for j in range(m):
                        if due(32 * g + m * e + j - m + 1 if e else 0):
                            dve.wait_ge(*upto("s_acc", 32 * g + m * e + j - m + 1 if e else 0))
                        c_ = s_cg[s][:, 8 * j + e:8 * j + e + 1]
                        dve.scalar_tensor_tensor(s_o[s][:, j, :], bank[4 + j // 2][:, C * (j % 2):C * (j % 2) + C], c_,
                                                 s_o[s][:, j, :], ALU.mult, ALU.add).then_inc(sem("s_acc"), 1)
            phase_end(dve)

        @block.tensor
        def _(pe):
            mm = pe.matmul

            def transposes(dst_, src_, n_=KC):
                for k in range(n_):
                    last = pe.transpose(dst_[:, P * k:P * k + P], src_[:, P * k:P * k + P], ident[:, :])
                return last

            pe.wait_ge(*upto("q_viol", 1))
            for k, v in enumerate((e_win[:, 0:1], e_win[:, ECOLS - 1:ECOLS], q_viol)):
                last = mm(bank[5][0:1, EROWS * k:EROWS * (k + 1)], v, ident[0:EROWS, 0:EROWS], start=True, stop=True)
            last.then_inc(sem("q_rows_mm"), 1)
            pe.wait_ge(*upto("q_flag", 1))
            unsorted = pe.value_load(q_flag, min_val=0, max_val=1)
            with pe.If(unsorted > 0):
                pe.wait_ge(*upto("q_start", 3))
                for w in target_windows(pe):
                    pe.wait_ge(*upto("q_pre", w + 1))
                    if due(w):
                        pe.wait_ge(*upto("q_base", w))
                    total = q_pre[:, ECOLS - 1:ECOLS]
                    mm(bank[5][0:EROWS, 0:1], q_tri, total, start=True, stop=True)
                    mm(bank[5][0:EROWS, 1:2], ones[0:EROWS, 0:EROWS], total, start=True, stop=True).then_inc(sem("q_offs_mm"), 1)
            pe.wait_ge(*upto("rows_ready", 1))
            for b_ in range(TB):
                cols = slice(P * b_, P * b_ + P)
                if due(3 * (b_ - 1)):
                    pe.wait_ge(*upto("tables", 3 * (b_ - 1)))
                mm(bank[b_ % 2][:, 0:P], r_dl[:, cols], ident[:, :], start=True, stop=True).then_inc(sem("tables_mm"), 1)
                mm(bank[b_ % 2][:, P:2 * P], r_idx[:, cols], ident[:, :], start=True, stop=True).then_inc(sem("tables_mm"), 1)
                mm(bank[b_ % 2][0:1, 2 * P:3 * P], r_w0[:, b_:b_ + 1], ident[:, :], start=True, stop=True).then_inc(sem("tables_mm"), 1)
            for v, b2_ in ((r_dst, 2), (r_idx, 3)):
                for b_ in range(TB):
                    last = mm(bank[b2_][:, 0:NT - 1], v[:, P * b_:P * b_ + P], r_sel[:, (NT - 1) * b_:(NT - 1) * (b_ + 1)],
                              start=b_ == 0, stop=b_ == TB - 1)
                last.then_inc(sem("extra_mm"), 1)
            if phase_end(pe):
                return
            pe.wait_ge(*upto("gate_w", 4))
            for k in range(KC):
                last = mm(bank[7][:, 0:64], ones[:, :], wg1[:, k, :], start=k == 0, stop=k == KC - 1)
            last.then_inc(sem("gate_w_mm"), 1)
            for k in range(KC):
                last = mm(bank[6][:, 0:64], lnb_b[:, k, :], wg1_raw[:, k, :], start=k == 0, stop=k == KC - 1)
            last.then_inc(sem("gate_w_mm"), 1)
            pe.wait_ge(*upto("gate_b", 1))
            pe.wait_ge(*upto("zerob", 1))
            mm(bank[7][:, :], zerob[:, 0:P], zerob, start=True, stop=False, skip_group_check=True)

            def count(t, ks, ws):
                for k in ks:
                    g = t * CPT + k
                    pe.wait_ge(*upto("ct_oh", 2 * g + 2))
                    for j in range(GRP):
                        last = mm(bank[7][:, bass.ds(ws[GRP * (k - ks[0]) + j], R)],
                                  c_oh[k][:, j, :], c_toh[k][:, j, :], start=False, stop=False, skip_group_check=True)
                    last.then_inc(sem("ct_mm"), 1)

            def count_beside(t, ks):
                if t is not None:
                    count(t, ks, windows(pe, (t * CPT + ks[0]) * GRP, GRP * len(ks), cnt_at, (NT - 1) * R))

            for t, s, n in skewed(pe):
                tc = t[0]
                if s[0] is not None:
                    t_, s_, n_ = s
                    pe.wait_ge(*upto("n0_xnt", t_ + 1))
                    for b_ in range(4):
                        if b_ % 2:
                            if due(2 * t_ - 1 + b_ // 2):
                                pe.wait_ge(*upto("n0_y_dve", 2 * t_ - 1 + b_ // 2))
                        else:
                            if due(2 * t_ - 1 + b_ // 2):
                                pe.wait_ge(*upto("n0_y_act", 2 * t_ - 1 + b_ // 2))
                        for k in range(KC):
                            last = mm(bank[b_][:, :], xnt[s_][:, P * k:P * k + P], w_all[:, k, 512 * b_:512 * b_ + 512], start=k == 0, stop=k == KC - 1)
                        last.then_inc(sem(f"n0_y_mm{b_}"), 1)
                    if due(t_):
                        pe.wait_ge(*upto("n0_ga", t_))
                    for k in range(KC):
                        mm(bank[5][:, 0:C], xnt[s_][:, P * k:P * k + P], w_root[:, k, :], start=k == 0, stop=k == KC - 1)
                    for k in range(KC):
                        last = mm(bank[5][:, C:C + 64], xnt[s_][:, P * k:P * k + P], wg1[:, k, :], start=k == 0, stop=k == KC - 1)
                    last.then_inc(sem("n0_root_mm"), 1)
                if tc is not None:
                    t_, s_, n_ = t
                    pe.wait_ge(*upto("n0_xn", t_ + 1))
                    if s[0] is not None and due(s[0]):
                        pe.wait_ge(*upto("n0_hgt", s[0]))
                    transposes(bank[4], xn[s_]).then_inc(sem("n0_t"), 1)
                    count_beside(tc, (0, 1, 2, 3))
                if s[0] is not None:
                    t_, s_, n_ = s
                    if due(t_):
                        pe.wait_ge(*upto("n0_km", t_))
                    for m in range(KC):
                        for k in range(KC):
                            last = mm(bank[6][:, P * m:P * m + P], w_k0[:, k, P * m:P * m + P], xnt[s_][:, P * k:P * k + P], start=k == 0, stop=k == KC - 1)
                    last.then_inc(sem("n0_km_mm"), 1)
                count_beside(tc, (4, 5, 6, 7))
                if s[0] is not None:
                    t_, s_, n_ = s
                    pe.wait_ge(*upto("n0_hg", t_ + 1))
                    pe.wait_ge(*upto("n0_xnt", t_ + 1 if tc is None else t_ + 2))
                    alone(pe)
                    pe.transpose(bank[4][0:64, C:C + P], hg[s_], ident[:, :]).then_inc(sem("n0_hg_t"), 1)
            for g in range(NT * CPT, NG):
                count_beside(g // CPT, (g % CPT,))
            pe.wait_ge(*upto("kmax", 1))
            pe.wait_ge(*upto("n0_y_act", 2 * NT))
            for k in range(KC):
                last = mm(bank[0][0:1, P * k:P * k + P], kmax1[:, k:k + 1], ident[:, :], start=True, stop=True)
            last.then_inc(sem("kmax_mm"), 1)
            if phase_end(pe):
                return
            def sum_rows(pre, g, again, lhs, h):
                pe.wait_ge(*upto(f"{pre}_rows{h}", 16 * GRP * (again + 1)))
                for j in range(GRP):
                    if j % 2 == 0 and due(g):
                        pe.wait_ge(*upto(pre + "_add", GRP * (g - 1) + j + 2))
                    last = mm(bank[j // 2][:, C * (j % 2):C * (j % 2) + C], lhs[:, j, :], ring[GRP * h + j], start=True, stop=True)
                    if j % 2:
                        last.then_inc(sem(pre + "_sum_mm"), 1)

            def turn(g, h):
                pe.wait_ge(*upto("g0_oh", g + 1))
                if due(g):
                    pe.wait_ge(*upto("g0_oht", g))
                for j in range(GRP):
                    last = mm(bank[6][:, P * j:P * j + P], ohb[h][:, j, :], identb[:, :], start=True, stop=True)
                last.then_inc(sem("g0_oht_mm"), 1)

            def look(g, h, ws):
                pe.wait_ge(*upto("g0_oht", g + 1))
                if due(g):
                    pe.wait_ge(*upto("g0_wsel", g))
                for j in range(GRP):
                    last = mm(bank[7][:, 3 * R * j:3 * R * (j + 1)], oht[h % 2][:, P * j:P * j + P], at(rc3, ws[j]), start=True, stop=True)
                last.then_inc(sem("g0_look_mm"), 1)

            ws = windows(pe, 0, 2 * GRP)
            for g in range(2):
                turn(g, g)
                look(g, g, ws[GRP * g:GRP * g + GRP])
            def mixer_keys(m, h):
                if h == 0:
                    pe.wait_ge(*upto("m1_in", 16 * (m + 1)))
                    if due(m):
                        pe.wait_ge(*upto("m1_ek", m))
                    mm(bank[4][:, 0:C], ones[0:1, :], negmax, start=True, stop=False)
                    for k in range(KC):
                        last = mm(bank[4][:, 0:C], m_xnt[:, P * k:P * k + P], w_k0[:, k, :], start=False, stop=k == KC - 1)
                    last.then_inc(sem("m1_k_mm"), 1)
                    if due(m):
                        pe.wait_ge(*upto("m1_v", m))
                    for k in range(KC):
                        last = mm(bank[5][:, 0:C], m_xnt[:, P * k:P * k + P], w_v0[:, k, :], start=k == 0, stop=k == KC - 1)
                    last.then_inc(sem("m1_v_mm"), 1)
                if h == 2:
                    r = rows_of(m)
                    pe.wait_ge(*upto("m1_ek", m + 1))
                    pe.wait_ge(*upto("m1_v", m + 1))
                    pe.wait_ge(*upto("m1_ones", KC))
                    for k in range(KC):
                        last = mm(bank[2 + k][:, 0:P + 1], m_ek[0:r, P * k:P * k + P], m_v[0:r, (P + 1) * k:(P + 1) * (k + 1)],
                                  start=isinstance(m, int) and m == 0, stop=is_last(m), skip_group_check=True)
                    last.then_inc(sem("m1_ctx_mm"), 1)

            def mixer_context(h):
                if h == 1:
                    pe.wait_ge(*upto("w_mix_in", 80))
                    pe.wait_ge(*upto("m_bdc", KC))
                    pe.wait_ge(*upto("m1_v", NT))
                    for i_ in range(KC):
                        for j in range(KC):
                            last = mm(bank[4 + i_][:, P * j:P * j + P], w_qt[:, j, P * i_:P * i_ + P], bdc[:, j, :], start=True, stop=True)
                        last.then_inc(sem("m_qc_mm"), 1)

            def mixer_queries(m, h):
                if h == 0:
                    pe.wait_ge(*upto("m2_in", 48 * (m + 1)))
                    if not due(m):
                        pe.wait_ge(*upto("m_qc", KC))
                    if due(m):
                        pe.wait_ge(*upto("m2_pr", m))
                        pe.wait_ge(*upto("m2_sig", m))
                    for k in range(KC):
                        mm(bank[4][:, 0:C], m_xnt[:, P * k:P * k + P], w_qc[:, k, :], start=k == 0, stop=k == KC - 1)
                    mm(bank[5][:, 0:C], ones[0:1, :], bg2, start=True, stop=False)
                    mm(bank[5][:, 0:C], m_hgt, wg2, start=False, stop=True).then_inc(sem("m2_g_mm"), 1)
                if h == 2:
                    pe.wait_ge(*upto("m2_pr", m + 1))
                    if due(m):
                        pe.wait_ge(*upto("m2_prt", m))
                    transposes(bank[2], m_pr).then_inc(sem("m2_prt_mm"), 1)
                if h == 3:
                    pe.wait_ge(*upto("m2_prt", m + 1))
                    if due(m):
                        pe.wait_ge(*upto("m2_out", m))
                    for k in range(KC):
                        last = mm(bank[3][:, 0:C], m_prt[:, P * k:P * k + P], w_proj[:, k, :], start=k == 0, stop=k == KC - 1)
                    last.then_inc(sem("m2_f_mm"), 1)

            for i, m1, m2 in gather_bodies(pe):
                ws = windows(pe, i * BODY + 2 * GRP, BODY)
                for h in range(BPB):
                    g = i * BPB + h
                    turn(g + 2, (h + 2) % BPB)
                    pe.wait_ge(*upto("g0_woh", g + 1))
                    sum_rows("g0", g, i, woh[h % 2], h)
                    look(g + 2, h, ws[GRP * h:GRP * h + GRP])
                    if m1 is not None:
                        mixer_keys(m1, h)
                    if between(i):
                        mixer_context(h)
                    if m2 is not None:
                        mixer_queries(m2, h)
            if phase_end(pe):
                return
            pe.wait_ge(*upto("w_ffn_in", 16 * 23))
            pe.wait_ge(*upto("rtemp", 1))
            for i in range(KC):
                for j in range(4):
                    last = mm(bank[i][:, P * j:P * j + P], wx_t[:, j, P * i:P * i + P], wsl_bd, start=True, stop=True)
                last.then_inc(sem("wl_mm"), 1)
            mm(bank[2][:, 0:8], ones[0:1, :], rtemp_r, start=True, stop=True).then_inc(sem("wl_mm"), 1)
            for j in range(4):
                last = mm(bank[3][0:1, P * j:P * j + P], bx_c[:, j:j + 1], wsl_bd, start=True, stop=True)
            last.then_inc(sem("wl_mm"), 1)
            pe.wait_ge(*upto("w_log", 3))
            pe.wait_ge(*upto("a_ones", 2))
            for _, (t, s, n), (t_, s_, n_) in staged(pe):
                if t is not None:
                    pe.wait_ge(*upto("f1_xn", t + 1))
                    if due(t):
                        pe.wait_ge(*upto("f1_xnt", t))
                    transposes(bank[0], a_xn[s]).then_inc(sem("f1_t"), 1)
                    if due(t - 1):
                        pe.wait_ge(*upto("f1_lg", t - 1))
                    mm(bank[1 + s][:, :], ones[0:1, :], b_log, start=True, stop=False)
                    pe.wait_ge(*upto("f1_xnt", t + 1))
                    for k in range(KC):
                        last = mm(bank[1 + s][:, :], a_xnt[s][:, P * k:P * k + P], w_log[:, k, :], start=False, stop=k == KC - 1)
                    last.then_inc(sem("f1_l_mm"), 1)
                if t_ is not None:
                    r = rows_of(t_)
                    pe.wait_ge(*upto("f1_sw", t_ + 1))
                    if due(t_):
                        pe.wait_ge(*upto("f1_swt", t_))
                    for j in range(4):
                        last = pe.transpose(bank[3][:, P * j:P * j + P], a_sw[s_][:, P * j:P * j + P], ident[:, :])
                    last.then_inc(sem("f1_swt_mm"), 1)
                    for j in range(4):
                        last = mm(bank[4 + j][:, 0:257], a_sw[s_][0:r, P * j:P * j + P], a_xn[s_][0:r, :],
                                  start=isinstance(t_, int) and t_ == 0, stop=is_last(t_), skip_group_check=True)
                    last.then_inc(sem("f1_u_mm"), 1)
            blk = lambda v, j: v[:, P * j:P * j + P]
            pe.wait_ge(*upto("fs_u", 4))
            for k in range(KC):
                for j in range(4):
                    last = pe.transpose(bank[k][:, P * j:P * j + P], f_u[:, j, P * k:P * k + P], ident[:, :])
                last.then_inc(sem("fs_ut_mm"), 1)
            pe.wait_ge(*upto("fs_ut", 2))
            for j in range(4):
                for k in range(KC):
                    last = mm(blk(bank[2], j), f_ut[:, k, P * j:P * j + P], w_fx[:, k, P * j:P * j + P], start=k == 0, stop=k == KC - 1)
            last.then_inc(sem("fs_tok_mm"), 1)
            pe.wait_ge(*upto("fs_tok", 4))
            for j in range(4):
                last = pe.transpose(blk(bank[0], j), blk(f_tok2, j), ident[:, :])
            last.then_inc(sem("fs_tokt_mm"), 1)
            pe.wait_ge(*upto("fs_tokt", 1))
            for w_, b_ in ((wq_bd, 1), (wk_bd, 2)):
                last = mm(bank[b_][:, :], w_, f_tokt, start=True, stop=True)
                last.then_inc(sem("fs_qkv_mm"), 1)
            for j in range(4):
                last = mm(blk(bank[4], j), blk(f_tokt, j), wv_bd, start=True, stop=True)
            last.then_inc(sem("fs_qkv_mm"), 1)
            pe.wait_ge(*upto("fs_qkv", 3))
            for j in range(4):
                last = mm(blk(bank[5], j), blk(f_qt, j), blk(f_kt, j), start=True, stop=True)
            last.then_inc(sem("fs_s_mm"), 1)
            pe.wait_ge(*upto("fs_a", 4))
            for j in range(4):
                last = pe.transpose(blk(bank[0], j), blk(f_s, j), ident[:, :])
            last.then_inc(sem("fs_at_mm"), 1)
            pe.wait_ge(*upto("fs_at", 1))
            for j in range(4):
                last = mm(blk(bank[1], j), blk(f_v, j), blk(f_at, j), start=True, stop=True)
            last.then_inc(sem("fs_ost_mm"), 1)
            pe.wait_ge(*upto("fs_ost", 1))
            for j in range(4):
                mm(bank[4 + j][:, 0:C], blk(f_ost, j), w_out[:, j, :], start=True, stop=True).then_inc(sem("fs_m_mm"), 1)
            if phase_end(pe):
                return
            for (t, s, n), (t_, s_, n_), _ in staged(pe):
                if t is not None:
                    pe.wait_ge(*upto(f"f2_in{s}", 32 * (n + 1)))
                    if due(t - 1):
                        pe.wait_ge(*upto("f2_x2", t - 1))
                    mm(bank[s][:, 0:C], ones[0:1, :], bout_r, start=True, stop=False)
                    for j in range(4):
                        last = mm(bank[s][:, 0:C], k_swt[s][:, P * j:P * j + P], f_m[:, j, :], start=False, stop=j == 3)
                    last.then_inc(sem("f2_o_mm"), 1)
                if t_ is not None:
                    pe.wait_ge(*upto("f2_xn", t_ + 1))
                    if due(t_):
                        pe.wait_ge(*upto("f2_xnt", t_))
                    transposes(bank[2], a_xn[s_]).then_inc(sem("f2_t"), 1)
            if phase_end(pe):
                return
            def keys_values(m, h):
                if h == 0:
                    pe.wait_ge(*upto("kv_in", 16 * (m + 1)))
                    if not due(m):
                        pe.wait_ge(*upto("w_kv", KC))
                    if due(m):
                        pe.wait_ge(*upto("kv_kn", m))
                    for k in range(KC):
                        last = mm(bank[2][:, :], k_xnt[:, P * k:P * k + P], w_kv1[:, k, 0:512], start=k == 0, stop=k == KC - 1)
                    last.then_inc(sem("kv_k_mm"), 1)
                    if due(m):
                        pe.wait_ge(*upto("kv_v", m))
                    for k in range(KC):
                        last = mm(bank[3][:, :], k_xnt[:, P * k:P * k + P], w_kv1[:, k, 512:1024], start=k == 0, stop=k == KC - 1)
                    last.then_inc(sem("kv_v_mm"), 1)
                if h == 3:
                    r = rows_of(m)
                    pe.wait_ge(*upto("kv_kn", m + 1))
                    pe.wait_ge(*upto("kv_v", m + 1))
                    for j in range(4):
                        last = mm(bank[4 + j][:, 0:P], k_v[0:r, P * j:P * j + P], k_kn[0:r, P * j:P * j + P],
                                  start=isinstance(m, int) and m == 0, stop=is_last(m), skip_group_check=True)
                    last.then_inc(sem("kv_dots_mm"), 1)

            for i, m1, m2 in gather_bodies(pe):
                for h in range(BPB):
                    g = i * BPB + h
                    pe.wait_ge(*upto("g1_oh", g + 1))
                    sum_rows("g1", g, i, oh[h % 2], h)
                    if m1 is not None:
                        keys_values(m1, h)
            pe.wait_ge(*upto("g1_add", T))
            pe.wait_ge(*upto("d_bd", 1))
            for j in range(4):
                mm(bank[j][:, 0:C], blk(d_bd, j), w_o1t[:, j, :], start=True, stop=True).then_inc(sem("d_t1_mm"), 1)
            pe.wait_ge(*upto("d_t1", 4))
            for k in range(KC):
                for j in range(4):
                    last = mm(bank[4 + k][:, 0:C], w_q1[:, j, P * k:P * k + P], d_t1[:, j, :], start=j == 0, stop=j == 3)
                last.then_inc(sem("d_f_mm"), 1)
            if phase_end(pe):
                return
            for (t, s, n), (tb, sb_, nb), (t_, s_, n_) in staged(pe):
                if tb is not None:
                    pe.wait_ge(*upto("c_hnt", tb + 1))
                    pe.wait_ge(*upto(f"c_in{sb_}", 32 * (nb + 1)))
                    if due(tb):
                        pe.wait_ge(*upto("c_x3", tb))
                    mm(bank[1][:, 0:C], ones[0:1, :], b_comb, start=True, stop=False)
                    for k in range(KC):
                        mm(bank[1][:, 0:C], c_hnt[sb_][:, P * k:P * k + P], w_neigh[:, k, :], start=False, stop=False)
                    for k in range(KC):
                        last = mm(bank[1][:, 0:C], c_xnt[sb_][:, P * k:P * k + P], w_comb[:, k, :], start=False, stop=k == KC - 1)
                    last.then_inc(sem("c_x_mm"), 1)
                if t_ is not None:
                    pe.wait_ge(*upto("c_xn", t_ + 1))
                    if due(t_):
                        pe.wait_ge(*upto("c_x4t", t_))
                    transposes(bank[2], c_xn[s_]).then_inc(sem("c_x4_t"), 1)
                if t is not None:
                    pe.wait_ge(*upto("c_hn", t + 1))
                    if due(t):
                        pe.wait_ge(*upto("c_hnt", t))
                    transposes(bank[0], c_hn[s]).then_inc(sem("c_hn_t"), 1)
                if t_ is not None:
                    pe.wait_ge(*upto("c_x4t", t_ + 1))
                    if due(t_):
                        pe.wait_ge(*upto("c_r", t_))
                    for k in range(KC):
                        last = mm(bank[3][:, 0:8], c_x4t[s_][:, P * k:P * k + P], w_rt[:, k, :], start=k == 0, stop=k == KC - 1)
                    last.then_inc(sem("c_r_mm"), 1)
            if phase_end(pe):
                return
            pe.wait_ge(*upto("w_moe_in", 64))
            for g, s, n, m in expert_groups(pe):
                pe.wait_ge(*upto(f"s_in{s}", 32 * (n + 1)))
                if due(g):
                    pe.wait_ge(*upto("s_ct", g))
                pe.wait_ge(*upto("s_cg", g + 1))
                for j in range(m):
                    last = pe.transpose(bank[6][0:8, P * j:P * j + P], s_cg[s][:, 8 * j:8 * j + 8], ident[:, :])
                last.then_inc(sem("s_ct_mm"), 1)
                pe.wait_ge(*upto("s_ct", g + 1))
                if due(32 * g):
                    pe.wait_ge(*upto("s_acc", 32 * g))
                for j in range(m):
                    last = mm(bank[4 + j // 2][:, C * (j % 2):C * (j % 2) + C], s_ct[s][:, P * j:P * j + P], b2_sb, start=True, stop=True)
                last.then_inc(sem("s_cb_mm"), 1)

                def hidden(e):
                    for f in range(KC):
                        if due(16 * g + 2 * e + f - 3):
                            pe.wait_ge(*upto("s_h", 16 * g + 2 * e + f - 3))
                        for k in range(KC):
                            last = mm(bank[2 * (e % 2) + f][:, 0:m * P], w1_sb[:, e, k, P * f:P * f + P], s_xt[s][:, 0:m, k, :], start=k == 0, stop=k == KC - 1)
                        last.then_inc(sem("s_h_mm"), 1)

                hidden(0)
                for e in range(8):
                    if e < 7:
                        hidden(e + 1)
                    pe.wait_ge(*upto("s_h", 16 * g + 2 * e + 2))
                    pe.wait_ge(*upto("s_base", 4 * g + m))
                    if due(32 * g + m * e):
                        pe.wait_ge(*upto("s_acc", 32 * g + m * e))
                    for j in range(m):
                        for f in range(KC):
                            last = mm(bank[4 + j // 2][:, C * (j % 2):C * (j % 2) + C], s_h[e % 2][f][:, P * j:P * j + P], w2_sb[:, e, f, :], start=f == 0, stop=f == KC - 1)
                    last.then_inc(sem("s_y_mm"), 1)
            phase_end(pe)



def kernel(x, src, dst, edge_type_8, L0_gnn_W, L0_gnn_W_root, L0_gnn_bias, L0_mix_Wqkv, L0_mix_Wproj, L0_mix_bproj,
           L0_mix_ln_g, L0_mix_ln_b, L0_mix_Wg1, L0_mix_bg1, L0_mix_Wg2, L0_mix_bg2, L0_ffn_W_fx, L0_ffn_b_fx,
           L0_ffn_W_x, L0_ffn_b_x, L0_ffn_W_slice, L0_ffn_b_slice, L0_ffn_W_q, L0_ffn_W_k, L0_ffn_W_v, L0_ffn_W_out,
           L0_ffn_b_out, L0_ffn_temperature, L1_gnn_w_neigh, L1_gnn_w_self, L1_gnn_b_self, L1_mix_Wqkv, L1_mix_Wout,
           L1_mix_bout, L1_ffn_router_w, L1_ffn_w1, L1_ffn_b1, L1_ffn_w2, L1_ffn_b2):
    import numpy as np
    import concourse.bacc as bacc
    from concourse.bass_utils import run_bass_kernel_spmd

    a = np.asarray
    arrays = {
        "x": a(x), "src": a(src), "dst": a(dst), "etype": a(edge_type_8),
        "gnn0_w": a(L0_gnn_W).transpose(1, 0, 2).reshape(C, R * C), "gnn0_root": a(L0_gnn_W_root),
        "gnn0_bias": a(L0_gnn_bias), "mix_wqkv": a(L0_mix_Wqkv), "mix_wq_t": a(L0_mix_Wqkv)[:, 0:C].T,
        "mix_wproj": a(L0_mix_Wproj), "mix_bproj": a(L0_mix_bproj), "mix_ln_g": a(L0_mix_ln_g).reshape(KC, P).T,
        "mix_ln_b": a(L0_mix_ln_b).reshape(KC, P).T, "mix_wg1": a(L0_mix_Wg1), "mix_bg1": a(L0_mix_bg1), "mix_wg2": a(L0_mix_Wg2),
        "mix_bg2": a(L0_mix_bg2), "ffn_wfx": a(L0_ffn_W_fx), "ffn_bfx": a(L0_ffn_b_fx), "ffn_wx_t": a(L0_ffn_W_x).T,
        "ffn_bx": a(L0_ffn_b_x).reshape(4, P).T, "ffn_wslice": a(L0_ffn_W_slice), "ffn_bslice": a(L0_ffn_b_slice),
        "ffn_wq": a(L0_ffn_W_q), "ffn_wk": a(L0_ffn_W_k), "ffn_wv": a(L0_ffn_W_v), "ffn_wout": a(L0_ffn_W_out),
        "ffn_bout": a(L0_ffn_b_out), "ffn_temp": a(L0_ffn_temperature).reshape(1, 8),
        "gnn1_wneigh_t": a(L1_gnn_w_neigh).T, "gnn1_wself_t": a(L1_gnn_w_self).T, "gnn1_bself": a(L1_gnn_b_self),
        "mix1_wqkv": a(L1_mix_Wqkv), "mix1_wkv_t": a(L1_mix_Wqkv)[512:1536, :].T, "mix1_wout_t": a(L1_mix_Wout).T,
        "mix1_bout": a(L1_mix_bout), "router_t": a(L1_ffn_router_w).T, "w1": a(L1_ffn_w1), "b1": a(L1_ffn_b1).reshape(8 * KC, P).T,
        "w2": a(L1_ffn_w2), "b2": a(L1_ffn_b2),
    }
    nc = bacc.Bacc("TRN2", target_bir_lowering=False, num_devices=1)
    given, args = {}, {}
    for name, v in arrays.items():
        given[f"in_{name}"] = v = np.ascontiguousarray(v)
        args[name] = nc.dram_tensor(f"in_{name}", v.shape, mybir.dt.from_np(v.dtype), kind="ExternalInput").ap()
    args["out"] = nc.dram_tensor("out_x", (N, C), FP32, kind="ExternalOutput").ap()
    build(nc, **args)
    r = run_bass_kernel_spmd(nc, [given], core_ids=[0])
    return r.results[0]["out_x"]
```
